# Optimizing a Trainium2 kernel written in Bass

```python
import numpy as np
import jax
import jax.numpy as jnp

def _softmax(x, axis=-1):
    return jax.nn.softmax(x, axis=axis)

def _gelu(x):
    return jax.nn.gelu(x, approximate=True)

def _silu(x):
    return jax.nn.silu(x)

def _sigmoid(x):
    return jax.nn.sigmoid(x)

def _layernorm(x, axis=-1, eps=1e-05):
    m = jnp.mean(x, axis=axis, keepdims=True)
    v = jnp.var(x, axis=axis, keepdims=True)
    return (x - m) / jnp.sqrt(v + eps)

def _scatter_add(tgt, idx, src, axis=0):
    return tgt.at[idx].add(src)

def _segment_sum(src, seg, n):
    return jax.ops.segment_sum(src, seg, n)
kernel_name = 'mk_flamingo_gated_d4_seqx_r8_9f0a8d'

def setup_inputs(seed: int=0):
    np.random.seed(seed)
    _w = jnp.asarray

    def _rec_inputs():
        import jax
        import jax.numpy as jnp
        _rk = jax.random.key(seed)
        x = -0.0003929 + 0.9999 * jax.random.normal(jax.random.fold_in(_rk, 1), (4, 512, 128), jnp.float32)
        _lenS = 512 - jax.random.randint(jax.random.fold_in(_rk, 7), (4,), 0, max(1, 512 // 4) + 1, jnp.int32)
        _lenS2 = 77 - jax.random.randint(jax.random.fold_in(_rk, 8), (4,), 0, max(1, 77 // 4) + 1, jnp.int32)
        _ctx_512P = jax.random.normal(jax.random.fold_in(_rk, 11), (4, 16, 64), jnp.float32)
        _ctx_512c = jax.random.dirichlet(jax.random.fold_in(_rk, 511), 0.3 * jnp.ones((16,), jnp.float32), (4, 77))
        _ctx_512t = jnp.einsum('bsk,bkd->bsd', _ctx_512c, _ctx_512P)
        _ctx_512t = _ctx_512t * jax.lax.rsqrt(jnp.mean(jnp.square(_ctx_512t)) + 1e-12) * 0.953939
        ctx_512 = -1.39393e-06 + 0.999914 * (_ctx_512t + 0.3 * jax.random.normal(jax.random.fold_in(_rk, 611), (4, 77, 64), jnp.float32))
        _g = jax.random.normal(jax.random.fold_in(_rk, 9001), (2, 4), jnp.float32)
        _g = jnp.sign(_g) * jnp.maximum(jnp.abs(_g), 1.0) + (_g == 0) * 1.0
        g_xattn = _g[0]
        g_ffn = _g[1]
        return (x, ctx_512, g_xattn, g_ffn)
    x, ctx_512, g_xattn, g_ffn = _rec_inputs()

    def _L0_xattn_setup():
        import jax, jax.numpy as jnp
        import numpy as np
        HEADS = 16
        D_MODEL = 128
        IMG_MODEL = 64
        D_K = D_MODEL // HEADS
        key = jax.random.key(seed)
        ks = jax.random.split(key, 12)
        B, LQ, LKV = (8, 256, 128)
        s_dm = 1.0 / np.sqrt(D_MODEL)
        s_im = 1.0 / np.sqrt(IMG_MODEL)
        return {'q': jax.random.normal(ks[0], (B, LQ, D_MODEL), jnp.float32), 'k': jax.random.normal(ks[1], (B, LKV, IMG_MODEL), jnp.float32), 'v': jax.random.normal(ks[2], (B, LKV, IMG_MODEL), jnp.float32), 'Wq': jax.random.normal(ks[3], (D_MODEL, D_MODEL), jnp.float32) * s_dm, 'bq': jnp.zeros((D_MODEL,), jnp.float32), 'Wk': jax.random.normal(ks[4], (IMG_MODEL, D_MODEL), jnp.float32) * s_im, 'bk': jnp.zeros((D_MODEL,), jnp.float32), 'Wv': jax.random.normal(ks[5], (IMG_MODEL, D_MODEL), jnp.float32) * s_im, 'bv': jnp.zeros((D_MODEL,), jnp.float32), 'Wo': jax.random.normal(ks[6], (D_MODEL, D_MODEL), jnp.float32) * s_dm, 'bo': jnp.zeros((D_MODEL,), jnp.float32)}
    _L0_xattn_all = _L0_xattn_setup()
    _L0_xattn_in = {k: v for k, v in _L0_xattn_all.items() if k in ('Wq', 'bq', 'Wk', 'bk', 'Wv', 'bv', 'Wo', 'bo')}
    del _L0_xattn_all

    def _L0_ffn_setup():
        import jax, jax.numpy as jnp
        import numpy as np
        ALPHA = 1.702
        LIMIT = 9.0
        TOP_K = 2

        def swiglu(x):
            g, v = (x[..., 0::2], x[..., 1::2])
            g = jnp.clip(g, None, LIMIT)
            v = jnp.clip(v, -LIMIT, LIMIT)
            return g * jax.nn.sigmoid(ALPHA * g) * (v + 1)
        key = jax.random.key(seed)
        ks = jax.random.split(key, 6)
        B, L, D = (2, 256, 128)
        E, F = (8, 256)
        s_gate = 1.0 / np.sqrt(D)
        s1 = 1.0 / np.sqrt(D)
        s2 = 1.0 / np.sqrt(F)
        return {'x': jax.random.normal(ks[0], (B, L, D), dtype=jnp.float32), 'gate_w': jax.random.normal(ks[1], (D, E), dtype=jnp.float32) * s_gate, 'dense_1_w': jax.random.normal(ks[2], (E, 2 * F, D), dtype=jnp.float32) * s1, 'dense_1_b': jnp.zeros((E, 2 * F), dtype=jnp.float32), 'dense_2_w': jax.random.normal(ks[3], (E, D, F), dtype=jnp.float32) * s2, 'dense_2_b': jnp.zeros((E, D), dtype=jnp.float32)}
    _L0_ffn_all = _L0_ffn_setup()
    _L0_ffn_in = {k: v for k, v in _L0_ffn_all.items() if k in ('gate_w', 'dense_1_w', 'dense_1_b', 'dense_2_w', 'dense_2_b')}
    del _L0_ffn_all

    def _L1_xattn_setup():
        import jax, jax.numpy as jnp
        import numpy as np
        H, D, C1, C2, S, M, B, W = (16, 32, 128, 64, 256, 64, 2, 4)

        def _ln(x, g, b):
            m = jnp.mean(x, -1, keepdims=True)
            v = jnp.var(x, -1, keepdims=True)
            return (x - m) * jax.lax.rsqrt(v + 1e-05) * g + b

        def _mha(x, y, wq, wk, wv, li1_w, li1_b, lnx_g, lnx_b, lny_g, lny_b, ln3_g, ln3_b, li2_w, li2_b, li3_w, li3_b, causal):
            xn = _ln(x, lnx_g, lnx_b)
            yn = _ln(y, lny_g, lny_b)
            q = jnp.einsum('bsc,hcd->bhsd', xn, wq)
            k = jnp.einsum('btc,hcd->bhtd', yn, wk)
            v = jnp.einsum('btc,hcd->bhtd', yn, wv)
            a = jax.nn.softmax(jnp.einsum('bhsd,bhtd->bhst', q, k) * D ** (-0.5), axis=-1)
            if causal:
                s, t = (a.shape[-2], a.shape[-1])
                mask = (jnp.arange(t)[None, :] > jnp.arange(s)[:, None]).astype(a.dtype)
                a = a * mask
            o = jnp.einsum('bhst,bhtd->bhsd', a, v)
            o = o.transpose(0, 2, 1, 3).reshape(x.shape[0], x.shape[1], H * D)
            x_out = x + o @ li1_w + li1_b
            h = jax.nn.gelu(_ln(x_out, ln3_g, ln3_b) @ li2_w + li2_b, approximate=False)
            return x_out + h @ li3_w + li3_b
        key = jax.random.key(seed)
        ks = iter(jax.random.split(key, 64))

        def w(shape, scale=0.02):
            return jax.random.normal(next(ks), shape, jnp.float32) * scale
        inp = {'xx': jax.random.normal(next(ks), (B, S, C1), jnp.float32), 'ee': jax.random.normal(next(ks), (B, M, C2), jnp.float32), 'ln1_g': jnp.ones(C1, jnp.float32), 'ln1_b': jnp.zeros(C1, jnp.float32), 'ln2_g': jnp.ones(C1, jnp.float32), 'ln2_b': jnp.zeros(C1, jnp.float32)}
        for pfx, cy in (('a1', C1), ('a2', C2)):
            inp[pfx + '_wq'] = w((H, C1, D))
            inp[pfx + '_wk'] = w((H, cy, D))
            inp[pfx + '_wv'] = w((H, cy, D))
            inp[pfx + '_li1_w'] = w((H * D, C1))
            inp[pfx + '_li1_b'] = jnp.zeros(C1, jnp.float32)
            inp[pfx + '_lnx_g'] = jnp.ones(C1, jnp.float32)
            inp[pfx + '_lnx_b'] = jnp.zeros(C1, jnp.float32)
            inp[pfx + '_lny_g'] = jnp.ones(cy, jnp.float32)
            inp[pfx + '_lny_b'] = jnp.zeros(cy, jnp.float32)
            inp[pfx + '_ln3_g'] = jnp.ones(C1, jnp.float32)
            inp[pfx + '_ln3_b'] = jnp.zeros(C1, jnp.float32)
            inp[pfx + '_li2_w'] = w((C1, C1 * W))
            inp[pfx + '_li2_b'] = jnp.zeros(C1 * W, jnp.float32)
            inp[pfx + '_li3_w'] = w((C1 * W, C1))
            inp[pfx + '_li3_b'] = jnp.zeros(C1, jnp.float32)
        inp['training'] = 0
        return inp
    _L1_xattn_all = _L1_xattn_setup()
    _L1_xattn_in = {k: v for k, v in _L1_xattn_all.items() if k in ('ln1_g', 'ln1_b', 'ln2_g', 'ln2_b', 'a1_wq', 'a1_wk', 'a1_wv', 'a1_li1_w', 'a1_li1_b', 'a1_lnx_g', 'a1_lnx_b', 'a1_lny_g', 'a1_lny_b', 'a1_ln3_g', 'a1_ln3_b', 'a1_li2_w', 'a1_li2_b', 'a1_li3_w', 'a1_li3_b', 'a2_wq', 'a2_wk', 'a2_wv', 'a2_li1_w', 'a2_li1_b', 'a2_lnx_g', 'a2_lnx_b', 'a2_lny_g', 'a2_lny_b', 'a2_ln3_g', 'a2_ln3_b', 'a2_li2_w', 'a2_li2_b', 'a2_li3_w', 'a2_li3_b')}
    del _L1_xattn_all

    def _L1_ffn_setup():
        import jax, jax.numpy as jnp
        import numpy as np
        TOP_K = 4
        key = jax.random.key(seed)
        ks = jax.random.split(key, 8)
        B, S, H = (1, 256, 128)
        E, I = (16, 64)
        SI = 64 * 2
        w = 0.02
        return {'hidden_states': jax.random.normal(ks[0], (B, S, H), jnp.float32), 'gate_w': jax.random.normal(ks[1], (E, H), jnp.float32) * w, 'expert_gate': jax.random.normal(ks[2], (E, H, I), jnp.float32) * w, 'expert_up': jax.random.normal(ks[3], (E, H, I), jnp.float32) * w, 'expert_down': jax.random.normal(ks[4], (E, I, H), jnp.float32) * w, 'shared_gate': jax.random.normal(ks[5], (H, SI), jnp.float32) * w, 'shared_up': jax.random.normal(ks[6], (H, SI), jnp.float32) * w, 'shared_down': jax.random.normal(ks[7], (SI, H), jnp.float32) * w}
    _L1_ffn_all = _L1_ffn_setup()
    _L1_ffn_in = {k: v for k, v in _L1_ffn_all.items() if k in ('gate_w', 'expert_gate', 'expert_up', 'expert_down', 'shared_gate', 'shared_up', 'shared_down')}
    del _L1_ffn_all

    def _L2_xattn_setup():
        import jax, jax.numpy as jnp
        import numpy as np
        B, LQ, LK = (8, 256, 256)
        QD, KD, VD = (128, 64, 64)
        key = jax.random.key(seed)
        ks = jax.random.split(key, 9)
        s = 0.02
        return {'query': jax.random.normal(ks[0], (B, LQ, QD), jnp.float32), 'key': jax.random.normal(ks[1], (B, LK, KD), jnp.float32), 'value': jax.random.normal(ks[2], (B, LK, VD), jnp.float32), 'Wq': jax.random.normal(ks[3], (QD, QD), jnp.float32) * s, 'bq': jnp.zeros((QD,), jnp.float32), 'Wk': jax.random.normal(ks[4], (KD, QD), jnp.float32) * s, 'bk': jnp.zeros((QD,), jnp.float32), 'Wv': jax.random.normal(ks[5], (VD, QD), jnp.float32) * s, 'bv': jnp.zeros((QD,), jnp.float32)}
    _L2_xattn_all = _L2_xattn_setup()
    _L2_xattn_in = {k: v for k, v in _L2_xattn_all.items() if k in ('Wq', 'bq', 'Wk', 'bk', 'Wv', 'bv')}
    del _L2_xattn_all

    def _L2_ffn_setup():
        import jax, jax.numpy as jnp
        import numpy as np
        import math
        D_IN = 128
        FEATURES = (512, 512, 128)
        BATCH, SEQ = (8, 256)

        def _conn_dense(kernel_bool, x):
            w = jnp.where(kernel_bool, jnp.float32(1.0), jnp.float32(-1.0))
            return x @ w
        key = jax.random.key(seed)
        kx, kk0, kk1, kk2 = jax.random.split(key, 4)
        x = jax.random.normal(kx, (BATCH, SEQ, D_IN), dtype=jnp.float32)
        k0 = jax.random.randint(kk0, (2 * D_IN, FEATURES[0]), 0, 2).astype(jnp.bool_)
        k1 = jax.random.randint(kk1, (FEATURES[0], FEATURES[1]), 0, 2).astype(jnp.bool_)
        k2 = jax.random.randint(kk2, (FEATURES[1], FEATURES[2]), 0, 2).astype(jnp.bool_)
        s0 = jnp.asarray(1.0 / math.sqrt(2 * D_IN), dtype=jnp.float32)
        s1 = jnp.asarray(1.0 / math.sqrt(FEATURES[0]), dtype=jnp.float32)
        s2 = jnp.asarray(1.0 / math.sqrt(FEATURES[1]), dtype=jnp.float32)
        return {'x': x, 'k0': k0, 'k1': k1, 'k2': k2, 's0': s0, 's1': s1, 's2': s2}
    _L2_ffn_all = _L2_ffn_setup()
    _L2_ffn_in = {k: v for k, v in _L2_ffn_all.items() if k in ('k0', 'k1', 'k2', 's0', 's1', 's2')}
    del _L2_ffn_all

    def _L3_xattn_setup():
        import jax, jax.numpy as jnp
        import numpy as np
        HEADS = 16
        D_MODEL = 128
        IMG_MODEL = 64
        D_K = D_MODEL // HEADS
        key = jax.random.key(seed)
        ks = jax.random.split(key, 12)
        B, LQ, LKV = (8, 256, 128)
        s_dm = 1.0 / np.sqrt(D_MODEL)
        s_im = 1.0 / np.sqrt(IMG_MODEL)
        return {'q': jax.random.normal(ks[0], (B, LQ, D_MODEL), jnp.float32), 'k': jax.random.normal(ks[1], (B, LKV, IMG_MODEL), jnp.float32), 'v': jax.random.normal(ks[2], (B, LKV, IMG_MODEL), jnp.float32), 'Wq': jax.random.normal(ks[3], (D_MODEL, D_MODEL), jnp.float32) * s_dm, 'bq': jnp.zeros((D_MODEL,), jnp.float32), 'Wk': jax.random.normal(ks[4], (IMG_MODEL, D_MODEL), jnp.float32) * s_im, 'bk': jnp.zeros((D_MODEL,), jnp.float32), 'Wv': jax.random.normal(ks[5], (IMG_MODEL, D_MODEL), jnp.float32) * s_im, 'bv': jnp.zeros((D_MODEL,), jnp.float32), 'Wo': jax.random.normal(ks[6], (D_MODEL, D_MODEL), jnp.float32) * s_dm, 'bo': jnp.zeros((D_MODEL,), jnp.float32)}
    _L3_xattn_all = _L3_xattn_setup()
    _L3_xattn_in = {k: v for k, v in _L3_xattn_all.items() if k in ('Wq', 'bq', 'Wk', 'bk', 'Wv', 'bv', 'Wo', 'bo')}
    del _L3_xattn_all

    def _L3_ffn_setup():
        import jax, jax.numpy as jnp
        import numpy as np
        B, N, D = (4, 256, 128)
        SPARSITY = 0.01
        key = jax.random.key(seed)
        k1, k2, k3 = jax.random.split(key, 3)
        x = jax.random.normal(k1, (B, N, D), dtype=jnp.float32)
        spatial = jax.random.normal(k2, (D, D), dtype=jnp.float32) * 0.02
        freq = jnp.fft.fft(spatial, axis=-1)
        k = int(D * SPARSITY)
        mag = jnp.abs(freq)
        kth = jax.lax.top_k(mag, k)[0][:, -1:]
        w_sparse = jnp.where(mag >= kth, freq, 0.0 + 0j)
        bias = jax.random.normal(k3, (D,), dtype=jnp.float32) * 0.01
        return {'x': x, 'w_freq_real': jnp.real(w_sparse).astype(jnp.float32), 'w_freq_imag': jnp.imag(w_sparse).astype(jnp.float32), 'bias': bias}
    _L3_ffn_all = _L3_ffn_setup()
    _L3_ffn_in = {k: v for k, v in _L3_ffn_all.items() if k in ('w_freq_real', 'w_freq_imag', 'bias')}
    del _L3_ffn_all
    return {'x': x, 'ctx_512': ctx_512, 'g_xattn': g_xattn, 'g_ffn': g_ffn, 'L0_xattn_Wq': _L0_xattn_in['Wq'], 'L0_xattn_bq': _L0_xattn_in['bq'], 'L0_xattn_Wk': _L0_xattn_in['Wk'], 'L0_xattn_bk': _L0_xattn_in['bk'], 'L0_xattn_Wv': _L0_xattn_in['Wv'], 'L0_xattn_bv': _L0_xattn_in['bv'], 'L0_xattn_Wo': _L0_xattn_in['Wo'], 'L0_xattn_bo': _L0_xattn_in['bo'], 'L0_ffn_gate_w': _L0_ffn_in['gate_w'], 'L0_ffn_dense_1_w': _L0_ffn_in['dense_1_w'], 'L0_ffn_dense_1_b': _L0_ffn_in['dense_1_b'], 'L0_ffn_dense_2_w': _L0_ffn_in['dense_2_w'], 'L0_ffn_dense_2_b': _L0_ffn_in['dense_2_b'], 'L1_xattn_ln1_g': _L1_xattn_in['ln1_g'], 'L1_xattn_ln1_b': _L1_xattn_in['ln1_b'], 'L1_xattn_ln2_g': _L1_xattn_in['ln2_g'], 'L1_xattn_ln2_b': _L1_xattn_in['ln2_b'], 'L1_xattn_a1_wq': _L1_xattn_in['a1_wq'], 'L1_xattn_a1_wk': _L1_xattn_in['a1_wk'], 'L1_xattn_a1_wv': _L1_xattn_in['a1_wv'], 'L1_xattn_a1_li1_w': _L1_xattn_in['a1_li1_w'], 'L1_xattn_a1_li1_b': _L1_xattn_in['a1_li1_b'], 'L1_xattn_a1_lnx_g': _L1_xattn_in['a1_lnx_g'], 'L1_xattn_a1_lnx_b': _L1_xattn_in['a1_lnx_b'], 'L1_xattn_a1_lny_g': _L1_xattn_in['a1_lny_g'], 'L1_xattn_a1_lny_b': _L1_xattn_in['a1_lny_b'], 'L1_xattn_a1_ln3_g': _L1_xattn_in['a1_ln3_g'], 'L1_xattn_a1_ln3_b': _L1_xattn_in['a1_ln3_b'], 'L1_xattn_a1_li2_w': _L1_xattn_in['a1_li2_w'], 'L1_xattn_a1_li2_b': _L1_xattn_in['a1_li2_b'], 'L1_xattn_a1_li3_w': _L1_xattn_in['a1_li3_w'], 'L1_xattn_a1_li3_b': _L1_xattn_in['a1_li3_b'], 'L1_xattn_a2_wq': _L1_xattn_in['a2_wq'], 'L1_xattn_a2_wk': _L1_xattn_in['a2_wk'], 'L1_xattn_a2_wv': _L1_xattn_in['a2_wv'], 'L1_xattn_a2_li1_w': _L1_xattn_in['a2_li1_w'], 'L1_xattn_a2_li1_b': _L1_xattn_in['a2_li1_b'], 'L1_xattn_a2_lnx_g': _L1_xattn_in['a2_lnx_g'], 'L1_xattn_a2_lnx_b': _L1_xattn_in['a2_lnx_b'], 'L1_xattn_a2_lny_g': _L1_xattn_in['a2_lny_g'], 'L1_xattn_a2_lny_b': _L1_xattn_in['a2_lny_b'], 'L1_xattn_a2_ln3_g': _L1_xattn_in['a2_ln3_g'], 'L1_xattn_a2_ln3_b': _L1_xattn_in['a2_ln3_b'], 'L1_xattn_a2_li2_w': _L1_xattn_in['a2_li2_w'], 'L1_xattn_a2_li2_b': _L1_xattn_in['a2_li2_b'], 'L1_xattn_a2_li3_w': _L1_xattn_in['a2_li3_w'], 'L1_xattn_a2_li3_b': _L1_xattn_in['a2_li3_b'], 'L1_ffn_gate_w': _L1_ffn_in['gate_w'], 'L1_ffn_expert_gate': _L1_ffn_in['expert_gate'], 'L1_ffn_expert_up': _L1_ffn_in['expert_up'], 'L1_ffn_expert_down': _L1_ffn_in['expert_down'], 'L1_ffn_shared_gate': _L1_ffn_in['shared_gate'], 'L1_ffn_shared_up': _L1_ffn_in['shared_up'], 'L1_ffn_shared_down': _L1_ffn_in['shared_down'], 'L2_xattn_Wq': _L2_xattn_in['Wq'], 'L2_xattn_bq': _L2_xattn_in['bq'], 'L2_xattn_Wk': _L2_xattn_in['Wk'], 'L2_xattn_bk': _L2_xattn_in['bk'], 'L2_xattn_Wv': _L2_xattn_in['Wv'], 'L2_xattn_bv': _L2_xattn_in['bv'], 'L2_ffn_k0': _L2_ffn_in['k0'], 'L2_ffn_k1': _L2_ffn_in['k1'], 'L2_ffn_k2': _L2_ffn_in['k2'], 'L2_ffn_s0': _L2_ffn_in['s0'], 'L2_ffn_s1': _L2_ffn_in['s1'], 'L2_ffn_s2': _L2_ffn_in['s2'], 'L3_xattn_Wq': _L3_xattn_in['Wq'], 'L3_xattn_bq': _L3_xattn_in['bq'], 'L3_xattn_Wk': _L3_xattn_in['Wk'], 'L3_xattn_bk': _L3_xattn_in['bk'], 'L3_xattn_Wv': _L3_xattn_in['Wv'], 'L3_xattn_bv': _L3_xattn_in['bv'], 'L3_xattn_Wo': _L3_xattn_in['Wo'], 'L3_xattn_bo': _L3_xattn_in['bo'], 'L3_ffn_w_freq_real': _L3_ffn_in['w_freq_real'], 'L3_ffn_w_freq_imag': _L3_ffn_in['w_freq_imag'], 'L3_ffn_bias': _L3_ffn_in['bias']}

def reference(x, ctx_512, g_xattn, g_ffn, L0_xattn_Wq, L0_xattn_bq, L0_xattn_Wk, L0_xattn_bk, L0_xattn_Wv, L0_xattn_bv, L0_xattn_Wo, L0_xattn_bo, L0_ffn_gate_w, L0_ffn_dense_1_w, L0_ffn_dense_1_b, L0_ffn_dense_2_w, L0_ffn_dense_2_b, L1_xattn_ln1_g, L1_xattn_ln1_b, L1_xattn_ln2_g, L1_xattn_ln2_b, L1_xattn_a1_wq, L1_xattn_a1_wk, L1_xattn_a1_wv, L1_xattn_a1_li1_w, L1_xattn_a1_li1_b, L1_xattn_a1_lnx_g, L1_xattn_a1_lnx_b, L1_xattn_a1_lny_g, L1_xattn_a1_lny_b, L1_xattn_a1_ln3_g, L1_xattn_a1_ln3_b, L1_xattn_a1_li2_w, L1_xattn_a1_li2_b, L1_xattn_a1_li3_w, L1_xattn_a1_li3_b, L1_xattn_a2_wq, L1_xattn_a2_wk, L1_xattn_a2_wv, L1_xattn_a2_li1_w, L1_xattn_a2_li1_b, L1_xattn_a2_lnx_g, L1_xattn_a2_lnx_b, L1_xattn_a2_lny_g, L1_xattn_a2_lny_b, L1_xattn_a2_ln3_g, L1_xattn_a2_ln3_b, L1_xattn_a2_li2_w, L1_xattn_a2_li2_b, L1_xattn_a2_li3_w, L1_xattn_a2_li3_b, L1_ffn_gate_w, L1_ffn_expert_gate, L1_ffn_expert_up, L1_ffn_expert_down, L1_ffn_shared_gate, L1_ffn_shared_up, L1_ffn_shared_down, L2_xattn_Wq, L2_xattn_bq, L2_xattn_Wk, L2_xattn_bk, L2_xattn_Wv, L2_xattn_bv, L2_ffn_k0, L2_ffn_k1, L2_ffn_k2, L2_ffn_s0, L2_ffn_s1, L2_ffn_s2, L3_xattn_Wq, L3_xattn_bq, L3_xattn_Wk, L3_xattn_bk, L3_xattn_Wv, L3_xattn_bv, L3_xattn_Wo, L3_xattn_bo, L3_ffn_w_freq_real, L3_ffn_w_freq_imag, L3_ffn_bias):
    import jax
    import jax.numpy as jnp

    def _L0_xattn_ref(q, k, v, Wq, bq, Wk, bk, Wv, bv, Wo, bo):
        import jax, jax.numpy as jnp
        import numpy as np
        HEADS = 16
        D_MODEL = 128
        IMG_MODEL = 64
        D_K = D_MODEL // HEADS
        B, LQ, _ = q.shape
        LKV = k.shape[1]
        qh = (q @ Wq + bq).reshape(B, LQ, HEADS, D_K).transpose(0, 2, 1, 3)
        kh = (k @ Wk + bk).reshape(B, LKV, HEADS, D_K).transpose(0, 2, 1, 3)
        vh = (v @ Wv + bv).reshape(B, LKV, HEADS, D_K).transpose(0, 2, 1, 3)
        scale = 1.0 / np.sqrt(D_K)
        scores = jnp.einsum('bhqd,bhkd->bhqk', qh, kh) * scale
        attn = jax.nn.softmax(scores, axis=-1)
        out = jnp.einsum('bhqk,bhkd->bhqd', attn, vh)
        concat = out.transpose(0, 2, 1, 3).reshape(B, LQ, D_MODEL)
        return concat @ Wo + bo

    def _L0_ffn_ref(x, gate_w, dense_1_w, dense_1_b, dense_2_w, dense_2_b):
        import jax, jax.numpy as jnp
        import numpy as np
        ALPHA = 1.702
        LIMIT = 9.0
        TOP_K = 2

        def swiglu(x):
            g, v = (x[..., 0::2], x[..., 1::2])
            g = jnp.clip(g, None, LIMIT)
            v = jnp.clip(v, -LIMIT, LIMIT)
            return g * jax.nn.sigmoid(ALPHA * g) * (v + 1)
        B, L, D = x.shape
        xf = x.reshape(B * L, D)
        gate = xf @ gate_w
        weights, sel = jax.lax.top_k(gate, k=TOP_K)
        weights = jax.nn.softmax(weights, axis=-1)
        h = jnp.einsum('ecd,td->tec', dense_1_w, xf) + dense_1_b[None]
        h = swiglu(h)
        y = jnp.einsum('edf,tef->ted', dense_2_w, h) + dense_2_b[None]
        y_sel = jnp.take_along_axis(y, sel[:, :, None], axis=1)
        out = jnp.einsum('tkd,tk->td', y_sel, weights)
        return out.reshape(B, L, D)

    def _L1_xattn_ref(xx, ee, ln1_g, ln1_b, ln2_g, ln2_b, a1_wq, a1_wk, a1_wv, a1_li1_w, a1_li1_b, a1_lnx_g, a1_lnx_b, a1_lny_g, a1_lny_b, a1_ln3_g, a1_ln3_b, a1_li2_w, a1_li2_b, a1_li3_w, a1_li3_b, a2_wq, a2_wk, a2_wv, a2_li1_w, a2_li1_b, a2_lnx_g, a2_lnx_b, a2_lny_g, a2_lny_b, a2_ln3_g, a2_ln3_b, a2_li2_w, a2_li2_b, a2_li3_w, a2_li3_b, training):
        import jax, jax.numpy as jnp
        import numpy as np
        H, D, C1, C2, S, M, B, W = (16, 32, 128, 64, 256, 64, 2, 4)

        def _ln(x, g, b):
            m = jnp.mean(x, -1, keepdims=True)
            v = jnp.var(x, -1, keepdims=True)
            return (x - m) * jax.lax.rsqrt(v + 1e-05) * g + b

        def _mha(x, y, wq, wk, wv, li1_w, li1_b, lnx_g, lnx_b, lny_g, lny_b, ln3_g, ln3_b, li2_w, li2_b, li3_w, li3_b, causal):
            xn = _ln(x, lnx_g, lnx_b)
            yn = _ln(y, lny_g, lny_b)
            q = jnp.einsum('bsc,hcd->bhsd', xn, wq)
            k = jnp.einsum('btc,hcd->bhtd', yn, wk)
            v = jnp.einsum('btc,hcd->bhtd', yn, wv)
            a = jax.nn.softmax(jnp.einsum('bhsd,bhtd->bhst', q, k) * D ** (-0.5), axis=-1)
            if causal:
                s, t = (a.shape[-2], a.shape[-1])
                mask = (jnp.arange(t)[None, :] > jnp.arange(s)[:, None]).astype(a.dtype)
                a = a * mask
            o = jnp.einsum('bhst,bhtd->bhsd', a, v)
            o = o.transpose(0, 2, 1, 3).reshape(x.shape[0], x.shape[1], H * D)
            x_out = x + o @ li1_w + li1_b
            h = jax.nn.gelu(_ln(x_out, ln3_g, ln3_b) @ li2_w + li2_b, approximate=False)
            return x_out + h @ li3_w + li3_b
        x = _ln(xx, ln1_g, ln1_b)
        x = x + _mha(x, x, a1_wq, a1_wk, a1_wv, a1_li1_w, a1_li1_b, a1_lnx_g, a1_lnx_b, a1_lny_g, a1_lny_b, a1_ln3_g, a1_ln3_b, a1_li2_w, a1_li2_b, a1_li3_w, a1_li3_b, causal=True)
        x = _ln(x, ln2_g, ln2_b)
        return x + _mha(x, ee, a2_wq, a2_wk, a2_wv, a2_li1_w, a2_li1_b, a2_lnx_g, a2_lnx_b, a2_lny_g, a2_lny_b, a2_ln3_g, a2_ln3_b, a2_li2_w, a2_li2_b, a2_li3_w, a2_li3_b, causal=False)

    def _L1_ffn_ref(hidden_states, gate_w, expert_gate, expert_up, expert_down, shared_gate, shared_up, shared_down):
        import jax, jax.numpy as jnp
        import numpy as np
        TOP_K = 4
        B, S, H = hidden_states.shape
        E = gate_w.shape[0]
        x = hidden_states.reshape(-1, H)
        T = x.shape[0]
        scores = jax.nn.sigmoid(x @ gate_w.T)
        topk_w, topk_idx = jax.lax.top_k(scores, TOP_K)
        topk_w = topk_w / (topk_w.sum(-1, keepdims=True) + 1e-20)
        combine = jnp.zeros((T, E), x.dtype).at[jnp.arange(T)[:, None], topk_idx].add(topk_w)
        g = jax.nn.silu(jnp.einsum('th,ehi->tei', x, expert_gate))
        u = jnp.einsum('th,ehi->tei', x, expert_up)
        expert_out = jnp.einsum('tei,eih->teh', g * u, expert_down)
        y = jnp.einsum('te,teh->th', combine, expert_out)
        sg = jax.nn.silu(x @ shared_gate)
        shared_out = sg * (x @ shared_up) @ shared_down
        return (y + shared_out).reshape(B, S, H)

    def _L2_xattn_ref(query, key, value, Wq, bq, Wk, bk, Wv, bv):
        import jax, jax.numpy as jnp
        import numpy as np
        B, LQ, LK = (8, 256, 256)
        QD, KD, VD = (128, 64, 64)
        q = jnp.einsum('bld,de->ble', query, Wq) + bq
        k = jnp.einsum('bld,de->ble', key, Wk) + bk
        v = jnp.einsum('bld,de->ble', value, Wv) + bv
        scores = jnp.einsum('bqe,bke->bqk', q, k)
        attn = jax.nn.softmax(scores, axis=-1)
        out = jnp.einsum('bqk,bke->bqe', attn, v)
        return out

    def _L2_ffn_ref(x, k0, k1, k2, s0, s1, s2):
        import jax, jax.numpy as jnp
        import numpy as np
        import math
        D_IN = 128
        FEATURES = (512, 512, 128)
        BATCH, SEQ = (8, 256)

        def _conn_dense(kernel_bool, x):
            w = jnp.where(kernel_bool, jnp.float32(1.0), jnp.float32(-1.0))
            return x @ w
        h = jnp.concatenate([x, -x], axis=-1)
        h = s0 * _conn_dense(k0, h)
        h = jax.nn.relu(h) * 2
        h = s1 * _conn_dense(k1, h)
        h = jax.nn.relu(h) * 2
        h = s2 * _conn_dense(k2, h)
        return h

    def _L3_xattn_ref(q, k, v, Wq, bq, Wk, bk, Wv, bv, Wo, bo):
        import jax, jax.numpy as jnp
        import numpy as np
        HEADS = 16
        D_MODEL = 128
        IMG_MODEL = 64
        D_K = D_MODEL // HEADS
        B, LQ, _ = q.shape
        LKV = k.shape[1]
        qh = (q @ Wq + bq).reshape(B, LQ, HEADS, D_K).transpose(0, 2, 1, 3)
        kh = (k @ Wk + bk).reshape(B, LKV, HEADS, D_K).transpose(0, 2, 1, 3)
        vh = (v @ Wv + bv).reshape(B, LKV, HEADS, D_K).transpose(0, 2, 1, 3)
        scale = 1.0 / np.sqrt(D_K)
        scores = jnp.einsum('bhqd,bhkd->bhqk', qh, kh) * scale
        attn = jax.nn.softmax(scores, axis=-1)
        out = jnp.einsum('bhqk,bhkd->bhqd', attn, vh)
        concat = out.transpose(0, 2, 1, 3).reshape(B, LQ, D_MODEL)
        return concat @ Wo + bo

    def _L3_ffn_ref(x, w_freq_real, w_freq_imag, bias):
        import jax, jax.numpy as jnp
        import numpy as np
        B, N, D = (4, 256, 128)
        SPARSITY = 0.01
        w = jax.lax.complex(w_freq_real, w_freq_imag)
        x_freq = jnp.fft.fft(x, axis=-1)
        y_freq = jnp.einsum('bnd,do->bno', x_freq, w)
        y = jnp.real(jnp.fft.ifft(y_freq, axis=-1))
        return y + bias
    x = x + jnp.tanh(g_xattn[0]) * _L0_xattn_ref(_layernorm(x, axis=-1), ctx_512, ctx_512, L0_xattn_Wq, L0_xattn_bq, L0_xattn_Wk, L0_xattn_bk, L0_xattn_Wv, L0_xattn_bv, L0_xattn_Wo, L0_xattn_bo)
    x = x + jnp.tanh(g_ffn[0]) * _L0_ffn_ref(_layernorm(x, axis=-1), L0_ffn_gate_w, L0_ffn_dense_1_w, L0_ffn_dense_1_b, L0_ffn_dense_2_w, L0_ffn_dense_2_b)
    x = x + jnp.tanh(g_xattn[1]) * _L1_xattn_ref(_layernorm(x, axis=-1), ctx_512, L1_xattn_ln1_g, L1_xattn_ln1_b, L1_xattn_ln2_g, L1_xattn_ln2_b, L1_xattn_a1_wq, L1_xattn_a1_wk, L1_xattn_a1_wv, L1_xattn_a1_li1_w, L1_xattn_a1_li1_b, L1_xattn_a1_lnx_g, L1_xattn_a1_lnx_b, L1_xattn_a1_lny_g, L1_xattn_a1_lny_b, L1_xattn_a1_ln3_g, L1_xattn_a1_ln3_b, L1_xattn_a1_li2_w, L1_xattn_a1_li2_b, L1_xattn_a1_li3_w, L1_xattn_a1_li3_b, L1_xattn_a2_wq, L1_xattn_a2_wk, L1_xattn_a2_wv, L1_xattn_a2_li1_w, L1_xattn_a2_li1_b, L1_xattn_a2_lnx_g, L1_xattn_a2_lnx_b, L1_xattn_a2_lny_g, L1_xattn_a2_lny_b, L1_xattn_a2_ln3_g, L1_xattn_a2_ln3_b, L1_xattn_a2_li2_w, L1_xattn_a2_li2_b, L1_xattn_a2_li3_w, L1_xattn_a2_li3_b, 0)
    x = x + jnp.tanh(g_ffn[1]) * _L1_ffn_ref(_layernorm(x, axis=-1), L1_ffn_gate_w, L1_ffn_expert_gate, L1_ffn_expert_up, L1_ffn_expert_down, L1_ffn_shared_gate, L1_ffn_shared_up, L1_ffn_shared_down)
    x = x + jnp.tanh(g_xattn[2]) * _L2_xattn_ref(_layernorm(x, axis=-1), ctx_512, ctx_512, L2_xattn_Wq, L2_xattn_bq, L2_xattn_Wk, L2_xattn_bk, L2_xattn_Wv, L2_xattn_bv)
    x = x + jnp.tanh(g_ffn[2]) * _L2_ffn_ref(_layernorm(x, axis=-1), L2_ffn_k0, L2_ffn_k1, L2_ffn_k2, L2_ffn_s0, L2_ffn_s1, L2_ffn_s2)
    x = x + jnp.tanh(g_xattn[3]) * _L3_xattn_ref(_layernorm(x, axis=-1), ctx_512, ctx_512, L3_xattn_Wq, L3_xattn_bq, L3_xattn_Wk, L3_xattn_bk, L3_xattn_Wv, L3_xattn_bv, L3_xattn_Wo, L3_xattn_bo)
    x = x + jnp.tanh(g_ffn[3]) * _L3_ffn_ref(_layernorm(x, axis=-1), L3_ffn_w_freq_real, L3_ffn_w_freq_imag, L3_ffn_bias)
    return x

_drawn_inputs = setup_inputs


def setup_inputs(seed=0):
    import zlib

    import numpy as np

    out = dict(_drawn_inputs(seed))
    spreads = {'L0_xattn_bq': (0.0, 0.1),
     'L0_xattn_bk': (0.0, 2.0),
     'L0_xattn_bv': (0.0, 0.1),
     'L0_xattn_bo': (0.0, 0.1),
     'L0_ffn_dense_1_b': (0.0, 0.1),
     'L0_ffn_dense_2_b': (0.0, 0.1),
     'L1_xattn_ln1_g': (1.0, 0.2),
     'L1_xattn_ln1_b': (0.0, 0.1),
     'L1_xattn_ln2_g': (1.0, 0.2),
     'L1_xattn_ln2_b': (0.0, 0.1),
     'L1_xattn_a1_li1_b': (0.0, 0.1),
     'L1_xattn_a1_lnx_g': (1.0, 0.6),
     'L1_xattn_a1_lnx_b': (0.0, 0.8),
     'L1_xattn_a1_lny_g': (1.0, 0.6),
     'L1_xattn_a1_lny_b': (0.0, 0.8),
     'L1_xattn_a1_ln3_g': (1.0, 0.6),
     'L1_xattn_a1_ln3_b': (0.0, 0.8),
     'L1_xattn_a1_li2_b': (0.0, 0.329),
     'L1_xattn_a1_li3_b': (0.0, 0.1),
     'L1_xattn_a2_li1_b': (0.0, 0.1),
     'L1_xattn_a2_lnx_g': (1.0, 0.6),
     'L1_xattn_a2_lnx_b': (0.0, 0.8),
     'L1_xattn_a2_lny_g': (1.0, 0.6),
     'L1_xattn_a2_lny_b': (0.0, 0.8),
     'L1_xattn_a2_ln3_g': (1.0, 0.6),
     'L1_xattn_a2_ln3_b': (0.0, 0.8),
     'L1_xattn_a2_li2_b': (0.0, 0.321),
     'L1_xattn_a2_li3_b': (0.0, 0.1),
     'L2_xattn_bq': (0.0, 2.0),
     'L2_xattn_bk': (0.0, 2.0),
     'L2_xattn_bv': (0.0, 0.429),
     'L3_xattn_bq': (0.0, 0.765),
     'L3_xattn_bk': (0.0, 2.0),
     'L3_xattn_bv': (0.0, 0.562),
     'L3_xattn_bo': (0.0, 0.506)}
    factors = {'g_ffn': 7.214,
     'L1_xattn_a1_wq': 8.0,
     'L1_xattn_a1_wk': 8.0,
     'L1_xattn_a2_wq': 8.0,
     'L1_xattn_a2_wk': 8.0,
     'L1_ffn_gate_w': 8.0,
     'L1_ffn_expert_gate': 8.0,
     'L1_ffn_expert_up': 8.0,
     'L1_ffn_expert_down': 8.0,
     'L1_ffn_shared_gate': 8.0,
     'L1_ffn_shared_up': 8.0,
     'L1_ffn_shared_down': 8.0,
     'L2_xattn_Wq': 4.865,
     'L2_xattn_Wk': 4.864,
     'L3_ffn_bias': 27.808}
    for name, (base, spread) in spreads.items():
        noise = np.random.default_rng([zlib.crc32(name.encode()), seed]).standard_normal(out[name].shape)
        drawn = base * np.exp(spread * noise) if base else spread * noise
        out[name] = jnp.asarray(drawn.astype(out[name].dtype))
    for name, factor in factors.items():
        out[name] = (out[name] * factor).astype(out[name].dtype)
    return out
```

```python
from contextlib import ExitStack

import numpy as np

import concourse.bass as bass
from concourse import mybir

F32 = mybir.dt.float32
F32R = mybir.dt.float32r
BF16 = mybir.dt.bfloat16
U32 = mybir.dt.uint32
U8 = mybir.dt.uint8
ALU = mybir.AluOpType
ACT = mybir.ActivationFunctionType
AX = mybir.AxisListType.X

P = 128
B, T, D = 4, 512, 128
NT = T // P
PAIR = 2
NK, NKE = 77, 78
NC = 64
H = 16
DH = 32
KSLOT = 80
STK = 96
STKM = STK + 8
E0, F0 = 8, 256
E1, F1 = 16, 64
EPS = 1e-5



def _layout(items):
    out, at = {}, 0
    for name, width in items:
        out[name] = (at, width)
        at += width
    return out, at


SPLIT, N_SPLIT = _layout([
    ("L0q", 128), ("L3q", 128), ("L2q", 128), ("g0", E0), ("g1", E1),
    ("a1q", 512), ("a1k", 512), ("a1v", 512), ("a1li2", 512), ("a2q", 512), ("a2li2", 512),
    ("eg", 1024), ("sg", 128), ("eu", 1024), ("su", 128), ("M", 128)])
N_STAGED = SPLIT["M"][0]
WF, N_WF = _layout([("L0o", 128), ("L3o", 128), ("a1li1", 512), ("a1li3", 512), ("a2li1", 512), ("a2li3", 512)])
W64, N_W64 = _layout([("L0k", 128), ("L0v", 128), ("L2k", 128), ("L2v", 128), ("L3k", 128), ("L3v", 128),
                      ("a2k", 512), ("a2v", 512)])
ROW, N_ROW = _layout([(n, 128) for n in (
    "L0bv", "L2bv", "L3bv", "L0bo", "L3bo", "L3fb", "a1li1b", "a1li3b", "a2li1b", "a2li3b",
    "ln1g", "ln1b", "ln2g", "ln2b")])
COL, N_COL = _layout([
    ("L0bq", 1), ("L0bk", 1), ("L2bq", 1), ("L2bk", 1), ("L3bq", 1), ("L3bk", 1),
    ("a1gx", 1), ("a1bx", 1), ("a1gy", 1), ("a1by", 1), ("a1g3", 1), ("a1b3", 1), ("a1li2b", 4),
    ("a2gx", 1), ("a2bx", 1), ("a2gy", 1), ("a2by", 1), ("a2g3", 1), ("a2b3", 1), ("a2li2b", 4),
    ("b1", 4 * E0), ("gx", 4), ("gf", 4), ("s", 3)])
CST, N_CST = _layout([
    ("ident", 128), ("mask", 128), ("ones", 128), ("onesm", 160), ("ksel", 4), ("iota", 16), ("half", 8),
    ("C", 128), ("S", 128), ("nS", 128), ("Cn", 128), ("nSn", 128)])
N_CST_KEPT = CST["C"][0]


class Ring:

    def __init__(self, banks, full, free):
        self.banks, self.full, self.free = banks, full, free
        self.n, self.number = 0, {}

    def fill(self, pe, name):
        n = self.number[name] = self.n
        self.n += 1
        if n >= len(self.banks):
            pe.wait_ge(self.free, n - len(self.banks) + 1)
        return self.banks[n % len(self.banks)]

    def read(self, eng, name):
        n = self.number[name]
        eng.wait_ge(self.full, n + 1)
        return self.banks[n % len(self.banks)]

    def done(self, eng, name):
        eng.wait_ge(self.free, self.number[name] + 1)


class Chain:

    def __init__(self, eng, sem):
        self.eng, self.sem, self.n = eng, sem, 0

    def link(self, ins):
        ins.then_inc(self.sem, 1)
        self.n += 1
        self.eng.wait_ge(self.sem, self.n)


def f32(ap):
    return ap.bitcast(F32)


class Core:

    def __init__(self, nc, io, ctx):
        self.nc, self.io = nc, io
        self.ctx = ctx
        self.psum = ctx.enter_context(nc.psum_tensor("banks", [P, 8, T], F32))
        sb = self.sb(ctx)
        self.x = sb("x_res", [P, PAIR * NT, D])
        self.n = sb("x_norm", [P, PAIR * NT, D])
        self.nh = sb("normT_hi", [P, PAIR, T], F32R)
        self.nl = sb("normT_lo", [P, PAIR, T], F32R)
        self.wh = sb("w_hi", [P, N_SPLIT], F32R)
        self.wl = sb("w_lo", [P, N_SPLIT], F32R)
        self.wf = sb("w_f32", [P, N_WF])
        self.w64 = sb("w_ctx", [NC, N_W64])
        self.row = sb("rows", [P, N_ROW])
        self.col = sb("cols", [P, N_COL])
        self.cst = sb("consts", [P, N_CST_KEPT])
        self.identb = sb("ident_bf", [P, P], BF16)
        self.ones2 = sb("ones2_bf", [2, NKE], BF16)
        self.sel48 = sb("sel48_bf", [3 * E1, E1 // 2 * P], BF16)
        self.ctxp = sb("ctxT_pair", [NC, PAIR, NKE])
        self.ctxr = sb("ctx_pair", [NK, PAIR, NC])
        self.tg = sb("tanh_g", [P, 8])
        self.bias = sb("proj_bias", [P, 24])
        self.vb1 = sb("a1_vbias", [P, 512])
        self.vb2 = sb("a2_vbias", [P, 512])
        self.qs = sb("q_stack", [P, 3, 4, T], F32R)
        self.x1 = sb("x_inner", [P, PAIR * NT, D])
        self.st = sb("bn_stats", [P, PAIR * NT, 6])
        self.mv = sb("mean_var", [P, PAIR * NT, 2])
        self.ve = sb("var_eps", [P, PAIR * NT])
        self.rstd = sb("rstd", [P, PAIR * NT])
        self.qkd = nc.dram_tensor("qk_scratch", (PAIR, 2, 4, 2, P, T), F32).ap()
        self.kd = nc.dram_tensor("k_scratch", (PAIR, 4, 2, P, NKE), F32).ap()

    def sb(self, ctx, prefix=""):
        nc = self.nc
        return lambda name, shape, dt=F32: ctx.enter_context(nc.sbuf_tensor(prefix + name, shape, dt))

    def W(self, name, hi, a=0, b=None):
        s, w = SPLIT[name]
        return (self.wh if hi else self.wl)[:, s + a:s + (w if b is None else b)]

    def F(self, name, a=0, b=None):
        s, w = WF[name]
        return self.wf[:, s + a:s + (w if b is None else b)]

    def X(self, name, a=0, b=None):
        s, w = W64[name]
        return self.w64[:, s + a:s + (w if b is None else b)]

    def R(self, name):
        s, w = ROW[name]
        return self.row[:, s:s + w]

    def rows(self, name, n):
        s, w = ROW[name]
        return self.row[:, s:s + w].unsqueeze(1).to_broadcast([P, n, w])

    def Cc(self, name, k=0, p=P):
        s, _ = COL[name]
        return self.col[0:p, s + k:s + k + 1]

    def K(self, name, a=0, b=None, p=P):
        s, w = CST[name]
        return self.cst[0:p, s + a:s + (w if b is None else b)]

    def toks(self, t, u):
        return t[:, NT * u:NT * u + NT, :]


class Block:

    def __init__(self, core, name):
        self.core, self.name, self.nc = core, name, core.nc

    def __enter__(self):
        self.stack = ExitStack()
        self.sems = []
        bk = self.core.psum
        one = lambda i: bk[:, i, :]
        self.A = Ring([one(0), one(1)], self.sem("A_full"), self.sem("A_free"))
        self.D = Ring([one(2), one(3)], self.sem("D_full"), self.sem("D_free"))
        self.O = Ring([one(4), one(6)], self.sem("O_full"), self.sem("O_free"))
        self.S = Ring([one(5), one(7)], self.sem("S_full"), self.sem("S_free"))
        self.block = self.stack.enter_context(self.nc.Block())
        return self

    def sem(self, name):
        s = self.stack.enter_context(self.nc.semaphore(f"{self.name}_{name}"))
        self.sems.append(s.num)
        return s

    def __exit__(self, *_):
        self.stack.close()
        self.nc.all_engine_barrier(sems_to_clear=range(min(self.sems), max(self.sems) + 1))
        return False


class Norm:

    def __init__(self, b, name, src, dst, width=D, parts=P, tiles=PAIR * NT):
        self.core, self.src, self.dst = b.core, src, dst
        self.tiles, self.parts = tiles, parts
        self.s_var = b.sem(name + "_var")
        self.s_rstd = b.sem(name + "_rstd")
        self.s_n = b.sem(name + "_n")

    def vector_stats(self, v, ch):
        c, p = self.core, self.parts
        for t in range(self.tiles):
            last = v.bn_stats(c.st[0:p, t, :], self.src[:, t, :])
        ch.link(last)
        for t in range(self.tiles):
            last = v.bn_aggr(c.mv[0:p, t, :], c.st[0:p, t, :])
        ch.link(last)
        v.tensor_scalar(c.ve[0:p, 0:self.tiles], c.mv[0:p, 0:self.tiles, 1], EPS, None, ALU.add).then_inc(self.s_var, 1)

    def gpsimd(self, g):
        c, p = self.core, self.parts
        g.wait_ge(self.s_var, 1)
        g.tensor_tensor(c.rstd[0:p, 0:self.tiles], c.ve[0:p, 0:self.tiles], c.K("half", 0, self.tiles, p), ALU.pow)\
            .then_inc(self.s_rstd, 1)

    def vector_apply(self, v):
        c, p = self.core, self.parts
        v.wait_ge(self.s_rstd, 1)
        for t in range(self.tiles):
            ins = v.tensor_scalar(self.dst[:, t, :], self.src[:, t, :], c.mv[0:p, t, 0:1], c.rstd[0:p, t:t + 1],
                                  ALU.subtract, ALU.mult)
            if t % (self.tiles // PAIR) == self.tiles // PAIR - 1:
                ins.then_inc(self.s_n, 1)


class Turn:

    def __init__(self, b, name, norm):
        self.b, self.core, self.name, self.norm = b, b.core, name, norm
        self.s_hi = b.sem(name + "_hi")

    def tensor(self, pe):
        for u in range(PAIR):
            pe.wait_ge(self.norm.s_n, u + 1)
            bank = self.b.D.fill(pe, (self.name, u))
            for t in range(NT):
                mm = pe.transpose(bank[:, t * P:(t + 1) * P], self.core.n[:, NT * u + t, :], self.core.K("ident"))
            mm.then_inc(self.b.D.full, 1)

    def scalar(self, a):
        for u in range(PAIR):
            bank = self.b.D.read(a, (self.name, u))
            a.activation(self.core.nh[:, u, :], bank, ACT.Copy).then_inc(self.s_hi, 1)

    def vector(self, v):
        for u in range(PAIR):
            bank = self.b.D.read(v, (self.name, u))
            v.wait_ge(self.s_hi, u + 1)
            v.tensor_tensor(self.core.nl[:, u, :], bank, f32(self.core.nh[:, u, :]), ALU.subtract)\
                .then_inc(self.b.D.free, 1)

    def ready(self, pe, u):
        self.b.D.done(pe, (self.name, u))


def product(pe, core, out, w, u, a=0, b=None):
    pe.matmul(out, core.W(w, 1, a, b), core.nh[:, u, :], start=True, stop=False)
    pe.matmul(out, core.W(w, 1, a, b), core.nl[:, u, :], start=False, stop=False)
    return pe.matmul(out, core.W(w, 0, a, b), core.nh[:, u, :], start=False, stop=True)


def product_rows(pe, core, out, w, u, t, a=0, b=None):
    tok = slice(t * P, (t + 1) * P)
    pe.matmul(out, core.nh[:, u, tok], core.W(w, 1, a, b), start=True, stop=False)
    pe.matmul(out, core.nl[:, u, tok], core.W(w, 1, a, b), start=False, stop=False)
    return pe.matmul(out, core.nh[:, u, tok], core.W(w, 0, a, b), start=False, stop=True)


class Attention:

    def __init__(self, b, name, kind, t, scale, wq, bq, wk, bk):
        self.b, self.core, self.name, self.kind, self.t, self.scale = b, b.core, name, kind, t, scale
        self.wq, self.bq, self.wk, self.bk = wq, bq, wk, bk
        self.own = kind == "self"
        self.narrow = kind == "narrow"
        self.nkt = NT if self.own else 1
        self.keys = P if self.own else NK
        self.steps = [(u, m) for u in range(PAIR) for m in range(4)]
        self.tiles = 1 if self.narrow else 4
        self.items = []
        for u in range(PAIR):
            for m in range(self.tiles):
                self.items += [(u, 0, m), (u, 1, m)]
        self.s_hi = b.sem("a_hi")
        self.s_out = [b.sem(f"a_out{i}") for i in range(2)]
        self.s_q = [b.sem(f"a_q{i}") for i in range(3)]
        self.s_k = b.sem("a_k")
        self.s_nm = b.sem("a_nm")
        self.s_pm = b.sem("a_pm")
        self.s_pv = b.sem("a_pv")
        self.s_rs = b.sem("a_rs")
        self.s_v = b.sem("a_v")

    def last_of_unit(self, i):
        n, kt = divmod(i, self.nkt)
        return kt == self.nkt - 1 and (not self.narrow or self.steps[n][1] == 3)

    def sums(self, n):
        u, m = self.steps[n]
        return (self.name, "sum", u) if self.narrow else (self.name, "sum", u, m)

    def wait_pv(self, eng, i):
        if self.last_of_unit(i):
            self.b.S.read(eng, self.sums(i // self.nkt))
        else:
            eng.wait_ge(self.s_pv, sum(not self.last_of_unit(j) for j in range(i + 1)))

    def head(self, m, lane):
        return 4 * lane + m if self.narrow else 4 * m + lane

    def n_keys(self, kind):
        return T if (self.own or not kind) else NKE

    def tensor_project(self, pe, turn):
        c = self.core
        for j, (u, kind, m) in enumerate(self.items):
            if m == 0 and kind == 0:
                turn.ready(pe, u)
            bank = self.b.D.fill(pe, (self.name, "p", j))
            cols = (m * P, m * P + P)
            if kind == 0 or self.own:
                mm = product(pe, c, bank, self.wk if kind else self.wq, u, *cols)
            else:
                mm = pe.matmul(bank[:, 0:NKE], c.X(self.wk, *cols), self.t.ctx[:, u, :], start=True, stop=True)
            mm.then_inc(self.b.D.full, 1)

    def scalar_project(self, a):
        for j, (u, kind, m) in enumerate(self.items):
            bank = self.b.D.read(a, (self.name, "p", j))
            w = self.n_keys(kind)
            if j >= 2:
                a.wait_ge(self.s_out[j % 2], 32 * (j // 2))
            a.activation(self.t.sh[:, j % 2, 0:w], bank[:, 0:w], ACT.Identity,
                         bias=(self.bk if kind else self.bq)(m)).then_inc(self.s_hi, 1)

    def vector_project(self, v):
        for j, (u, kind, m) in enumerate(self.items):
            bank = self.b.D.read(v, (self.name, "p", j))
            w = self.n_keys(kind)
            v.wait_ge(self.s_hi, j + 1)
            if j >= 2:
                v.wait_ge(self.s_out[j % 2], 32 * (j // 2))
            v.scalar_tensor_tensor(self.t.sl[:, j % 2, 0:w], bank[:, 0:w], (self.bk if kind else self.bq)(m),
                                   f32(self.t.sh[:, j % 2, 0:w]), ALU.add, ALU.subtract).then_inc(self.b.D.free, 1)

    def dram(self, u, kind, m, part):
        c = self.core
        return c.qkd[u, kind, m, part] if (self.own or not kind) else c.kd[u, m, part]

    def sync_project(self, sp):
        for j, (u, kind, m) in enumerate(self.items):
            self.b.D.done(sp, (self.name, "p", j))
            w = self.n_keys(kind)
            sp.dma_start(self.dram(u, kind, m, 0), f32(self.t.sh[:, j % 2, 0:w])).then_inc(self.s_out[j % 2], 16)
            sp.dma_start(self.dram(u, kind, m, 1), f32(self.t.sl[:, j % 2, 0:w])).then_inc(self.s_out[j % 2], 16)
        for i in range(2):
            sp.wait_ge(self.s_out[i], 32 * (len(self.items) // 2))

    def sync_stacks(self, sp):
        c = self.core
        if not self.own:
            for u in range(PAIR):
                for g, part in enumerate((0, 1, 0)):
                    if self.narrow:
                        sp.dma_start(f32(self.t.ks[32 * g:32 * g + 8, u, :, :]),
                                     c.kd[u, 0, part].rearrange("(h d) n -> d h n", h=H)).then_inc(self.s_k, 16)
                    else:
                        for m in range(4):
                            sp.dma_start(f32(self.t.ks[32 * g:32 * g + 32, u, 4 * m:4 * m + 4, :]),
                                         c.kd[u, m, part].rearrange("(q d) n -> d q n", q=4)).then_inc(self.s_k, 16)
        for n, (u, m) in enumerate(self.steps):
            if n >= 3:
                self.b.A.read(sp, (self.name, "st", n - 3, self.nkt - 1, 3))
            for kind in range(2 if self.own else 1):
                for g, part in enumerate((0, 1, 0) if kind else (0, 0, 1)):
                    if self.narrow:
                        src = c.qkd[u, 0, 0, part].rearrange("(q m d) n -> m d q n", q=4, m=4)[m]
                        dst = c.qs[32 * g:32 * g + 8, n % 3, :, :]
                    else:
                        src = c.qkd[u, kind, m, part].rearrange("(q d) n -> d q n", q=4)
                        dst = (self.t.ks if kind else c.qs)[32 * g:32 * g + 32, n % 3, :, :]
                    sp.dma_start(f32(dst), src).then_inc(self.s_q[n % 3], 16)

    def key_stack(self, n, lane, rows, cols):
        u, m = self.steps[n]
        if self.own:
            return self.t.ks[0:rows, n % 3, lane, cols]
        return self.t.ks[0:rows, u, self.head(m, lane), cols]

    def tensor_scores(self, pe, n, t):
        c = self.core
        u, m = self.steps[n]
        tok = slice(t * P, (t + 1) * P)
        if t == 0:
            pe.wait_ge(self.s_q[n % 3], 16 * (6 if self.own else 3) * (n // 3 + 1))
            if not self.own:
                pe.wait_ge(self.s_k, 16 * (6 if self.narrow else 24))
        for lane in range(4):
            if self.own:
                bank = self.b.D.fill(pe, (self.name, "s", n, t, lane))
                pe.matmul(bank, c.qs[0:STK, n % 3, lane, tok], self.key_stack(n, lane, STK, slice(0, T)),
                          start=True, stop=True).then_inc(self.b.D.full, 1)
            else:
                if lane == 0:
                    bank = self.b.D.fill(pe, (self.name, "s", n, t))
                mm = pe.matmul(bank[:, KSLOT * lane:KSLOT * lane + NKE], c.qs[0:STK, n % 3, lane, tok],
                               self.key_stack(n, lane, STK, slice(0, NKE)), start=True, stop=True)
        if not self.own:
            mm.then_inc(self.b.D.full, 1)

    def vector_max(self, v, n, t):
        if self.own:
            for lane in range(4):
                bank = self.b.D.read(v, (self.name, "s", n, t, lane))
                v.tensor_reduce(self.t.mx[:, t, lane:lane + 1], bank, AX, ALU.max).then_inc(self.b.D.free, 1)
        else:
            bank = self.b.D.read(v, (self.name, "s", n, t))
            v.tensor_reduce(self.t.mx[:, t, :], bank[:, 0:4 * KSLOT].rearrange("p (q k) -> p q k", q=4)[:, :, 0:NK],
                            AX, ALU.max).then_inc(self.b.D.free, 1)
        self.last_max = (n, t)

    def vector_negate(self, v, ch, n):
        last = (self.name, "s", n, 3, 3) if self.own else (self.name, "s", n, 3)
        self.b.D.done(v, last)
        hi, lo = self.t.nm[:, :, :, 0], self.t.nm[:, :, :, 1]
        if n >= 1:
            self.b.A.read(v, (self.name, "nm", n - 1))
        ch.link(v.tensor_scalar(hi, self.t.mx[:, :, :], -1.0, None, ALU.mult))
        v.scalar_tensor_tensor(lo, self.t.mx[:, :, :], -1.0, hi, ALU.mult, ALU.subtract).then_inc(self.s_nm, 1)

    def tensor_turn_max(self, pe, n):
        c = self.core
        pe.wait_ge(self.s_nm, n + 1)
        bank = self.b.A.fill(pe, (self.name, "nm", n)).bitcast(BF16)
        for t in range(NT):
            mm = pe.transpose(bank[STK:STKM, t * P:(t + 1) * P], self.t.nm[:, t, :, :].rearrange("p q e -> p (q e)"),
                              c.identb[:, :])
        mm.then_inc(self.b.A.full, 1)

    def scalar_max(self, a, n):
        bank = self.b.A.read(a, (self.name, "nm", n)).bitcast(BF16)
        a.activation(self.core.qs[STK:STKM, n % 3, :, :],
                     bank[STK:STKM, 0:T].unsqueeze(1).to_broadcast([8, 4, T]), ACT.Copy).then_inc(self.b.A.free, 1)

    def tensor_exps(self, pe, n, kt):
        if kt == 0:
            self.b.A.done(pe, (self.name, "nm", n))
        for lane in range(4):
            bank = self.b.A.fill(pe, (self.name, "st", n, kt, lane))
            cols = slice(kt * P, kt * P + self.keys)
            pe.matmul(bank[0:self.keys, :], self.key_stack(n, lane, STKM, cols),
                      self.core.qs[0:STKM, n % 3, lane, :], start=True, stop=True).then_inc(self.b.A.full, 1)

    def scalar_exps(self, a, n, kt):
        i = n * self.nkt + kt
        if i >= 2:
            self.wait_pv(a, i - 2)
            if self.own:
                a.wait_ge(self.s_pm, i - 1)
        for lane in range(4):
            bank = self.b.A.read(a, (self.name, "st", n, kt, lane))
            a.activation(self.t.p[0:self.keys, i % 2, lane, :], bank[0:self.keys, :], ACT.Exp, scale=self.scale)\
                .then_inc(self.b.A.free, 1)

    def gpsimd_mask(self, g):
        for i in range(len(self.steps) * self.nkt):
            n, kt = divmod(i, self.nkt)
            self.b.A.done(g, (self.name, "st", n, kt, 3))
            if i >= 2:
                self.wait_pv(g, i - 2)
            g.tensor_tensor(self.t.pm[:, i % 2, :, :], self.t.p[:, i % 2, :, kt * P:(kt + 1) * P],
                            self.core.K("mask").unsqueeze(1).to_broadcast([P, 4, P]), ALU.mult).then_inc(self.s_pm, 1)

    def tensor_values(self, pe, n, kt):
        c, k = self.core, self.keys
        u, m = self.steps[n]
        i = n * self.nkt + kt
        if kt == 0 and (not self.narrow or m == 0):
            self.obank = self.b.O.fill(pe, self.sums(n))
            self.sbank = self.b.S.fill(pe, self.sums(n))
        self.b.A.done(pe, (self.name, "st", n, kt, 3))
        if self.own:
            pe.wait_ge(self.s_pm, i + 1)
        first, last = kt == 0 and (not self.narrow or m == 0), self.last_of_unit(i)

        def lanes(bank, stationary, moving, cols, start):
            for q in range(4):
                mm = pe.matmul(bank[32 * q:32 * q + 32, cols], stationary(q), moving(q), start=start, stop=last,
                               skip_group_check=True)
            return mm

        v = lambda q: self.t.v(u, kt, m, q)
        if self.own:
            mm = lanes(self.obank, v, lambda q: self.t.pm[:, i % 2, q, :], slice(kt * P, kt * P + P), first)
            if kt:
                mm = lanes(self.obank, v, lambda q: self.t.p[:, i % 2, q, 0:kt * P], slice(0, kt * P), False)
        else:
            mm = lanes(self.obank, v, lambda q: self.t.p[0:k, i % 2, q, :], slice(0, T), first)
        if last:
            mm.then_inc(self.b.O.full, 1)
        if self.narrow:
            ones = lambda q: c.K("onesm", 32 * m, 32 * m + 32, k)
        else:
            ones = lambda q: c.K("ones", 0, 32, k)
        mm = lanes(self.sbank, ones, lambda q: self.t.p[0:k, i % 2, q, :], slice(0, T), first)
        mm.then_inc(self.b.S.full if last else self.s_pv, 1)

    def scalar_inverse(self, a, n):
        key = self.sums(n)
        k = self.b.S.number[key]
        bank = self.b.S.read(a, key)
        if k:
            a.wait_ge(self.b.O.free, k)
        a.activation(self.t.rs[:, :], bank, ACT.Ln).then_inc(self.b.S.free, 1)
        a.wait_ge(self.b.S.free, k + 1)
        a.activation(self.t.rs[:, :], self.t.rs[:, :], ACT.Exp, scale=-1.0).then_inc(self.s_rs, 1)

    def vector_divide(self, v, n):
        key = self.sums(n)
        bank = self.b.O.read(v, key)
        v.wait_ge(self.s_rs, self.b.O.number[key] + 1)
        v.tensor_tensor(self.t.o(*self.steps[n]), bank, self.t.rs[:, :], ALU.mult).then_inc(self.b.O.free, 1)

    def tensor(self, pe, out):
        for t in range(NT):
            self.tensor_scores(pe, 0, t)
        self.tensor_turn_max(pe, 0)
        for n in range(8):
            for r in range(4):
                if n < 7:
                    self.tensor_scores(pe, n + 1, r)
                if self.own:
                    self.tensor_exps(pe, n, r)
                    if r:
                        self.tensor_values(pe, n, r - 1)
                elif r == 0:
                    self.tensor_exps(pe, n, 0)
            if n < 7:
                self.tensor_turn_max(pe, n + 1)
            self.tensor_values(pe, n, self.nkt - 1)
            if n == 4:
                out(pe, 0)
        out(pe, 1)

    def scalar(self, a):
        self.scalar_max(a, 0)
        for n in range(8):
            for kt in range(self.nkt):
                self.scalar_exps(a, n, kt)
            if n < 7:
                self.scalar_max(a, n + 1)
            if self.last_of_unit(n * self.nkt + self.nkt - 1):
                self.scalar_inverse(a, n)

    def vector(self, v, ch, out):
        for t in range(NT):
            self.vector_max(v, 0, t)
        self.vector_negate(v, ch, 0)
        for n in range(8):
            if n == 5:
                out(v, 0)
            for t in range(NT):
                if n < 7:
                    self.vector_max(v, n + 1, t)
                if t == 0 and n and self.last_of_unit(n * self.nkt - 1):
                    self.vector_divide(v, n - 1)
            if n < 7:
                self.vector_negate(v, ch, n + 1)
        self.vector_divide(v, 7)
        out(v, 1)


def fill_key_ones(v, core, ks, kind):
    s, _ = CST["ksel"]
    one = core.cst[STK:STKM, s:s + 4]
    last = None
    if kind == "self":
        for slot in range(3):
            last = v.tensor_copy(ks[STK:STKM, slot, :, :], one.unsqueeze(2).to_broadcast([8, 4, T]))
    else:
        for u in range(PAIR):
            if kind == "narrow":
                out = ks[STK:STKM, u, :, :].rearrange("p (q m) n -> p q (m n)", q=4)
                last = v.tensor_copy(out, one.unsqueeze(2).to_broadcast([8, 4, 4 * NKE]))
            else:
                out = ks[STK:STKM, u, :, :].rearrange("p (m q) n -> p m q n", q=4)
                last = v.tensor_copy(out, one.unsqueeze(1).unsqueeze(3).to_broadcast([8, 4, 4, NKE]))
    return last


class Space:
    pass


def attention_tensors(core, sb, kind):
    t = Space()
    t.sh = sb("proj_hi", [P, 2, T], F32R)
    t.sl = sb("proj_lo", [P, 2, T], F32R)
    t.mx = sb("score_max", [P, NT, 4])
    t.nm = sb("neg_max", [P, NT, 4, 2], BF16)
    t.p = sb("weights", [P, 2, 4, T])
    t.rs = sb("inv_sums", [P, T])
    if kind == "self":
        t.pm = sb("masked", [P, 2, 4, P])
        t.ks = sb("k_stack", [P, 3, 4, T], F32R)
        t.vv = sb("v_self", [P, PAIR, NT, T])
        t.v = lambda u, kt, m, q: t.vv[:, u, kt, DH * (4 * m + q):DH * (4 * m + q) + DH]
    else:
        t.ks = sb("k_stack", [P, PAIR, H, NKE], F32R)
    if kind == "wide":
        t.vv = sb("v_wide", [P, PAIR, T])
        t.v = lambda u, kt, m, q: t.vv[0:NK, u, DH * (4 * m + q):DH * (4 * m + q) + DH]
    if kind == "narrow":
        t.vv = sb("v_narrow", [P, PAIR, 4, 160])
        t.v = lambda u, kt, m, q: t.vv[0:NK, u, q, 32 * m:32 * m + 32]
        t.ot = sb("heads_out", [P, PAIR, T])
        t.o = lambda u, m: t.ot[:, u, :]
    else:
        t.ot = sb("heads_out", [P, 4, T])
        t.o = lambda u, m: t.ot[:, m, :]
    return t


def block_narrow(core, layer, pair, load):
    L = f"L{layer}"
    with ExitStack() as mem, Block(core, f"{L}x") as b:
        sb = core.sb(mem, b.name + "_")
        t = attention_tensors(core, sb, "narrow")
        t.ctx = core.ctxp
        norm = Norm(b, "norm", core.x, core.n)
        turn = Turn(b, "turn", norm)
        col = lambda name: (lambda m: core.Cc(name))
        att = Attention(b, "att", "narrow", t, (D // H) ** -0.5, L + "q", col(L + "bq"), L + "k", col(L + "bk"))
        s_ld = b.sem("load")
        s_xb = b.sem("xb")
        s_zero = b.sem("zero")
        s_ones = b.sem("ones")
        D_ = b.D

        @b.block.tensor
        def _(pe):
            turn.tensor(pe)
            if load:
                pe.wait_ge(s_ld, 48)
            att.tensor_project(pe, turn)
            for u in range(PAIR):
                bank = D_.fill(pe, ("v", u))
                pe.matmul(bank[0:NK, 0:P], core.ctxp[:, u, 0:NK], core.X(L + "v"), start=True, stop=True)\
                    .then_inc(D_.full, 1)

            def out(pe, u):
                b.O.done(pe, att.sums(4 * u + 3))
                bank = D_.fill(pe, ("o", u))
                for i in range(NT):
                    tok = slice(i * P, i * P + P)
                    mm = pe.matmul(bank[:, tok], t.ot[:, u, tok], core.F(L + "o"), start=True, stop=True)
                mm.then_inc(D_.full, 1)

            att.tensor(pe, out)

        @b.block.vector
        def _(v):
            ch = Chain(v, b.sem("chain"))
            if load:
                v.wait_ge(s_ld, 48)
            norm.vector_stats(v, ch)
            v.wait_ge(s_zero, 1)
            fill_key_ones(v, core, t.ks, "narrow").then_inc(s_ones, 1)
            norm.vector_apply(v)
            turn.vector(v)
            att.vector_project(v)
            for u in range(PAIR):
                bank = D_.read(v, ("v", u))
                v.wait_ge(s_zero, 2)
                v.tensor_tensor(t.vv[0:NK, u, :, :].rearrange("p q (m e) -> p q m e", e=40)[:, :, :, 0:8],
                                bank[0:NK, 0:P].rearrange("p (q m e) -> p q m e", q=4, m=4),
                                core.R(L + "bv")[0:NK].rearrange("p (q m e) -> p q m e", q=4, m=4),
                                ALU.add).then_inc(D_.free, 1)

            def out(v, u):
                bank = D_.read(v, ("o", u))
                v.wait_ge(s_xb, 1)
                x = core.toks(core.x, u).rearrange("p t d -> p (t d)")
                v.scalar_tensor_tensor(x, bank, core.tg[:, layer:layer + 1], x, ALU.mult, ALU.add)\
                    .then_inc(D_.free, 1)

            att.vector(v, ch, out)

        @b.block.scalar
        def _(a):
            turn.scalar(a)
            att.scalar_project(a)
            att.scalar(a)

        @b.block.gpsimd
        def _(g):
            g.memset(f32(t.ks[:, :, :, :]), 0.0).then_inc(s_zero, 1)
            g.memset(t.vv[:, :, :, :], 0.0).then_inc(s_zero, 1)
            norm.gpsimd(g)
            g.wait_ge(norm.s_n, PAIR)
            g.tensor_tensor(core.x[:, :, :], core.x[:, :, :], core.rows(L + "bo", PAIR * NT), ALU.add).then_inc(s_xb, 1)

        @b.block.sync
        def _(sp):
            if load:
                sp.dma_start(core.x[:, :, :], core.io["x"][bass.ds(pair * PAIR, PAIR)]
                             .rearrange("b (t p) d -> p (b t) d", p=P)).then_inc(s_ld, 16)
                sp.dma_start(core.ctxp[:, :, :], core.io["ctxT"][:, bass.ds(pair * PAIR, PAIR), :]).then_inc(s_ld, 16)
                sp.dma_start(core.ctxr[:, :, :], core.io["ctx"][bass.ds(pair * PAIR, PAIR)]
                             .rearrange("b k c -> k b c")).then_inc(s_ld, 16)
            att.sync_project(sp)
            sp.wait_ge(s_ones, 1)
            att.sync_stacks(sp)


def block_experts0(core):
    with ExitStack() as mem, Block(core, "e0") as b:
        sb = core.sb(mem, b.name + "_")
        raw = sb("w1_raw", [P, 2, 4 * F0])
        wl = sb("w1_lo", [P, 2 * E0 * F0], F32R)
        wh = sb("w1_hi", [P, 2 * E0 * F0], F32R)
        w2 = sb("w2", [P, 2 * E0, D])
        b2 = sb("b2", [E0, D])
        bv = sb("b_value", [P, E0, 2])
        lg = sb("logits", [P, PAIR * NT, E0])
        gate = Gate(core, sb, E0)
        wt = sb("w_turned", [E0, PAIR * NT, P])
        gc = sb("gate_clipped", [P, 3, T])
        sg = sb("gate_sigmoid", [P, 3, T])
        vc = sb("value", [P, 3, T])
        h = sb("hidden", [P, 3, T])
        acc = sb("acc", [P, NT, D])
        diff = sb("logit_diff", [P, PAIR * NT])
        w01 = sb("weights01", [P, 2, PAIR * NT])
        comb = sb("combine", [P, PAIR * NT, E0])
        part = sb("combine_part", [P, PAIR * NT, E0])
        norm = Norm(b, "norm", core.x, core.n)
        turn = Turn(b, "turn", norm)
        s_ld = [b.sem(f"load{i}") for i in range(3)]
        s_wh = b.sem("w_hi")
        s_wl = b.sem("w_lo")
        s_diff = b.sem("diff")
        s_w01 = b.sem("w01")
        s_comb = b.sem("comb")
        s_wt = b.sem("wt")
        s_gc = b.D.free
        s_bv = b.sem("bv")
        s_sg = b.sem("sg")
        s_t = b.sem("t")
        s_h = b.sem("h")
        s_y = b.sem("y")
        units = [(u, e, s) for u in range(PAIR) for e in range(E0) for s in range(2)]
        b1, _ = COL["b1"]

        def bias1(e, what, s):
            k = b1 + 4 * e + 2 * what + s
            return core.col[:, k:k + 1]

        def w1(w, e, what, s):
            k = (2 * e + what) * F0 + s * P
            return w[:, k:k + P]

        def chunk(c):
            return slice(4 * F0 * c, 4 * F0 * (c + 1))

        def wait_y(eng, j):
            u, e, s = units[j]
            if s:
                b.O.read(eng, ("y", u, e))
            else:
                eng.wait_ge(s_y, j // 2 + 1)

        @b.block.tensor
        def _(pe):
            turn.tensor(pe)
            bank = b.S.fill(pe, "logits")
            for u in range(PAIR):
                turn.ready(pe, u)
                for i in range(NT):
                    k = E0 * (NT * u + i)
                    mm = product_rows(pe, core, bank[:, k:k + E0], "g0", u, i)
            mm.then_inc(b.S.full, 1)
            def hidden(j):
                u, e, s = units[j]
                if u == 0 and s == 0:
                    pe.wait_ge(s_wl, e // 2 + 1)
                for what, ring in ((0, b.D), (1, b.A)):
                    bank = ring.fill(pe, ("h", j))
                    pe.matmul(bank, w1(wh, e, what, s), core.nh[:, u, :], start=True, stop=False)
                    pe.matmul(bank, w1(wh, e, what, s), core.nl[:, u, :], start=False, stop=False)
                    pe.matmul(bank, w1(wl, e, what, s), core.nh[:, u, :], start=False, stop=True).then_inc(ring.full, 1)

            def down(j):
                u, e, s = units[j]
                if s == 0:
                    self_bank[0] = b.O.fill(pe, ("y", u, e))
                pe.wait_ge(s_h, j + 1)
                for i in range(NT):
                    mm = pe.matmul(self_bank[0][:, i * P:i * P + P], h[:, j % 3, i * P:i * P + P], w2[:, 2 * e + s, :],
                                   start=s == 0 and i == 0, stop=s == 1, skip_group_check=True)
                mm.then_inc(b.O.full if s else s_y, 1)

            self_bank = [None]
            hidden(0)
            hidden(1)
            pe.wait_ge(s_comb, 1)
            pe.wait_ge(s_ld[2], 32)
            for u in range(PAIR):
                bank = b.S.fill(pe, ("wt", u))
                for i in range(NT):
                    mm = pe.transpose(bank[0:E0, i * P:i * P + P], comb[:, NT * u + i, :], core.K("ident"))
                mm.then_inc(b.S.full, 1)
            for u in range(PAIR):
                b.S.done(pe, ("wt", u))
                bank = b.S.fill(pe, ("bias", u))
                for i in range(NT):
                    mm = pe.matmul(bank[:, i * P:i * P + P], wt[:, NT * u + i, :], b2[:, :], start=True, stop=True)
                mm.then_inc(b.S.full, 1)
            for j in range(2, len(units)):
                hidden(j)
                down(j - 2)
            down(len(units) - 2)
            down(len(units) - 1)

        @b.block.scalar
        def _(a):
            turn.scalar(a)
            for c in range(E0 // 2):
                a.wait_ge(s_ld[c % 2], 16 * (c // 2 + 1))
                a.activation(wh[:, chunk(c)], raw[:, c % 2, :], ACT.Copy).then_inc(s_wh, 1)
            a.wait_ge(s_diff, 1)
            a.activation(w01[:, 0, :], diff[:, :], ACT.Sigmoid)
            a.activation(w01[:, 1, :], diff[:, :], ACT.Sigmoid, scale=-1.0).then_inc(s_w01, 1)
            a.wait_ge(s_bv, 1)
            for j, (u, e, s) in enumerate(units):
                bank = b.A.read(a, ("h", j))
                if j >= 3:
                    a.wait_ge(s_h, j - 2)
                a.activation(vc[:, j % 3, :], bank, ACT.Identity, bias=bv[:, e, s:s + 1]).then_inc(b.A.free, 1)
                b.D.done(a, ("h", j))
                a.activation(sg[:, j % 3, :], gc[:, j % 3, :], ACT.Sigmoid, scale=1.702).then_inc(s_sg, 1)

        @b.block.gpsimd
        def _(g):
            norm.gpsimd(g)
            for c in range(E0 // 2):
                g.wait_ge(s_wh, c + 1)
                g.tensor_tensor(wl[:, chunk(c)], raw[:, c % 2, :], f32(wh[:, chunk(c)]), ALU.subtract).then_inc(s_wl, 1)
            for j, (u, e, s) in enumerate(units):
                b.A.done(g, ("h", j))
                g.tensor_scalar(vc[:, j % 3, :], vc[:, j % 3, :], -8.0, 10.0, ALU.max, ALU.min)
                g.wait_ge(s_sg, j + 1)
                g.tensor_tensor(sg[:, j % 3, :], sg[:, j % 3, :], gc[:, j % 3, :], ALU.mult).then_inc(s_t, 1)

        @b.block.vector
        def _(v):
            ch = Chain(v, b.sem("chain"))
            norm.vector_stats(v, ch)
            norm.vector_apply(v)
            v.tensor_scalar(bv[:, :, :], core.col[:, b1:b1 + 4 * E0].rearrange("p (e w s) -> p e w s", e=E0, w=2)[:, :, 1, :],
                            1.0, None, ALU.add).then_inc(s_bv, 1)
            turn.vector(v)
            bank = b.S.read(v, "logits")
            ins = v.tensor_copy(lg[:, :, :], bank[:, 0:PAIR * NT * E0].rearrange("p (t e) -> p t e", e=E0))
            ins.then_inc(b.S.free, 1)
            b.S.done(v, "logits")
            gate.largest(v, ch, lg)
            v.tensor_tensor(diff[:, :], gate.mx[:, :, 0], gate.mx[:, :, 1], ALU.subtract).then_inc(s_diff, 1)
            v.wait_ge(s_w01, 1)
            for k, out in ((0, comb), (1, part)):
                ch.link(gate.one_hot(v, out[:, :, :], k))
                ch.link(v.tensor_tensor(out[:, :, :], out[:, :, :], w01[:, k, :].unsqueeze(2).to_broadcast([P, PAIR * NT, E0]),
                                        ALU.mult))
            ins = v.tensor_tensor(comb[:, :, :], comb[:, :, :], part[:, :, :], ALU.add)
            ins.then_inc(s_comb, 1)
            v.wait_ge(s_comb, 1)

            def clip(j):
                u, e, s = units[j]
                bank = b.D.read(v, ("h", j))
                v.tensor_scalar(gc[:, j % 3, :], bank, bias1(e, 0, s), 9.0, ALU.add, ALU.min).then_inc(b.D.free, 1)

            def combine(u, e):
                bank = b.O.read(v, ("y", u, e))
                if e == 0:
                    src = b.S.read(v, ("bias", u))
                    ins = v.tensor_copy(acc[:, :, :], src.rearrange("p (t d) -> p t d", t=NT))
                    ins.then_inc(b.S.free, 1)
                    b.S.done(v, ("bias", u))
                for i in range(NT):
                    ins = v.scalar_tensor_tensor(acc[:, i, :], bank[:, i * P:i * P + P], comb[:, NT * u + i, e:e + 1],
                                                 acc[:, i, :], ALU.mult, ALU.add)
                ins.then_inc(b.O.free, 1)
                b.O.done(v, ("y", u, e))
                if e == E0 - 1:
                    x = core.toks(core.x, u)
                    ch.link(v.scalar_tensor_tensor(x, acc[:, :, :], core.tg[:, 4:5], x, ALU.mult, ALU.add))

            clip(0)
            clip(1)
            for u in range(PAIR):
                bank = b.S.read(v, ("wt", u))
                v.tensor_copy(wt[:, NT * u:NT * u + NT, :], bank[0:E0, :].rearrange("p (t d) -> p t d", t=NT))\
                    .then_inc(b.S.free, 1)
            n = len(units)
            for j in range(n + 2):
                if 2 <= j < n:
                    clip(j)
                if j < n:
                    v.wait_ge(s_t, j + 1)
                    if j >= 3:
                        wait_y(v, j - 3)
                    v.tensor_tensor(h[:, j % 3, :], sg[:, j % 3, :], vc[:, j % 3, :], ALU.mult).then_inc(s_h, 1)
                k = j - 3
                if k >= 0 and units[k][2]:
                    combine(*units[k][:2])
            combine(*units[n - 1][:2])

        @b.block.sync
        def _(sp):
            for c in range(E0 // 2):
                if c >= 2:
                    sp.wait_ge(s_wl, c - 1)
                sp.dma_start(raw[:, c % 2, :], core.io["w1"][:, chunk(c)]).then_inc(s_ld[c % 2], 16)
                if c == 1:
                    sp.dma_start(w2[:, :, :], core.io["w2"]).then_inc(s_ld[2], 16)
                    sp.dma_start(b2[:, :], core.io["b2"]).then_inc(s_ld[2], 16)


class Gate:

    def __init__(self, core, sb, experts):
        n = PAIR * NT
        self.core, self.experts = core, experts
        self.mx = sb("largest", [P, n, 8])
        self.ix = sb("largest_at", [P, n, 8], U32)
        self.ixf = sb("largest_at_f", [P, n, 8])

    def largest(self, v, ch, scores):
        for t in range(PAIR * NT):
            last = v.max(self.mx[:, t, :], scores[:, t, :])
        ch.link(last)
        for t in range(PAIR * NT):
            last = v.max_index(self.ix[:, t, :], self.mx[:, t, :], scores[:, t, :])
        ch.link(last)
        ch.link(v.tensor_copy(self.ixf[:, :, :], self.ix[:, :, :]))

    def one_hot(self, v, out, k):
        n = PAIR * NT
        return v.tensor_tensor(out, self.core.K("iota", 0, self.experts).unsqueeze(1).to_broadcast([P, n, self.experts]),
                               self.ixf[:, :, k:k + 1].to_broadcast([P, n, self.experts]), ALU.is_equal)


class Tail:

    def __init__(self, b, a, att, xo, k_bias):
        self.b, self.core, self.a, self.att, self.xo, self.k_bias = b, b.core, a, att, xo, k_bias
        self.s_xb = b.sem("t_xb")
        self.s_xo = b.sem("t_xo")
        self.s_r = b.sem("t_r")
        self.norm = Norm(b, "t_norm", xo, b.core.n)
        self.turn = Turn(b, "t_turn", self.norm)

    def hidden(self, u, m):
        t = self.att.t
        return (t.sh, t.sl)[m // 2][:, m % 2, :].bitcast(F32) if u else t.ot[:, m, :]

    def tensor_out(self, pe, u):
        b, att = self.b, self.att
        b.O.done(pe, att.sums(4 * u + 3))
        bank = b.D.fill(pe, ("li1", u))
        for i in range(NT):
            tok = slice(i * P, i * P + P)
            for m in range(4):
                mm = pe.matmul(bank[:, tok], att.t.ot[:, m, tok], self.core.F(self.a + "li1", m * P, m * P + P),
                               start=m == 0, stop=m == 3)
        mm.then_inc(b.D.full, 1)

    def vector_out(self, v, u):
        bank = self.b.D.read(v, ("li1", u))
        if u == 0:
            v.wait_ge(self.s_xb, 1)
        x = self.core.toks(self.xo, u).rearrange("p t d -> p (t d)")
        v.tensor_tensor(x, bank, x, ALU.add).then_inc(self.b.D.free, 1)

    def gpsimd_bias(self, g):
        c = self.core
        g.tensor_tensor(self.xo[:, :, :], c.x1[:, :, :], c.rows(self.a + "li1b", PAIR * NT), ALU.add)\
            .then_inc(self.s_xb, 1)

    def tensor(self, pe):
        b, c = self.b, self.core
        self.turn.tensor(pe)
        for u in range(PAIR):
            self.turn.ready(pe, u)
            for m in range(4):
                bank = b.A.fill(pe, ("li2", u, m))
                product(pe, c, bank, self.a + "li2", u, m * P, m * P + P).then_inc(b.A.full, 1)
            if u:
                self.tensor_last(pe, 0)
        self.tensor_last(pe, 1)

    def tensor_last(self, pe, u):
        b, c = self.b, self.core
        bank = b.D.fill(pe, ("li3", u))
        b.A.done(pe, ("li2", u, 3))
        for i in range(NT):
            tok = slice(i * P, i * P + P)
            for m in range(4):
                mm = pe.matmul(bank[:, tok], self.hidden(u, m)[:, tok], c.F(self.a + "li3", m * P, m * P + P),
                               start=m == 0, stop=m == 3)
        mm.then_inc(b.D.full, 1)

    def scalar(self, a):
        self.turn.scalar(a)
        for u in range(PAIR):
            for m in range(4):
                bank = self.b.A.read(a, ("li2", u, m))
                k = self.k_bias + m
                a.activation(self.hidden(u, m), bank, ACT.Gelu, bias=self.core.bias[:, k:k + 1])\
                    .then_inc(self.b.A.free, 1)

    def gpsimd(self, g):
        c = self.core
        self.norm.gpsimd(g)
        s = self.b.sem("t_g")
        g.tensor_tensor(c.x1[:, :, :], c.x1[:, :, :], c.rows(self.a + "li3b", PAIR * NT), ALU.add).then_inc(s, 1)
        g.wait_ge(s, 1)
        g.tensor_tensor(c.x1[:, :, :], c.x1[:, :, :], self.xo[:, :, :], ALU.add).then_inc(self.s_r, 1)

    def vector(self, v, ch):
        self.b.D.done(v, ("li1", 1))
        self.norm.vector_stats(v, ch)
        self.norm.vector_apply(v)
        self.turn.vector(v)
        for u in range(PAIR):
            bank = self.b.D.read(v, ("li3", u))
            v.wait_ge(self.s_r, 1)
            x = self.core.toks(self.core.x1, u).rearrange("p t d -> p (t d)")
            v.tensor_tensor(x, bank, x, ALU.add).then_inc(self.b.D.free, 1)
        self.b.D.done(v, ("li3", 1))


def gains(v, core, ch, name):
    ch.link(v.tensor_tensor(core.x1[:, :, :], core.n[:, :, :], core.rows(name + "g", PAIR * NT), ALU.mult))
    ch.link(v.tensor_tensor(core.x1[:, :, :], core.x1[:, :, :], core.rows(name + "b", PAIR * NT), ALU.add))


def block_self(core):
    with ExitStack() as mem, Block(core, "s1") as b:
        sb = core.sb(mem, b.name + "_")
        t = attention_tensors(core, sb, "self")
        xo = sb("x_out", [P, PAIR * NT, D])
        outer = Norm(b, "outer", core.x, core.n)
        first = Norm(b, "first", core.n, core.n)
        norm = Norm(b, "norm", core.x1, core.n)
        turn = Turn(b, "turn", norm)
        col = lambda k: (lambda m: core.bias[:, k + m:k + m + 1])
        att = Attention(b, "att", "self", t, DH ** -0.5, "a1q", col(0), "a1k", col(4))
        tail = Tail(b, "a1", att, xo, 8)
        last = Norm(b, "last", core.x1, core.n)
        s_ones = b.sem("ones")

        @b.block.tensor
        def _(pe):
            turn.tensor(pe)
            att.tensor_project(pe, turn)
            for u in range(PAIR):
                for kt in range(NT):
                    bank = b.D.fill(pe, ("v", u, kt))
                    product_rows(pe, core, bank, "a1v", u, kt).then_inc(b.D.full, 1)
            b.D.done(pe, ("v", 1, NT - 1))
            att.tensor(pe, tail.tensor_out)
            tail.tensor(pe)

        @b.block.scalar
        def _(a):
            turn.scalar(a)
            att.scalar_project(a)
            att.scalar(a)
            tail.scalar(a)

        @b.block.gpsimd
        def _(g):
            outer.gpsimd(g)
            first.gpsimd(g)
            norm.gpsimd(g)
            tail.gpsimd_bias(g)
            att.gpsimd_mask(g)
            tail.gpsimd(g)
            last.gpsimd(g)

        @b.block.vector
        def _(v):
            ch = Chain(v, b.sem("chain"))
            outer.vector_stats(v, ch)
            outer.vector_apply(v)
            v.wait_ge(outer.s_n, PAIR)
            first.vector_stats(v, ch)
            first.vector_apply(v)
            v.wait_ge(first.s_n, PAIR)
            gains(v, core, ch, "ln1")
            norm.vector_stats(v, ch)
            norm.vector_apply(v)
            fill_key_ones(v, core, t.ks, "self").then_inc(s_ones, 1)
            turn.vector(v)
            att.vector_project(v)
            for u in range(PAIR):
                for kt in range(NT):
                    bank = b.D.read(v, ("v", u, kt))
                    v.tensor_tensor(t.vv[:, u, kt, :], bank, core.vb1[:, :], ALU.add).then_inc(b.D.free, 1)
            att.vector(v, ch, tail.vector_out)
            tail.vector(v, ch)
            last.vector_stats(v, ch)
            last.vector_apply(v)
            v.wait_ge(last.s_n, PAIR)
            gains(v, core, ch, "ln2")

        @b.block.sync
        def _(sp):
            att.sync_project(sp)
            sp.wait_ge(s_ones, 1)
            att.sync_stacks(sp)


def block_wide(core):
    with ExitStack() as mem, Block(core, "w1") as b:
        sb = core.sb(mem, b.name + "_")
        t = attention_tensors(core, sb, "wide")
        t.ctx = sb("ctxT_norm", [NC, PAIR, NKE])
        cn = sb("ctx_norm", [NK, PAIR, NC])
        xo = sb("x_out", [P, PAIR * NT, D])
        cnorm = Norm(b, "cnorm", core.ctxr, cn, parts=NK, tiles=PAIR)
        norm = Norm(b, "norm", core.x1, core.n)
        turn = Turn(b, "turn", norm)
        col = lambda k: (lambda m: core.bias[:, k + m:k + m + 1])
        att = Attention(b, "att", "wide", t, DH ** -0.5, "a2q", col(12), "a2k", col(20))
        tail = Tail(b, "a2", att, xo, 16)
        s_zero = b.sem("zero")
        s_ones = b.sem("ones")

        @b.block.tensor
        def _(pe):
            for u in range(PAIR):
                pe.wait_ge(cnorm.s_n, u + 1)
                bank = b.D.fill(pe, ("ctx", u))
                pe.transpose(bank[0:NC, 0:NK], cn[:, u, :], core.K("ident", 0, NK, NK)).then_inc(b.D.full, 1)
            turn.tensor(pe)
            b.D.done(pe, ("ctx", 1))
            att.tensor_project(pe, turn)
            for u in range(PAIR):
                bank = b.D.fill(pe, ("v", u))
                pe.matmul(bank[0:NK, :], t.ctx[:, u, 0:NK], core.X("a2v"), start=True, stop=True).then_inc(b.D.full, 1)
            b.D.done(pe, ("v", 1))
            att.tensor(pe, tail.tensor_out)
            tail.tensor(pe)

        @b.block.scalar
        def _(a):
            turn.scalar(a)
            att.scalar_project(a)
            att.scalar(a)
            tail.scalar(a)

        @b.block.gpsimd
        def _(g):
            g.memset(t.ctx[:, :, :], 0.0).then_inc(s_zero, 1)
            cnorm.gpsimd(g)
            norm.gpsimd(g)
            tail.gpsimd_bias(g)
            tail.gpsimd(g)

        @b.block.vector
        def _(v):
            ch = Chain(v, b.sem("chain"))
            cnorm.vector_stats(v, ch)
            cnorm.vector_apply(v)
            norm.vector_stats(v, ch)
            norm.vector_apply(v)
            v.wait_ge(s_zero, 1)
            for u in range(PAIR):
                bank = b.D.read(v, ("ctx", u))
                v.tensor_copy(t.ctx[:, u, 0:NK], bank[0:NC, 0:NK]).then_inc(b.D.free, 1)
            fill_key_ones(v, core, t.ks, "wide").then_inc(s_ones, 1)
            turn.vector(v)
            att.vector_project(v)
            for u in range(PAIR):
                bank = b.D.read(v, ("v", u))
                v.tensor_tensor(t.vv[0:NK, u, :], bank[0:NK, :], core.vb2[0:NK, :], ALU.add).then_inc(b.D.free, 1)
            att.vector(v, ch, tail.vector_out)
            tail.vector(v, ch)
            v.scalar_tensor_tensor(core.x[:, :, :], core.x1[:, :, :], core.tg[:, 1:2], core.x[:, :, :], ALU.mult, ALU.add)

        @b.block.sync
        def _(sp):
            att.sync_project(sp)
            sp.wait_ge(s_ones, 1)
            att.sync_stacks(sp)


def block_experts1(core):
    TILES = E1 // 2
    with ExitStack() as mem, Block(core, "e1") as b:
        sb = core.sb(mem, "e1_")
        n = PAIR * NT
        down = sb("w_down", [P, TILES + 1, D])
        gate = Gate(core, sb, E1)
        score = sb("scores", [P, n, E1])
        comb = sb("combine", [P, n, E1])
        hot = sb("one_hot", [P, n, E1])
        total = sb("top_sum", [P, n])
        c3 = sb("combine_parts", [P, n, 3, E1], BF16)
        ct = sb("combine_turned", [3 * E1, PAIR, T], BF16)
        sg = sb("gate_silu", [P, 3, T])
        up = sb("hidden_raw", [P, 3, T])
        h = sb("hidden", [P, 3, T])
        norm = Norm(b, "norm", core.x, core.n)
        turn = Turn(b, "turn", norm)
        s_ld = b.sem("load")
        s_score = b.sem("score")
        s_comb = b.sem("comb")
        s_y = b.sem("y")
        units = [(u, j) for u in range(PAIR) for j in range(TILES + 1)]

        def wait_y(eng, i):
            u, j = units[i]
            if j == TILES:
                b.O.read(eng, ("y", u))
            else:
                eng.wait_ge(s_y, i + 1 - u)

        @b.block.tensor
        def _(pe):
            turn.tensor(pe)
            bank = b.S.fill(pe, "logits")
            for u in range(PAIR):
                turn.ready(pe, u)
                for i in range(NT):
                    k = E1 * (NT * u + i)
                    mm = product_rows(pe, core, bank[:, k:k + E1], "g1", u, i)
            mm.then_inc(b.S.full, 1)

            def hidden(i):
                u, j = units[i]
                for what, ring in ((0, b.A), (1, b.D)):
                    bank = ring.fill(pe, ("h", i))
                    if j < TILES:
                        product(pe, core, bank, ("eg", "eu")[what], u, j * P, j * P + P).then_inc(ring.full, 1)
                    else:
                        product(pe, core, bank, ("sg", "su")[what], u).then_inc(ring.full, 1)
                if j < TILES:
                    bank = b.S.fill(pe, ("c", i))
                    pe.matmul(bank, core.sel48[:, j * P:j * P + P], ct[:, u, :], start=True, stop=True).then_inc(b.S.full, 1)

            def down_sum(i):
                u, j = units[i]
                if j == 0:
                    y[0] = b.O.fill(pe, ("y", u))
                if i == 0:
                    pe.wait_ge(s_ld, 16)
                if j < TILES:
                    b.S.done(pe, ("c", i))
                else:
                    b.D.done(pe, ("h", i))
                for t in range(NT):
                    mm = pe.matmul(y[0][:, t * P:t * P + P], h[:, i % 3, t * P:t * P + P], down[:, j, :],
                                   start=j == 0 and t == 0, stop=j == TILES, skip_group_check=True)
                mm.then_inc(b.O.full if j == TILES else s_y, 1)

            y = [None]
            pe.wait_ge(s_comb, 1)
            for u in range(PAIR):
                bank = b.S.fill(pe, ("ct", u)).bitcast(BF16)
                for t in range(NT):
                    mm = pe.transpose(bank[0:3 * E1, t * P:t * P + P], c3[:, NT * u + t, :, :].rearrange("p k e -> p (k e)"),
                                      core.identb[:, :])
                mm.then_inc(b.S.full, 1)
            b.S.done(pe, ("ct", 1))
            for i in range(len(units)):
                hidden(i)
                if i >= 2:
                    down_sum(i - 2)
            down_sum(len(units) - 2)
            down_sum(len(units) - 1)

        @b.block.scalar
        def _(a):
            turn.scalar(a)
            bank = b.S.read(a, "logits")
            a.activation(score[:, :, :], bank[:, 0:n * E1].rearrange("p (t e) -> p t e", e=E1), ACT.Sigmoid)\
                .then_inc(b.S.free, 1)
            for i in range(len(units)):
                bank = b.A.read(a, ("h", i))
                if i >= 3:
                    b.D.done(a, ("h", i - 3))
                a.activation(sg[:, i % 3, :], bank, ACT.Silu).then_inc(b.A.free, 1)

        @b.block.gpsimd
        def _(g):
            norm.gpsimd(g)

        @b.block.vector
        def _(v):
            ch = Chain(v, b.sem("chain"))
            norm.vector_stats(v, ch)
            norm.vector_apply(v)
            turn.vector(v)
            b.S.done(v, "logits")
            gate.largest(v, ch, score)
            ch.link(v.tensor_reduce(total[:, :], gate.mx[:, :, 0:4], AX, ALU.add))
            ch.link(v.tensor_scalar(total[:, :], total[:, :], 1e-20, None, ALU.add))
            ch.link(v.reciprocal(total[:, :], total[:, :]))
            ch.link(gate.one_hot(v, comb[:, :, :], 0))
            for k in range(1, 4):
                ch.link(gate.one_hot(v, hot[:, :, :], k))
                ch.link(v.tensor_tensor(comb[:, :, :], comb[:, :, :], hot[:, :, :], ALU.add))
            ch.link(v.tensor_tensor(comb[:, :, :], comb[:, :, :], score[:, :, :], ALU.mult))
            ch.link(v.tensor_tensor(comb[:, :, :], comb[:, :, :], total[:, :].unsqueeze(2).to_broadcast([P, n, E1]), ALU.mult))
            for k in range(3):
                ins = v.tensor_copy(c3[:, :, k, :], comb[:, :, :])
                if k < 2:
                    ch.link(ins)
                    ch.link(v.tensor_tensor(comb[:, :, :], comb[:, :, :], c3[:, :, k, :], ALU.subtract))
            ins.then_inc(s_comb, 1)
            for u in range(PAIR):
                bank = b.S.read(v, ("ct", u)).bitcast(BF16)
                v.tensor_copy(ct[:, u, :], bank[0:3 * E1, 0:T]).then_inc(b.S.free, 1)

            def add(u):
                bank = b.O.read(v, ("y", u))
                x = core.toks(core.x, u).rearrange("p t d -> p (t d)")
                v.scalar_tensor_tensor(x, bank, core.tg[:, 5:6], x, ALU.mult, ALU.add).then_inc(b.O.free, 1)

            for i, (u, j) in enumerate(units):
                bank = b.D.read(v, ("h", i))
                b.A.done(v, ("h", i))
                if i >= 3:
                    wait_y(v, i - 3)
                out = up if j < TILES else h
                v.tensor_tensor(out[:, i % 3, :], bank, sg[:, i % 3, :], ALU.mult).then_inc(b.D.free, 1)
                if j < TILES:
                    b.D.done(v, ("h", i))
                    bank = b.S.read(v, ("c", i))
                    v.tensor_tensor(h[:, i % 3, :], bank, up[:, i % 3, :], ALU.mult).then_inc(b.S.free, 1)
                if j == 2 and u:
                    add(0)
            add(1)

        @b.block.sync
        def _(sp):
            sp.dma_start(down[:, :, :], core.io["down"]).then_inc(s_ld, 16)


def block_single(core):
    with ExitStack() as mem, Block(core, "L2x") as b:
        sb = core.sb(mem, "L2x_")
        qh = sb("q_hi", [P, PAIR, T], F32R)
        ql = sb("q_lo", [P, PAIR, T], F32R)
        kh = sb("k_hi", [P, PAIR, NKE], F32R)
        kl = sb("k_lo", [P, PAIR, NKE], F32R)
        vv = sb("v", [NK, PAIR, D])
        mx = sb("score_max", [P, PAIR, NT])
        nm = sb("neg_max", [P, PAIR, NT, 2], BF16)
        nmt = sb("neg_max_turned", [2, PAIR, T], BF16)
        p = sb("weights", [NK, PAIR, T])
        rs = sb("inv_sums", [P, PAIR, NT])
        norm = Norm(b, "norm", core.x, core.n)
        turn = Turn(b, "turn", norm)
        s_hi = b.sem("hi")
        s_nm = b.sem("nm")
        s_sum = b.sem("sum")

        @b.block.tensor
        def _(pe):
            for u in range(PAIR):
                bank = b.S.fill(pe, ("k", u))
                pe.matmul(bank[:, 0:NKE], core.X("L2k"), core.ctxp[:, u, :], start=True, stop=True).then_inc(b.S.full, 1)
            for u in range(PAIR):
                bank = b.S.fill(pe, ("v", u))
                pe.matmul(bank[0:NK, 0:D], core.ctxp[:, u, 0:NK], core.X("L2v"), start=True, stop=True)\
                    .then_inc(b.S.full, 1)
            turn.tensor(pe)
            for u in range(PAIR):
                turn.ready(pe, u)
                bank = b.D.fill(pe, ("q", u))
                product(pe, core, bank, "L2q", u).then_inc(b.D.full, 1)
            for u in range(PAIR):
                b.D.done(pe, ("q", u))
                b.S.done(pe, ("k", u))
                bank = b.D.fill(pe, ("s", u))
                for t in range(NT):
                    tok = slice(t * P, t * P + P)
                    out = bank[:, t * KSLOT:t * KSLOT + NKE]
                    pe.matmul(out, qh[:, u, tok], kh[:, u, :], start=True, stop=False)
                    pe.matmul(out, qh[:, u, tok], kl[:, u, :], start=False, stop=False)
                    mm = pe.matmul(out, ql[:, u, tok], kh[:, u, :], start=False, stop=True)
                mm.then_inc(b.D.full, 1)
            for u in range(PAIR):
                pe.wait_ge(s_nm, u + 1)
                bank = b.S.fill(pe, ("nm", u)).bitcast(BF16)
                for t in range(NT):
                    mm = pe.transpose(bank[0:2, t * P:t * P + P], nm[:, u, t, :], core.identb[:, :])
                mm.then_inc(b.S.full, 1)
            for u in range(PAIR):
                bank = b.A.fill(pe, ("st", u))
                out = bank[0:NK, :]
                pe.matmul(out, kh[:, u, 0:NK], qh[:, u, :], start=True, stop=False)
                pe.matmul(out, kh[:, u, 0:NK], ql[:, u, :], start=False, stop=False)
                pe.matmul(out, kl[:, u, 0:NK], qh[:, u, :], start=False, stop=False)
                b.S.done(pe, ("nm", u))
                pe.matmul(out, core.ones2[:, 0:NK], nmt[:, u, :], start=False, stop=True).then_inc(b.A.full, 1)
            for u in range(PAIR):
                b.A.done(pe, ("st", u))
                b.S.done(pe, ("v", u))
                bank = b.O.fill(pe, ("y", u))
                sums = b.S.fill(pe, ("sum", u))
                for t in range(NT):
                    tok = slice(t * P, t * P + P)
                    pe.matmul(sums[:, 2 * t:2 * t + 2], p[:, u, tok], core.K("ones", 0, 2, NK), start=True, stop=True)
                    mm = pe.matmul(bank[:, tok], p[:, u, tok], vv[:, u, :], start=True, stop=True)
                mm.then_inc(b.O.full, 1)

        @b.block.scalar
        def _(a):
            for u in range(PAIR):
                bank = b.S.read(a, ("k", u))
                a.activation(kh[:, u, :], bank[:, 0:NKE], ACT.Identity, bias=core.Cc("L2bk")).then_inc(s_hi, 1)
            turn.scalar(a)
            for u in range(PAIR):
                bank = b.D.read(a, ("q", u))
                a.activation(qh[:, u, :], bank, ACT.Identity, bias=core.Cc("L2bq")).then_inc(s_hi, 1)
            for u in range(PAIR):
                bank = b.A.read(a, ("st", u))
                a.activation(p[:, u, :], bank[0:NK, :], ACT.Exp).then_inc(b.A.free, 1)

        @b.block.gpsimd
        def _(g):
            norm.gpsimd(g)

        @b.block.vector
        def _(v):
            ch = Chain(v, b.sem("chain"))
            for u in range(PAIR):
                bank = b.S.read(v, ("k", u))
                v.wait_ge(s_hi, u + 1)
                v.scalar_tensor_tensor(kl[:, u, :], bank[:, 0:NKE], core.Cc("L2bk"), f32(kh[:, u, :]), ALU.add,
                                       ALU.subtract).then_inc(b.S.free, 1)
            for u in range(PAIR):
                bank = b.S.read(v, ("v", u))
                v.tensor_tensor(vv[:, u, :], bank[0:NK, 0:D], core.R("L2bv")[0:NK], ALU.add).then_inc(b.S.free, 1)
            norm.vector_stats(v, ch)
            norm.vector_apply(v)
            turn.vector(v)
            for u in range(PAIR):
                bank = b.D.read(v, ("q", u))
                v.wait_ge(s_hi, PAIR + u + 1)
                v.scalar_tensor_tensor(ql[:, u, :], bank, core.Cc("L2bq"), f32(qh[:, u, :]), ALU.add, ALU.subtract)\
                    .then_inc(b.D.free, 1)
            for u in range(PAIR):
                bank = b.D.read(v, ("s", u))
                v.tensor_reduce(mx[:, u, :], bank[:, 0:NT * KSLOT].rearrange("p (t k) -> p t k", t=NT)[:, :, 0:NK], AX,
                                ALU.max).then_inc(b.D.free, 1)
                b.D.done(v, ("s", u))
                hi, lo = nm[:, u, :, 0], nm[:, u, :, 1]
                ch.link(v.tensor_scalar(hi, mx[:, u, :], -1.0, None, ALU.mult))
                v.scalar_tensor_tensor(lo, mx[:, u, :], -1.0, hi, ALU.mult, ALU.subtract).then_inc(s_nm, 1)
            for u in range(PAIR):
                bank = b.S.read(v, ("nm", u)).bitcast(BF16)
                v.tensor_copy(nmt[:, u, :], bank[0:2, 0:T]).then_inc(b.S.free, 1)
            for u in range(PAIR):
                bank = b.O.read(v, ("y", u))
                sums = b.S.banks[b.S.number[("sum", u)] % 2]
                ins = v.reciprocal(rs[:, u, :], sums[:, 0:2 * NT].rearrange("p (t e) -> p t e", e=2)[:, :, 0])
                ins.then_inc(b.S.free, 1)
                b.S.done(v, ("sum", u))
                ch.link(v.tensor_scalar(rs[:, u, :], rs[:, u, :], core.tg[:, 2:3], None, ALU.mult))
                for t in range(NT):
                    x = core.x[:, NT * u + t, :]
                    ins = v.scalar_tensor_tensor(x, bank[:, t * P:t * P + P], rs[:, u, t:t + 1], x, ALU.mult, ALU.add)
                ins.then_inc(b.O.free, 1)


def block_signs(core):
    with ExitStack() as mem, Block(core, "sg") as b:
        sb = core.sb(mem, "sg_")
        words = [sb("k0", [P, 2, T // 4], U32), sb("k1", [P, T], U32), sb("k2", [P, D], U32)]
        k0, k1, k2 = words[0][:, :, :].bitcast(U8), words[1][:, :].bitcast(U8), words[2][:, :].bitcast(U8)
        half = sb("w0_half", [P, 2, T])
        w0 = sb("w0", [P, T], F32R)
        w1 = sb("w1", [P, 4 * T], F32R)
        w2 = sb("w2", [P, 4 * D], F32R)
        s2x = sb("scales", [P, 3])
        r = sb("relu", [P, 3, T])
        hh = sb("h_hi", [P, PAIR, 2, 4, T], F32R)
        hl = sb("h_lo", [P, PAIR, 4, T], F32R)
        norm = Norm(b, "norm", core.x, core.n)
        turn = Turn(b, "turn", norm)
        s_ld = b.sem("load")
        s_w = b.sem("w")
        s_s = b.sem("scale")
        s_r = b.sem("r")
        s_hi = b.sem("hi")
        s_lo = b.sem("lo")
        units = [(layer, u, m) for layer in range(2) for u in range(PAIR) for m in range(4)]

        @b.block.tensor
        def _(pe):
            turn.tensor(pe)
            for i, (layer, u, m) in enumerate(units):
                if m == 0:
                    if layer == 0:
                        turn.ready(pe, u)
                    if u == 0:
                        pe.wait_ge(s_w, 1 + layer)
                    if layer == 1:
                        pe.wait_ge(s_lo, 4 * u + 4)
                bank = b.A.fill(pe, i)
                cols = slice(m * P, m * P + P)
                if layer == 0:
                    pe.matmul(bank, w0[:, cols], core.nh[:, u, :], start=True, stop=False)
                    mm = pe.matmul(bank, w0[:, cols], core.nl[:, u, :], start=False, stop=True)
                else:
                    for k in range(4):
                        w = w1[:, k * T + m * P:k * T + m * P + P]
                        pe.matmul(bank, w, hh[:, u, 0, k, :], start=k == 0, stop=False)
                        mm = pe.matmul(bank, w, hl[:, u, k, :], start=False, stop=k == 3)
                mm.then_inc(b.A.full, 1)
            pe.wait_ge(s_w, 3)
            for u in range(PAIR):
                pe.wait_ge(s_lo, 8 + 4 * u + 4)
                bank = b.D.fill(pe, ("y", u))
                for t in range(NT):
                    tok = slice(t * P, t * P + P)
                    for k in range(4):
                        w = w2[:, k * D:k * D + D]
                        pe.matmul(bank[:, tok], hh[:, u, 1, k, tok], w, start=k == 0, stop=False)
                        mm = pe.matmul(bank[:, tok], hl[:, u, k, tok], w, start=False, stop=k == 3)
                mm.then_inc(b.D.full, 1)

        @b.block.scalar
        def _(a):
            turn.scalar(a)
            a.wait_ge(s_s, 1)
            for i, (layer, u, m) in enumerate(units):
                bank = b.A.read(a, i)
                if i >= 3:
                    a.wait_ge(s_lo, i - 2)
                a.activation(r[:, i % 3, :], bank, ACT.Relu, scale=s2x[:, layer:layer + 1]).then_inc(b.A.free, 1)
                b.A.done(a, i)
                a.activation(hh[:, u, layer, m, :], r[:, i % 3, :], ACT.Copy).then_inc(s_hi, 1)

        @b.block.gpsimd
        def _(g):
            norm.gpsimd(g)
            g.wait_ge(s_ld, 48)
            s = b.sem("half")
            g.tensor_scalar(half[:, 0, :], k0[:, 0, :], 2.0, None, ALU.mult)
            g.tensor_scalar(half[:, 1, :], k0[:, 1, :], 2.0, None, ALU.mult).then_inc(s, 1)
            g.wait_ge(s, 1)
            g.tensor_tensor(w0[:, :], half[:, 0, :], half[:, 1, :], ALU.subtract).then_inc(s_w, 1)
            g.tensor_scalar(w1[:, :], k1[:, :], 2.0, 1.0, ALU.mult, ALU.subtract).then_inc(s_w, 1)
            g.tensor_scalar(w2[:, :], k2[:, :], 2.0, 1.0, ALU.mult, ALU.subtract).then_inc(s_w, 1)

        @b.block.vector
        def _(v):
            ch = Chain(v, b.sem("chain"))
            s, _ = COL["s"]
            v.tensor_scalar(s2x[:, 0:2], core.col[:, s:s + 2], 2.0, None, ALU.mult)
            v.tensor_tensor(s2x[:, 2:3], core.col[:, s + 2:s + 3], core.tg[:, 6:7], ALU.mult).then_inc(s_s, 1)
            norm.vector_stats(v, ch)
            norm.vector_apply(v)
            turn.vector(v)
            for i, (layer, u, m) in enumerate(units):
                v.wait_ge(s_hi, i + 1)
                if layer == 1 and m == 0:
                    b.A.read(v, 8 + 4 * u + 3)
                v.tensor_tensor(hl[:, u, m, :], r[:, i % 3, :], f32(hh[:, u, layer, m, :]), ALU.subtract)\
                    .then_inc(s_lo, 1)
            for u in range(PAIR):
                bank = b.D.read(v, ("y", u))
                x = core.toks(core.x, u).rearrange("p t d -> p (t d)")
                v.scalar_tensor_tensor(x, bank, s2x[:, 2:3], x, ALU.mult, ALU.add).then_inc(b.D.free, 1)

        @b.block.sync
        def _(sp):
            sp.dma_start(words[0][:, :, :], core.io["k0"].rearrange("h p n -> p h n")).then_inc(s_ld, 16)
            sp.dma_start(words[1][:, :], core.io["k1"]).then_inc(s_ld, 16)
            sp.dma_start(words[2][:, :], core.io["k2"]).then_inc(s_ld, 16)


def block_setup(core):
    nc, io = core.nc, core.io
    with ExitStack() as mem, Block(core, "setup") as b:
        sb = core.sb(mem, b.name + "_")
        raw = sb("raw", [P, N_STAGED])
        cst = sb("cst_all", [P, N_CST])
        sel = sb("sel_raw", [3 * E1, E1 // 2 * P])
        freq = sb("freq", [P, 2, D])
        at = sb("at", [P, 2, D])
        rep = sb("rep", [P, P])
        rep64 = sb("rep64", [NC, P])
        s_ld = b.sem("load")
        s_ones = b.sem("rep")
        s_pe = b.sem("pe")
        s_at = b.sem("at")
        s_th = b.sem("tanh")
        loads = 10
        R = lambda name: raw[:, SPLIT[name][0]:SPLIT[name][0] + SPLIT[name][1]]
        columns = [("a1q", "a1bx"), ("a1k", "a1by"), ("a1li2", "a1b3"), ("a2q", "a2bx"), ("a2li2", "a2b3")]
        bank = lambda i: core.psum[:, i, :]
        C = lambda name: cst[:, CST[name][0]:CST[name][0] + P]

        @b.block.sync
        def _(sp):
            for dst, name in ((raw, "wsplit"), (core.wf, "wf"), (core.w64, "w64"), (core.row, "row"), (core.col, "col"),
                              (cst, "cst"), (sel, "sel48")):
                sp.dma_start(dst[:, :], io[name]).then_inc(s_ld, 16)
            sp.dma_start(core.cst[:, :], io["cst"][:, 0:N_CST_KEPT]).then_inc(s_ld, 16)
            sp.dma_start(freq[:, 0, :], io["freq_re"]).then_inc(s_ld, 16)
            sp.dma_start(freq[:, 1, :], io["freq_im"]).then_inc(s_ld, 16)

        @b.block.gpsimd
        def _(g):
            g.memset(f32(core.qs[:, :, :, :]), 0.0)

        @b.block.tensor
        def _(pe):
            pe.wait_ge(s_ld, 16 * loads)
            k = 0
            for w, shift in columns:
                for m in range(4):
                    pe.matmul(bank(0)[:, k:k + 1], R(w)[:, m * P:m * P + P], core.Cc(shift), start=True, stop=True)
                    k += 1
            for m in range(4):
                mm = pe.matmul(bank(0)[:, k:k + 1], core.X("a2k", m * P, m * P + P), core.Cc("a2by", 0, NC),
                               start=True, stop=True)
                k += 1
            mm.then_inc(s_pe, 1)
            re, im = freq[:, 0, :], freq[:, 1, :]
            pe.matmul(bank(3)[:, 0:D], re, C("C"), start=True, stop=False)
            pe.matmul(bank(3)[:, 0:D], im, C("S"), start=False, stop=True)
            pe.matmul(bank(4)[:, 0:D], im, C("C"), start=True, stop=False)
            pe.matmul(bank(4)[:, 0:D], re, C("nS"), start=False, stop=True).then_inc(s_pe, 1)
            pe.wait_ge(s_ones, 1)
            pe.matmul(bank(1), rep[:, :], R("a1v"), start=True, stop=True)
            pe.matmul(bank(2)[:, :], rep64[:, :], core.X("a2v"), start=True, stop=True).then_inc(s_pe, 1)
            pe.wait_ge(s_at, 1)
            pe.matmul(bank(5)[:, 0:D], at[:, 0, :], C("Cn"), start=True, stop=False)
            pe.matmul(bank(5)[:, 0:D], at[:, 1, :], C("nSn"), start=False, stop=True).then_inc(s_pe, 1)

        @b.block.scalar
        def _(a):
            a.wait_ge(s_ld, 16 * loads)
            s, _ = COL["gx"]
            a.activation(core.tg[:, :], core.col[:, s:s + 8], ACT.Tanh).then_inc(s_th, 1)

        @b.block.vector
        def _(v):
            ch = Chain(v, b.sem("chain"))
            v.memset(core.ones2[:, :], 1.0)
            v.wait_ge(s_ld, 16 * loads)
            v.tensor_copy(core.identb[:, :], core.K("ident"))
            v.tensor_copy(core.sel48[:, :], sel[:, :])
            v.tensor_scalar(rep[:, :], C("ones"), core.Cc("a1by"), None, ALU.mult)
            v.tensor_scalar(rep64[:, :], cst[0:NC, CST["ones"][0]:CST["ones"][0] + P], core.Cc("a2by", 0, NC), None,
                            ALU.mult).then_inc(s_ones, 1)
            v.wait_ge(s_pe, 2)
            v.tensor_copy(at[:, 0, :], bank(3)[:, 0:D])
            v.tensor_copy(at[:, 1, :], bank(4)[:, 0:D]).then_inc(s_at, 1)
            ch.link(v.tensor_copy(core.bias[:, :], bank(0)[:, 0:24]))
            for k, name in ((8, "a1li2b"), (16, "a2li2b")):
                s, w = COL[name]
                v.tensor_tensor(core.bias[:, k:k + 4], core.bias[:, k:k + 4], core.col[:, s:s + w], ALU.add)
            v.wait_ge(s_pe, 3)
            v.tensor_copy(core.vb1[:, :], bank(1))
            v.tensor_copy(core.vb2[:, :], bank(2))
            for w, gain in (("a1q", "a1gx"), ("a1k", "a1gy"), ("a1v", "a1gy"), ("a1li2", "a1g3"), ("a2q", "a2gx"),
                            ("a2li2", "a2g3")):
                last = v.tensor_scalar(R(w), R(w), core.Cc(gain), None, ALU.mult)
            s, _ = W64["a2k"]
            both = core.w64[:, s:s + 1024]
            last = v.tensor_scalar(both, both, core.Cc("a2gy", 0, NC), None, ALU.mult)
            ch.link(last)
            ch.link(v.tensor_copy(core.wh[:, 0:N_STAGED], raw[:, :]))
            v.tensor_tensor(core.wl[:, 0:N_STAGED], raw[:, :], f32(core.wh[:, 0:N_STAGED]), ALU.subtract)
            v.wait_ge(s_pe, 4)
            ch.link(v.tensor_copy(core.W("M", 1), bank(5)[:, 0:D]))
            v.tensor_tensor(core.W("M", 0), bank(5)[:, 0:D], f32(core.W("M", 1)), ALU.subtract)
            v.wait_ge(s_th, 1)
            for name, k in (("L0bo", 0), ("L3bo", 3), ("L3fb", 7)):
                v.tensor_scalar(core.R(name), core.R(name), core.tg[:, k:k + 1], None, ALU.mult)


def block_last(core, pair):
    with ExitStack() as mem, Block(core, "last") as b:
        norm = Norm(b, "norm", core.x, core.n)
        turn = Turn(b, "turn", norm)
        s_xb = b.sem("xb")
        s_out = b.sem("out")

        @b.block.tensor
        def _(pe):
            turn.tensor(pe)
            for u in range(PAIR):
                turn.ready(pe, u)
                bank = b.D.fill(pe, ("y", u))
                for i in range(NT):
                    mm = product_rows(pe, core, bank[:, i * P:i * P + P], "M", u, i)
                mm.then_inc(b.D.full, 1)

        @b.block.vector
        def _(v):
            ch = Chain(v, b.sem("chain"))
            norm.vector_stats(v, ch)
            norm.vector_apply(v)
            turn.vector(v)
            v.wait_ge(s_xb, 1)
            for u in range(PAIR):
                x = core.toks(core.x, u).rearrange("p t d -> p (t d)")
                bank = b.D.read(v, ("y", u))
                v.scalar_tensor_tensor(x, bank, core.tg[:, 7:8], x, ALU.mult, ALU.add).then_inc(b.D.free, 1)

        @b.block.scalar
        def _(a):
            turn.scalar(a)

        @b.block.gpsimd
        def _(g):
            norm.gpsimd(g)
            g.wait_ge(norm.s_n, PAIR)
            g.tensor_tensor(core.x[:, :, :], core.x[:, :, :], core.rows("L3fb", PAIR * NT), ALU.add).then_inc(s_xb, 1)

        @b.block.sync
        def _(sp):
            for u in range(PAIR):
                b.D.done(sp, ("y", u))
                sp.dma_start(core.io["out"][bass.ds(pair * PAIR + u, 1)].rearrange("b (t p) d -> p (b t) d", p=P),
                             core.toks(core.x, u)).then_inc(s_out, 16)
            sp.wait_ge(s_out, 16 * PAIR)


IN = ["x", "ctxT", "ctx", "wsplit", "wf", "w64", "row", "col", "cst", "sel48", "freq_re", "freq_im",
      "w1", "w2", "b2", "down", "k0", "k1", "k2"]


def build(nc, io):
    with ExitStack() as ctx:
        core = Core(nc, io, ctx)
        block_setup(core)
        with nc.Fori(0, B // PAIR) as pair:
            block_narrow(core, 0, pair, True)
            block_experts0(core)
            block_self(core)
            block_wide(core)
            block_experts1(core)
            block_single(core)
            block_signs(core)
            block_narrow(core, 3, pair, False)
            block_last(core, pair)


def packed(layout, width, parts, given):
    out = np.zeros((parts, width), np.float32)
    for name, (at, w) in layout.items():
        if name in given:
            a = given[name]
            out[:a.shape[0], at:at + w] = a
    return out


def constants():
    i = np.arange(P)
    turn = 2 * np.pi * ((i[:, None] * i[None, :]) % D) / D
    c, s = np.cos(turn), np.sin(turn)
    onesm = np.zeros((P, 4, 40))
    onesm[:, :, 0:8] = 1
    ksel = np.zeros((P, 4))
    for q in range(4):
        ksel[STK + 2 * q:STK + 2 * q + 2, q] = 1
    given = {"ident": np.eye(P), "mask": i[:, None] > i[None, :], "ones": np.ones((P, P)), "onesm": onesm.reshape(P, 160),
             "ksel": ksel, "iota": np.tile(np.arange(16), (P, 1)), "half": np.full((P, 8), -0.5),
             "C": c, "S": s, "nS": -s, "Cn": c / D, "nSn": -s / D}
    sel = np.zeros((3, E1, E1 // 2, 2, F1), np.float32)
    for e in range(E1):
        sel[:, e, e // 2, e % 2] = 1
    return packed(CST, N_CST, P, given), sel.reshape(3 * E1, E1 // 2 * P)


def arrays(i):
    tile = lambda a, n: a.reshape(n, P, -1).transpose(1, 0, 2).reshape(P, -1)
    heads = lambda a: a.transpose(1, 0, 2).reshape(a.shape[1], -1)
    cols = lambda a: a.reshape(-1, P).T
    words = lambda a: np.ascontiguousarray(a).view(np.uint32)
    a1, a2 = "L1_xattn_a1_", "L1_xattn_a2_"
    split = {"L0q": i["L0_xattn_Wq"], "L3q": i["L3_xattn_Wq"], "L2q": i["L2_xattn_Wq"], "g0": i["L0_ffn_gate_w"],
             "g1": i["L1_ffn_gate_w"].T, "a1q": heads(i[a1 + "wq"]), "a1k": heads(i[a1 + "wk"]),
             "a1v": heads(i[a1 + "wv"]), "a1li2": i[a1 + "li2_w"], "a2q": heads(i[a2 + "wq"]), "a2li2": i[a2 + "li2_w"],
             "eg": heads(i["L1_ffn_expert_gate"]), "sg": i["L1_ffn_shared_gate"],
             "eu": heads(i["L1_ffn_expert_up"]), "su": i["L1_ffn_shared_up"]}
    wf = {"L0o": i["L0_xattn_Wo"], "L3o": i["L3_xattn_Wo"], "a1li1": tile(i[a1 + "li1_w"], 4),
          "a1li3": tile(i[a1 + "li3_w"], 4), "a2li1": tile(i[a2 + "li1_w"], 4), "a2li3": tile(i[a2 + "li3_w"], 4)}
    w64 = {f"L{n}{k}": i[f"L{n}_xattn_W{k}"] for n in (0, 2, 3) for k in "kv"}
    w64 |= {"a2k": heads(i[a2 + "wk"]), "a2v": heads(i[a2 + "wv"])}
    rows = {"L0bv": "L0_xattn_bv", "L2bv": "L2_xattn_bv", "L3bv": "L3_xattn_bv", "L0bo": "L0_xattn_bo",
            "L3bo": "L3_xattn_bo", "L3fb": "L3_ffn_bias", "a1li1b": a1 + "li1_b", "a1li3b": a1 + "li3_b",
            "a2li1b": a2 + "li1_b", "a2li3b": a2 + "li3_b", "ln1g": "L1_xattn_ln1_g", "ln1b": "L1_xattn_ln1_b",
            "ln2g": "L1_xattn_ln2_g", "ln2b": "L1_xattn_ln2_b"}
    row = {k: np.broadcast_to(i[v], (P, D)) for k, v in rows.items()}
    col = {f"L{n}b{k}": cols(i[f"L{n}_xattn_b{k}"]) for n in (0, 2, 3) for k in "qk"}
    for a, full in (("a1", a1), ("a2", a2)):
        for short, long in (("gx", "lnx_g"), ("bx", "lnx_b"), ("gy", "lny_g"), ("by", "lny_b"), ("g3", "ln3_g"),
                            ("b3", "ln3_b")):
            col[a + short] = i[full + long].reshape(-1, 1)
        col[a + "li2b"] = cols(i[full + "li2_b"])
    col["b1"] = cols(i["L0_ffn_dense_1_b"].reshape(E0, F0, 2).transpose(0, 2, 1).reshape(-1))
    col["gx"] = np.broadcast_to(i["g_xattn"], (P, 4))
    col["gf"] = np.broadcast_to(i["g_ffn"], (P, 4))
    col["s"] = np.broadcast_to(np.stack([i["L2_ffn_s0"], i["L2_ffn_s1"], i["L2_ffn_s2"]]), (P, 3))
    ctxT = np.zeros((NC, B, NKE), np.float32)
    ctxT[:, :, :NK] = i["ctx_512"].transpose(2, 0, 1)
    cst, sel = constants()
    return {
        "x": i["x"], "ctxT": ctxT, "ctx": i["ctx_512"],
        "wsplit": packed(SPLIT, N_STAGED, P, split), "wf": packed(WF, N_WF, P, wf), "w64": packed(W64, N_W64, NC, w64),
        "row": packed(ROW, N_ROW, P, row), "col": packed(COL, N_COL, P, col), "cst": cst, "sel48": sel,
        "freq_re": i["L3_ffn_w_freq_real"], "freq_im": i["L3_ffn_w_freq_imag"],
        "w1": i["L0_ffn_dense_1_w"].reshape(E0, F0, 2, D).transpose(3, 0, 2, 1).reshape(D, -1),
        "w2": i["L0_ffn_dense_2_w"].transpose(0, 2, 1).reshape(E0 * F0 // P, P, D).transpose(1, 0, 2),
        "b2": i["L0_ffn_dense_2_b"],
        "down": np.concatenate([i["L1_ffn_expert_down"].reshape(E1 * F1, D), i["L1_ffn_shared_down"]])
        .reshape(-1, P, D).transpose(1, 0, 2),
        "k0": words(i["L2_ffn_k0"].reshape(2, P, 512)), "k1": words(tile(i["L2_ffn_k1"], 4)),
        "k2": words(tile(i["L2_ffn_k2"], 4)),
    }


def kernel(**inputs):
    from concourse import bacc
    from concourse.bass_utils import run_bass_kernel_spmd

    given = arrays({k: np.asarray(v) for k, v in inputs.items()})
    nc = bacc.Bacc("TRN2", target_bir_lowering=False, num_devices=1)
    feed, io = {}, {}
    for name in IN:
        a = np.ascontiguousarray(given[name])
        feed["in_" + name] = a
        io[name] = nc.dram_tensor("in_" + name, a.shape, mybir.dt.from_np(a.dtype), kind="ExternalInput").ap()
    io["out"] = nc.dram_tensor("out_x", (B, T, D), F32, kind="ExternalOutput").ap()
    build(nc, io)
    r = run_bass_kernel_spmd(nc, [feed], core_ids=[0])
    return r.results[0]["out_x"]
```

```python
from contextlib import ExitStack

import numpy as np

import concourse.bass as bass
from concourse import mybir

F32 = mybir.dt.float32
F32R = mybir.dt.float32r
BF16 = mybir.dt.bfloat16
U32 = mybir.dt.uint32
U8 = mybir.dt.uint8
ALU = mybir.AluOpType
ACT = mybir.ActivationFunctionType
AX = mybir.AxisListType.X

P = 128
B, T, D = 4, 512, 128
NT = T // P
PAIR = 2
NK, NKE = 77, 78
NC = 64
H = 16
DH = 32
KSLOT = 80
STK = 96
STKM = STK + 8
E0, F0 = 8, 256
E1, F1 = 16, 64
EPS = 1e-5



def _layout(items):
    out, at = {}, 0
    for name, width in items:
        out[name] = (at, width)
        at += width
    return out, at


SPLIT, N_SPLIT = _layout([
    ("L0q", 128), ("L3q", 128), ("L2q", 128), ("g0", E0), ("g1", E1),
    ("a1q", 512), ("a1k", 512), ("a1v", 512), ("a1li2", 512), ("a2q", 512), ("a2li2", 512),
    ("eg", 1024), ("sg", 128), ("eu", 1024), ("su", 128), ("M", 128)])
N_STAGED = SPLIT["M"][0]
WF, N_WF = _layout([("L0o", 128), ("L3o", 128), ("a1li1", 512), ("a1li3", 512), ("a2li1", 512), ("a2li3", 512)])
W64, N_W64 = _layout([("L0k", 128), ("L0v", 128), ("L2k", 128), ("L2v", 128), ("L3k", 128), ("L3v", 128),
                      ("a2k", 512), ("a2v", 512)])
ROW, N_ROW = _layout([(n, 128) for n in (
    "L0bv", "L2bv", "L3bv", "L0bo", "L3bo", "L3fb", "a1li1b", "a1li3b", "a2li1b", "a2li3b",
    "ln1g", "ln1b", "ln2g", "ln2b")])
COL, N_COL = _layout([
    ("L0bq", 1), ("L0bk", 1), ("L2bq", 1), ("L2bk", 1), ("L3bq", 1), ("L3bk", 1),
    ("a1gx", 1), ("a1bx", 1), ("a1gy", 1), ("a1by", 1), ("a1g3", 1), ("a1b3", 1), ("a1li2b", 4),
    ("a2gx", 1), ("a2bx", 1), ("a2gy", 1), ("a2by", 1), ("a2g3", 1), ("a2b3", 1), ("a2li2b", 4),
    ("b1", 4 * E0), ("gx", 4), ("gf", 4), ("s", 3)])
CST, N_CST = _layout([
    ("ident", 128), ("mask", 128), ("ones", 32), ("onesm", 160), ("ksel", 4), ("iota", 16), ("half", 8),
    ("C", 128), ("ones128", 128), ("S", 128), ("nS", 128), ("Cn", 128), ("nSn", 128)])
N_CST_KEPT = CST["C"][0]


class Ring:

    def __init__(self, banks, full, free):
        self.banks, self.full, self.free = banks, full, free
        self.n, self.number = 0, {}

    def fill(self, pe, name):
        n = self.number[name] = self.n
        self.n += 1
        if n >= len(self.banks):
            pe.wait_ge(self.free, n - len(self.banks) + 1)
        return self.banks[n % len(self.banks)]

    def read(self, eng, name):
        n = self.number[name]
        eng.wait_ge(self.full, n + 1)
        return self.banks[n % len(self.banks)]

    def done(self, eng, name):
        eng.wait_ge(self.free, self.number[name] + 1)


class Chain:

    def __init__(self, eng, sem):
        self.eng, self.sem, self.n = eng, sem, 0

    def link(self, ins):
        ins.then_inc(self.sem, 1)
        self.n += 1
        self.eng.wait_ge(self.sem, self.n)


def f32(ap):
    return ap.bitcast(F32)


class Core:

    def __init__(self, nc, io, ctx):
        self.nc, self.io = nc, io
        self.ctx = ctx
        self.psum = ctx.enter_context(nc.psum_tensor("banks", [P, 8, T], F32))
        sb = self.sb(ctx)
        self.x = sb("x_res", [P, PAIR * NT, D])
        self.n = sb("x_norm", [P, PAIR * NT, D])
        self.nh = sb("normT_hi", [P, PAIR, T], F32R)
        self.nl = sb("normT_lo", [P, PAIR, T], F32R)
        self.wh = sb("w_hi", [P, N_SPLIT], F32R)
        self.wl = sb("w_lo", [P, N_SPLIT], F32R)
        self.wf = sb("w_f32", [P, N_WF])
        self.w64 = sb("w_ctx", [NC, N_W64])
        self.row = sb("rows", [P, N_ROW])
        self.col = sb("cols", [P, N_COL])
        self.cst = sb("consts", [P, N_CST_KEPT])
        self.identb = sb("ident_bf", [P, P], BF16)
        self.ones2 = sb("ones2_bf", [2, NKE], BF16)
        self.sel48 = sb("sel48_bf", [3 * E1, E1 // 2 * P], BF16)
        self.ctxp = sb("ctxT_pair", [NC, PAIR, NKE])
        self.ctxr = sb("ctx_pair", [NK, PAIR, NC])
        self.tg = sb("tanh_g", [P, 8])
        self.bias = sb("proj_bias", [P, 24])
        self.vb1 = sb("a1_vbias", [P, 512])
        self.vb2 = sb("a2_vbias", [P, 512])
        self.qs = sb("q_stack", [P, 3, 4, T], F32R)
        self.x1 = sb("x_inner", [P, PAIR * NT, D])
        self.st = sb("bn_stats", [P, PAIR * NT, 6])
        self.mv = sb("mean_var", [P, PAIR * NT, 2])
        self.ve = sb("var_eps", [P, PAIR * NT])
        self.rstd = sb("rstd", [P, PAIR * NT])
        self.qkd = nc.dram_tensor("qk_scratch", (PAIR, 2, 4, 2, P, T), F32).ap()
        self.kd = nc.dram_tensor("k_scratch", (PAIR, 2, 4, P, NKE), F32).ap()

    def sb(self, ctx, prefix=""):
        nc = self.nc
        return lambda name, shape, dt=F32: ctx.enter_context(nc.sbuf_tensor(prefix + name, shape, dt))

    def W(self, name, hi, a=0, b=None):
        s, w = SPLIT[name]
        return (self.wh if hi else self.wl)[:, s + a:s + (w if b is None else b)]

    def F(self, name, a=0, b=None):
        s, w = WF[name]
        return self.wf[:, s + a:s + (w if b is None else b)]

    def X(self, name, a=0, b=None):
        s, w = W64[name]
        return self.w64[:, s + a:s + (w if b is None else b)]

    def R(self, name):
        s, w = ROW[name]
        return self.row[:, s:s + w]

    def rows(self, name, n):
        s, w = ROW[name]
        return self.row[:, s:s + w].unsqueeze(1).to_broadcast([P, n, w])

    def Cc(self, name, k=0, p=P):
        s, _ = COL[name]
        return self.col[0:p, s + k:s + k + 1]

    def K(self, name, a=0, b=None, p=P):
        s, w = CST[name]
        return self.cst[0:p, s + a:s + (w if b is None else b)]

    def toks(self, t, u):
        return t[:, NT * u:NT * u + NT, :]


class Block:

    def __init__(self, core, name, attention=False):
        self.core, self.name, self.nc, self.attention = core, name, core.nc, attention

    def __enter__(self):
        self.stack = ExitStack()
        self.sems = []
        bk = self.core.psum
        one = lambda i: bk[:, i, :]
        self.A = Ring([one(0), one(1)], self.sem("A_full"), self.sem("A_free"))
        self.D = Ring([one(2), one(3)], self.sem("D_full"), self.sem("D_free"))
        self.O = Ring([one(4), one(6)], self.sem("O_full"), self.sem("O_free"))
        if self.attention:
            self.S = Ring([one(5)], self.sem("S_full"), self.sem("S_free"))
            self.N = Ring([one(7)], self.sem("N_full"), self.sem("N_free"))
        else:
            self.S = Ring([one(5), one(7)], self.sem("S_full"), self.sem("S_free"))
        self.block = self.stack.enter_context(self.nc.Block())
        return self

    def sem(self, name):
        s = self.stack.enter_context(self.nc.semaphore(f"{self.name}_{name}"))
        self.sems.append(s.num)
        return s

    def __exit__(self, *_):
        self.stack.close()
        self.nc.all_engine_barrier(sems_to_clear=range(min(self.sems), max(self.sems) + 1))
        return False


class Norm:

    def __init__(self, b, name, src, dst, width=D, parts=P, tiles=PAIR * NT):
        self.core, self.src, self.dst = b.core, src, dst
        self.tiles, self.parts = tiles, parts
        self.s_var = b.sem(name + "_var")
        self.s_rstd = b.sem(name + "_rstd")
        self.s_n = b.sem(name + "_n")

    def vector_stats(self, v, ch):
        c, p = self.core, self.parts
        for t in range(self.tiles):
            last = v.bn_stats(c.st[0:p, t, :], self.src[:, t, :])
        ch.link(last)
        for t in range(self.tiles):
            last = v.bn_aggr(c.mv[0:p, t, :], c.st[0:p, t, :])
        ch.link(last)
        v.tensor_scalar(c.ve[0:p, 0:self.tiles], c.mv[0:p, 0:self.tiles, 1], EPS, None, ALU.add).then_inc(self.s_var, 1)

    def gpsimd(self, g):
        c, p = self.core, self.parts
        g.wait_ge(self.s_var, 1)
        g.tensor_tensor(c.rstd[0:p, 0:self.tiles], c.ve[0:p, 0:self.tiles], c.K("half", 0, self.tiles, p), ALU.pow)\
            .then_inc(self.s_rstd, 1)

    def vector_apply(self, v):
        c, p = self.core, self.parts
        v.wait_ge(self.s_rstd, 1)
        for t in range(self.tiles):
            ins = v.tensor_scalar(self.dst[:, t, :], self.src[:, t, :], c.mv[0:p, t, 0:1], c.rstd[0:p, t:t + 1],
                                  ALU.subtract, ALU.mult)
            if t % (self.tiles // PAIR) == self.tiles // PAIR - 1:
                ins.then_inc(self.s_n, 1)


class Turn:

    def __init__(self, b, name, norm):
        self.b, self.core, self.name, self.norm = b, b.core, name, norm
        self.s_hi = b.sem(name + "_hi")

    def tensor(self, pe):
        for u in range(PAIR):
            pe.wait_ge(self.norm.s_n, u + 1)
            bank = self.b.D.fill(pe, (self.name, u))
            for t in range(NT):
                mm = pe.transpose(bank[:, t * P:(t + 1) * P], self.core.n[:, NT * u + t, :], self.core.K("ident"))
            mm.then_inc(self.b.D.full, 1)

    def scalar(self, a):
        for u in range(PAIR):
            bank = self.b.D.read(a, (self.name, u))
            a.activation(self.core.nh[:, u, :], bank, ACT.Copy).then_inc(self.s_hi, 1)

    def vector(self, v):
        for u in range(PAIR):
            bank = self.b.D.read(v, (self.name, u))
            v.wait_ge(self.s_hi, u + 1)
            v.tensor_tensor(self.core.nl[:, u, :], bank, f32(self.core.nh[:, u, :]), ALU.subtract)\
                .then_inc(self.b.D.free, 1)

    def ready(self, pe, u):
        self.b.D.done(pe, (self.name, u))


def product(pe, core, out, w, u, a=0, b=None):
    pe.matmul(out, core.W(w, 1, a, b), core.nh[:, u, :], start=True, stop=False)
    pe.matmul(out, core.W(w, 1, a, b), core.nl[:, u, :], start=False, stop=False)
    return pe.matmul(out, core.W(w, 0, a, b), core.nh[:, u, :], start=False, stop=True)


def product_rows(pe, core, out, w, u, t, a=0, b=None):
    tok = slice(t * P, (t + 1) * P)
    pe.matmul(out, core.nh[:, u, tok], core.W(w, 1, a, b), start=True, stop=False)
    pe.matmul(out, core.nl[:, u, tok], core.W(w, 1, a, b), start=False, stop=False)
    return pe.matmul(out, core.nh[:, u, tok], core.W(w, 0, a, b), start=False, stop=True)


class Attention:

    def __init__(self, b, name, kind, t, scale, wq, bq, wk, bk):
        self.b, self.core, self.name, self.kind, self.t, self.scale = b, b.core, name, kind, t, scale
        self.wq, self.bq, self.wk, self.bk = wq, bq, wk, bk
        self.own = kind == "self"
        self.narrow = kind == "narrow"
        self.nkt = NT if self.own else 1
        self.keys = P if self.own else NK
        self.slots = 3 if self.own else 4
        self.steps = [(u, m) for u in range(PAIR) for m in range(4)]
        self.units = len(self.steps) * self.nkt
        self.tiles = 1 if self.narrow else 4
        self.items = []
        for u in range(PAIR):
            for m in range(self.tiles):
                self.items += [(u, 0, m), (u, 1, m)]
        self.s_hi = b.sem("a_hi")
        self.s_lo = b.sem("a_lo")
        self.s_out = [b.sem(f"a_out{i}") for i in range(4)]
        self.s_q = [b.sem(f"a_q{i}") for i in range(self.slots)]
        self.s_k = [b.sem(f"a_k{u}") for u in range(PAIR)]
        self.s_nm = b.sem("a_nm")
        self.s_mr = b.sem("a_mr")
        self.s_pm = b.sem("a_pm")
        self.s_pv = b.sem("a_pv")
        self.s_ln = b.sem("a_ln")
        self.s_rs = b.sem("a_rs")

    def last_of_unit(self, i):
        n, kt = divmod(i, self.nkt)
        return kt == self.nkt - 1 and (not self.narrow or self.steps[n][1] == 3)

    def sums(self, n):
        u, m = self.steps[n]
        return (self.name, "sum", u) if self.narrow else (self.name, "sum", u, m)

    def wait_pv(self, eng, i):
        if self.last_of_unit(i):
            self.b.O.read(eng, self.sums(i // self.nkt))
        else:
            eng.wait_ge(self.s_pv, sum(not self.last_of_unit(j) for j in range(i + 1)))

    def head(self, m, lane):
        return 4 * lane + m if self.narrow else 4 * m + lane

    def n_keys(self, kind):
        return T if (self.own or not kind) else NKE

    def q(self, n):
        slot = n % self.slots
        return self.core.qs[:, slot, :, :] if slot < 3 else self.t.q4[:, :, :]

    def ring(self, j):
        return (self.b.D, self.b.A)[j % 2]

    def staged(self, j, part):
        return self.t.stage[:, part, j % 4, 0:self.n_keys(self.items[j][1])]

    def of(self, u):
        return [(j, item) for j, item in enumerate(self.items) if item[0] == u]

    def staging_done(self, eng, n_items):
        for i in range(4):
            k = len(range(i, n_items, 4))
            if k:
                eng.wait_ge(self.s_out[i], 32 * k)

    def tensor_project(self, pe, turn, u):
        c = self.core
        turn.ready(pe, u)
        for j, (_, kind, m) in self.of(u):
            ring = self.ring(j)
            bank = ring.fill(pe, (self.name, "p", j))
            cols = (m * P, m * P + P)
            if kind == 0 or self.own:
                mm = product(pe, c, bank, self.wk if kind else self.wq, u, *cols)
            else:
                mm = pe.matmul(bank[:, 0:NKE], c.X(self.wk, *cols), self.t.ctx[:, u, :], start=True, stop=True)
            mm.then_inc(ring.full, 1)

    def scalar_project(self, a, u):
        for j, (_, kind, m) in self.of(u):
            bank = self.ring(j).read(a, (self.name, "p", j))
            w = self.n_keys(kind)
            if j >= 4:
                a.wait_ge(self.s_out[j % 4], 32 * (j // 4))
            a.activation(self.staged(j, 0).bitcast(F32R), bank[:, 0:w], ACT.Identity,
                         bias=(self.bk if kind else self.bq)(m)).then_inc(self.s_hi, 1)

    def vector_project(self, v, u):
        for j, (_, kind, m) in self.of(u):
            ring = self.ring(j)
            bank = ring.read(v, (self.name, "p", j))
            w = self.n_keys(kind)
            v.wait_ge(self.s_hi, j + 1)
            if j >= 4:
                v.wait_ge(self.s_out[j % 4], 32 * (j // 4))
            v.scalar_tensor_tensor(self.staged(j, 1).bitcast(F32R), bank[:, 0:w], (self.bk if kind else self.bq)(m),
                                   self.staged(j, 0), ALU.add, ALU.subtract).then_inc(ring.free, 1)

    def sync_project(self, sp, u):
        c = self.core
        for j, (_, kind, m) in self.of(u):
            self.ring(j).done(sp, (self.name, "p", j))
            for part in range(2):
                dst = c.qkd[u, kind, m, part] if (self.own or not kind) else c.kd[u, part, m]
                sp.dma_start(dst, self.staged(j, part)).then_inc(self.s_out[j % 4], 16)
            if u == 0 and kind == 1 and m >= 1:
                self.staging_done(sp, 2 * m)
                self.sync_stacks(sp, [m - 1])
        self.staging_done(sp, j + 1)

    def sync_keys(self, sp, u):
        c = self.core
        for g, part in enumerate((0, 1, 0)):
            if self.narrow:
                dst, src = self.t.ks[32 * g:32 * g + 8, u, :, :], c.kd[u, part, 0].rearrange("(h d) n -> d h n", h=H)
            else:
                dst = self.t.ks[32 * g:32 * g + 32, u, :, :]
                src = c.kd[u, part].rearrange("m (q d) n -> d (m q) n", q=4)
            sp.dma_start(f32(dst), src).then_inc(self.s_k[u], 16)

    def sync_stacks(self, sp, steps):
        c = self.core
        for n in steps:
            u, m = self.steps[n]
            if n >= self.slots:
                self.b.A.read(sp, (self.name, "st", n - self.slots, self.nkt - 1, 3))
            for kind in range(2 if self.own else 1):
                for g, part in enumerate((0, 1, 0) if kind else (0, 0, 1)):
                    if self.narrow:
                        src = c.qkd[u, 0, 0, part].rearrange("(q m d) n -> m d q n", q=4, m=4)[m]
                        dst = self.q(n)[32 * g:32 * g + 8]
                    else:
                        src = c.qkd[u, kind, m, part].rearrange("(q d) n -> d q n", q=4)
                        dst = (self.t.ks[:, n % 3, :, :] if kind else self.q(n))[32 * g:32 * g + 32]
                    sp.dma_start(f32(dst), src).then_inc(self.s_q[n % self.slots], 16)

    def sync(self, sp):
        for u in range(PAIR):
            self.sync_project(sp, u)
            if not self.own:
                self.sync_keys(sp, u)
            if u == 0:
                self.sync_stacks(sp, range(self.tiles - 1, self.slots))
        self.sync_stacks(sp, range(self.slots, len(self.steps)))

    def key_stack(self, n, lane, rows, cols):
        u, m = self.steps[n]
        if self.own:
            return self.t.ks[0:rows, n % 3, lane, cols]
        return self.t.ks[0:rows, u, self.head(m, lane), cols]

    def scores(self, n):
        if n > 7:
            return []
        return [(n, t, lane) for t in range(NT) for lane in (range(4) if self.own else (None,))]

    def tensor_scores(self, pe, piece):
        n, t, lane = piece
        u, m = self.steps[n]
        tok = slice(t * P, (t + 1) * P)
        if t == 0 and not lane:
            pe.wait_ge(self.s_q[n % self.slots], 16 * (6 if self.own else 3) * (n // self.slots + 1))
            if not self.own and m == 0:
                pe.wait_ge(self.s_k[u], 16 * 3)
        bank = self.b.D.fill(pe, (self.name, "s", piece))
        if self.own:
            mm = pe.matmul(bank, self.q(n)[0:STK, lane, tok], self.key_stack(n, lane, STK, slice(0, T)),
                           start=True, stop=True)
        else:
            for q in range(4):
                mm = pe.matmul(bank[:, KSLOT * q:KSLOT * q + NKE], self.q(n)[0:STK, q, tok],
                               self.key_stack(n, q, STK, slice(0, NKE)), start=True, stop=True)
        mm.then_inc(self.b.D.full, 1)

    def vector_max(self, v, piece):
        n, t, lane = piece
        bank = self.b.D.read(v, (self.name, "s", piece))
        if self.own:
            ins = v.tensor_reduce(self.t.mx[:, n % 2, t, lane:lane + 1], bank, AX, ALU.max)
        else:
            ins = v.tensor_reduce(self.t.mx[:, n % 2, t, :], bank[:, 0:4 * KSLOT].rearrange("p (q k) -> p q k", q=4)[:, :, 0:NK],
                                  AX, ALU.max)
        ins.then_inc(self.b.D.free, 1)

    def vector_negate(self, v, ch, n):
        self.b.D.done(v, (self.name, "s", self.scores(n)[-1]))
        hi, lo = self.t.nm[:, :, :, 0], self.t.nm[:, :, :, 1]
        if n >= 1:
            self.b.N.read(v, (self.name, "nm", n - 1))
        ch.link(v.tensor_scalar(hi, self.t.mx[:, n % 2, :, :], -1.0, None, ALU.mult))
        v.scalar_tensor_tensor(lo, self.t.mx[:, n % 2, :, :], -1.0, hi, ALU.mult, ALU.subtract).then_inc(self.s_nm, 1)

    def tensor_turn_max(self, pe, n):
        c = self.core
        if n > 7:
            return
        pe.wait_ge(self.s_nm, n + 1)
        bank = self.b.N.fill(pe, (self.name, "nm", n)).bitcast(BF16)
        for t in range(NT):
            mm = pe.transpose(bank[STK:STKM, t * P:(t + 1) * P], self.t.nm[:, t, :, :].rearrange("p q e -> p (q e)"),
                              c.identb[:, :])
        mm.then_inc(self.b.N.full, 1)

    def scalar_max(self, a, n):
        if n <= 7:
            bank = self.b.N.read(a, (self.name, "nm", n)).bitcast(BF16)
            a.activation(self.q(n)[STK:STKM, 0, :], bank[STK:STKM, 0:T], ACT.Copy).then_inc(self.b.N.free, 1)

    def vector_max_rows(self, v, n):
        if n <= 7:
            self.b.N.done(v, (self.name, "nm", n))
            rows = self.q(n)[STK:STKM]
            v.tensor_copy(rows[:, 1:4, :], f32(rows[:, 0:1, :]).to_broadcast([8, 3, T])).then_inc(self.s_mr, 1)

    def tensor_exps(self, pe, i, lane):
        n, kt = divmod(i, self.nkt)
        if kt == 0 and lane == 0:
            pe.wait_ge(self.s_mr, n + 1)
        bank = self.b.A.fill(pe, (self.name, "st", n, kt, lane))
        cols = slice(kt * P, kt * P + self.keys)
        pe.matmul(bank[0:self.keys, :], self.key_stack(n, lane, STKM, cols), self.q(n)[0:STKM, lane, :],
                  start=True, stop=True).then_inc(self.b.A.full, 1)

    def scalar_exps(self, a, i, lane):
        n, kt = divmod(i, self.nkt)
        if i >= 3 and lane == 0:
            self.wait_pv(a, i - 3)
            if self.own:
                a.wait_ge(self.s_pm, i - 2)
        bank = self.b.A.read(a, (self.name, "st", n, kt, lane))
        a.activation(self.t.p[0:self.keys, i % 3, lane, :], bank[0:self.keys, :], ACT.Exp, scale=self.scale)\
            .then_inc(self.b.A.free, 1)

    def gpsimd_mask(self, g):
        for i in range(self.units):
            n, kt = divmod(i, self.nkt)
            self.b.A.done(g, (self.name, "st", n, kt, 3))
            if i >= 2:
                self.wait_pv(g, i - 2)
            g.tensor_tensor(self.t.pm[:, i % 2, :, :], self.t.p[:, i % 3, :, kt * P:(kt + 1) * P],
                            self.core.K("mask").unsqueeze(1).to_broadcast([P, 4, P]), ALU.mult).then_inc(self.s_pm, 1)

    def first_of_sums(self, i):
        n, kt = divmod(i, self.nkt)
        return kt == 0 and (not self.narrow or self.steps[n][1] == 0)

    def lanes(self, pe, i, bank, stationary, moving, cols, start):
        for q in range(4):
            mm = pe.matmul(bank[32 * q:32 * q + 32, cols], stationary(q), moving(q), start=start,
                           stop=self.last_of_unit(i), skip_group_check=True)
        return mm

    def tensor_sums(self, pe, i):
        n, kt = divmod(i, self.nkt)
        m = self.steps[n][1]
        first = self.first_of_sums(i)
        if first:
            self.sbank = self.b.S.fill(pe, self.sums(n))
        self.b.A.done(pe, (self.name, "st", n, kt, 3))
        ones = self.core.K("onesm", 32 * m, 32 * m + 32) if self.narrow else self.core.K("ones", 0, 32)
        mm = self.lanes(pe, i, self.sbank, lambda q: ones, lambda q: self.t.p[:, i % 3, q, :], slice(0, T), first)
        if self.last_of_unit(i):
            mm.then_inc(self.b.S.full, 1)

    def tensor_values(self, pe, i):
        n, kt = divmod(i, self.nkt)
        u, m = self.steps[n]
        first = self.first_of_sums(i)
        if first:
            self.obank = self.b.O.fill(pe, self.sums(n))
        v = lambda q: self.t.v(u, kt, m, q)
        if self.own:
            pe.wait_ge(self.s_pm, i + 1)
            mm = self.lanes(pe, i, self.obank, v, lambda q: self.t.pm[:, i % 2, q, :], slice(kt * P, kt * P + P), first)
            if kt:
                mm = self.lanes(pe, i, self.obank, v, lambda q: self.t.p[:, i % 3, q, 0:kt * P], slice(0, kt * P), False)
        else:
            mm = self.lanes(pe, i, self.obank, v, lambda q: self.t.p[:, i % 3, q, :], slice(0, T), first)
        mm.then_inc(self.b.O.full if self.last_of_unit(i) else self.s_pv, 1)

    def scalar_inverse(self, a, n):
        key = self.sums(n)
        k = self.b.S.number[key]
        bank = self.b.S.read(a, key)
        if k:
            a.wait_ge(self.b.O.free, k)
        a.activation(self.t.rs[:, :], bank, ACT.Ln).then_inc(self.s_ln, 1)
        a.wait_ge(self.s_ln, k + 1)
        a.activation(self.t.rs[:, :], self.t.rs[:, :], ACT.Exp, scale=-1.0).then_inc(self.s_rs, 1)

    def vector_divide(self, v, ch, n):
        key = self.sums(n)
        rs, rt = self.t.rs[:, :], self.t.rt[:, :]
        v.wait_ge(self.s_rs, self.b.O.number[key] + 1)
        v.tensor_tensor(rt, self.b.S.banks[0], rs, ALU.mult).then_inc(self.b.S.free, 1)
        self.b.S.done(v, key)
        ch.link(v.scalar_tensor_tensor(rt, rt, 2.0, rs, ALU.subtract, ALU.mult))
        bank = self.b.O.read(v, key)
        v.scalar_tensor_tensor(self.t.o(*self.steps[n]), bank, -1.0, rt, ALU.mult, ALU.mult).then_inc(self.b.O.free, 1)

    def ahead(self, i):
        n, kt = divmod(i, self.nkt)
        if not self.own:
            s = self.scores(n + 2)
            return s[:2], s[2:]
        s = self.scores(n + 1)
        a, b = ((0, 5), (5, 10), (10, 16), (16, 16))[kt]
        return s[a:(a + b) // 2], s[(a + b) // 2:b]

    def turns(self, i):
        n, kt = divmod(i, self.nkt)
        return n + 1 if kt == self.nkt - 1 else None

    def tensor(self, pe, out):
        for n in range(1 if self.own else 2):
            for piece in self.scores(n):
                self.tensor_scores(pe, piece)
            if n == 0:
                self.tensor_turn_max(pe, 0)
        for i in range(self.units):
            for half in range(2):
                pieces = list(self.ahead(i)[half])
                for lane in (2 * half, 2 * half + 1):
                    self.tensor_exps(pe, i, lane)
                    if pieces:
                        self.tensor_scores(pe, pieces.pop(0))
                for piece in pieces:
                    self.tensor_scores(pe, piece)
                if half == 0 and self.turns(i):
                    self.tensor_turn_max(pe, self.turns(i))
                if i and half == 0:
                    self.tensor_sums(pe, i - 1)
                if i and half == 1:
                    self.tensor_values(pe, i - 1)
            if i == 4 * self.nkt + 1:
                out(pe, 0)
        self.tensor_sums(pe, self.units - 1)
        self.tensor_values(pe, self.units - 1)
        out(pe, 1)

    def scalar(self, a):
        a.preload_act_table_set("natural_log_exp_and_others")
        self.scalar_max(a, 0)
        for i in range(self.units):
            for lane in range(4):
                self.scalar_exps(a, i, lane)
                if lane == 1 and self.turns(i):
                    self.scalar_max(a, self.turns(i))
            if i and self.last_of_unit(i - 1):
                self.scalar_inverse(a, (i - 1) // self.nkt)
        self.scalar_inverse(a, len(self.steps) - 1)

    def vector(self, v, ch, out):
        for piece in self.scores(0):
            self.vector_max(v, piece)
        self.vector_negate(v, ch, 0)
        self.vector_max_rows(v, 0)
        if not self.own:
            for piece in self.scores(1):
                self.vector_max(v, piece)
            self.vector_negate(v, ch, 1)
        for i in range(self.units):
            first, second = self.ahead(i)
            if not self.own:
                for piece in first:
                    self.vector_max(v, piece)
                self.vector_max_rows(v, self.turns(i))
                for piece in second:
                    self.vector_max(v, piece)
                if i + 2 <= 7:
                    self.vector_negate(v, ch, i + 2)
            else:
                for piece in first + second:
                    self.vector_max(v, piece)
                n, kt = divmod(i, self.nkt)
                if kt == 2 and n < 7:
                    self.vector_negate(v, ch, n + 1)
                if kt == 3:
                    self.vector_max_rows(v, n + 1)
            if i == 4 * self.nkt + 1:
                out(v, 0)
            if i and self.last_of_unit(i - 1):
                self.vector_divide(v, ch, (i - 1) // self.nkt)
        self.vector_divide(v, ch, len(self.steps) - 1)
        out(v, 1)


def fill_key_ones(v, core, ks, kind):
    s, _ = CST["ksel"]
    one = core.cst[STK:STKM, s:s + 4]
    last = None
    if kind == "self":
        for slot in range(3):
            last = v.tensor_copy(ks[STK:STKM, slot, :, :], one.unsqueeze(2).to_broadcast([8, 4, T]))
    else:
        for u in range(PAIR):
            if kind == "narrow":
                out = ks[STK:STKM, u, :, :].rearrange("p (q m) n -> p q (m n)", q=4)
                last = v.tensor_copy(out, one.unsqueeze(2).to_broadcast([8, 4, 4 * NKE]))
            else:
                out = ks[STK:STKM, u, :, :].rearrange("p (m q) n -> p m q n", q=4)
                last = v.tensor_copy(out, one.unsqueeze(1).unsqueeze(3).to_broadcast([8, 4, 4, NKE]))
    return last


class Space:
    pass


def attention_tensors(core, sb, kind):
    t = Space()
    t.mx = sb("score_max", [P, 2, NT, 4])
    t.nm = sb("neg_max", [P, NT, 4, 2], BF16)
    t.p = sb("weights", [P, 3, 4, T])
    t.rs = sb("inv_sums", [P, T])
    t.rt = sb("newton", [P, T])
    t.stage = t.p if kind == "self" else sb("proj_parts", [P, 2, 4, T])
    if kind == "self":
        t.pm = sb("masked", [P, 2, 4, P])
        t.ks = sb("k_stack", [P, 3, 4, T], F32R)
        t.vv = sb("v_self", [P, PAIR, NT, T])
        t.v = lambda u, kt, m, q: t.vv[:, u, kt, DH * (4 * m + q):DH * (4 * m + q) + DH]
    else:
        t.ks = sb("k_stack", [P, PAIR, H, NKE], F32R)
        t.q4 = sb("q_stack4", [P, 4, T], F32R)
    if kind == "wide":
        t.vv = sb("v_wide", [P, PAIR, T])
        t.v = lambda u, kt, m, q: t.vv[:, u, DH * (4 * m + q):DH * (4 * m + q) + DH]
    if kind == "narrow":
        t.vv = sb("v_narrow", [P, PAIR, 4, 160])
        t.v = lambda u, kt, m, q: t.vv[:, u, q, 32 * m:32 * m + 32]
        t.ot = sb("heads_out", [P, PAIR, T])
        t.o = lambda u, m: t.ot[:, u, :]
    else:
        t.ot = sb("heads_out", [P, 4, T])
        t.o = lambda u, m: t.ot[:, m, :]
    return t


def block_narrow(core, layer, pair, load):
    L = f"L{layer}"
    with ExitStack() as mem, Block(core, f"{L}x", attention=True) as b:
        sb = core.sb(mem, b.name + "_")
        t = attention_tensors(core, sb, "narrow")
        t.ctx = core.ctxp
        norm = Norm(b, "norm", core.x, core.n)
        turn = Turn(b, "turn", norm)
        col = lambda name: (lambda m: core.Cc(name))
        att = Attention(b, "att", "narrow", t, (D // H) ** -0.5, L + "q", col(L + "bq"), L + "k", col(L + "bk"))
        s_ld = b.sem("load")
        s_xb = b.sem("xb")
        s_zero = b.sem("zero")
        s_ones = b.sem("ones")
        D_ = b.D

        @b.block.tensor
        def _(pe):
            turn.tensor(pe)
            if load:
                pe.wait_ge(s_ld, 48)
            for u in range(PAIR):
                att.tensor_project(pe, turn, u)
                bank = D_.fill(pe, ("v", u))
                pe.matmul(bank[0:NK, 0:P], core.ctxp[:, u, 0:NK], core.X(L + "v"), start=True, stop=True)\
                    .then_inc(D_.full, 1)
            D_.done(pe, ("v", PAIR - 1))

            def out(pe, u):
                b.O.done(pe, att.sums(4 * u + 3))
                bank = D_.fill(pe, ("o", u))
                for i in range(NT):
                    tok = slice(i * P, i * P + P)
                    mm = pe.matmul(bank[:, tok], t.ot[:, u, tok], core.F(L + "o"), start=True, stop=True)
                mm.then_inc(D_.full, 1)

            att.tensor(pe, out)

        @b.block.vector
        def _(v):
            ch = Chain(v, b.sem("chain"))
            if load:
                v.wait_ge(s_ld, 48)
            norm.vector_stats(v, ch)
            v.wait_ge(s_zero, 1)
            fill_key_ones(v, core, t.ks, "narrow").then_inc(s_ones, 1)
            norm.vector_apply(v)
            turn.vector(v)
            for u in range(PAIR):
                att.vector_project(v, u)
                bank = D_.read(v, ("v", u))
                v.wait_ge(s_zero, 2)
                v.tensor_tensor(t.vv[0:NK, u, :, :].rearrange("p q (m e) -> p q m e", e=40)[:, :, :, 0:8],
                                bank[0:NK, 0:P].rearrange("p (q m e) -> p q m e", q=4, m=4),
                                core.R(L + "bv")[0:NK].rearrange("p (q m e) -> p q m e", q=4, m=4),
                                ALU.add).then_inc(D_.free, 1)

            def out(v, u):
                bank = D_.read(v, ("o", u))
                v.wait_ge(s_xb, 1)
                x = core.toks(core.x, u).rearrange("p t d -> p (t d)")
                v.scalar_tensor_tensor(x, bank, core.tg[:, layer:layer + 1], x, ALU.mult, ALU.add)\
                    .then_inc(D_.free, 1)

            att.vector(v, ch, out)

        @b.block.scalar
        def _(a):
            turn.scalar(a)
            for u in range(PAIR):
                att.scalar_project(a, u)
            a.wait_ge(s_zero, 4)
            att.scalar(a)

        @b.block.gpsimd
        def _(g):
            g.memset(f32(t.ks[:, :, :, :]), 0.0).then_inc(s_zero, 1)
            norm.gpsimd(g)
            g.memset(t.vv[:, :, :, :], 0.0).then_inc(s_zero, 1)
            g.memset(f32(t.q4[:, :, :]), 0.0).then_inc(s_zero, 1)
            g.memset(t.p[:, :, :, :], 0.0).then_inc(s_zero, 1)
            g.wait_ge(norm.s_n, PAIR)
            g.tensor_tensor(core.x[:, :, :], core.x[:, :, :], core.rows(L + "bo", PAIR * NT), ALU.add).then_inc(s_xb, 1)

        @b.block.sync
        def _(sp):
            if load:
                sp.dma_start(core.x[:, :, :], core.io["x"][bass.ds(pair * PAIR, PAIR)]
                             .rearrange("b (t p) d -> p (b t) d", p=P)).then_inc(s_ld, 16)
                sp.dma_start(core.ctxp[:, :, :], core.io["ctxT"][:, bass.ds(pair * PAIR, PAIR), :]).then_inc(s_ld, 16)
                sp.dma_start(core.ctxr[:, :, :], core.io["ctx"][bass.ds(pair * PAIR, PAIR)]
                             .rearrange("b k c -> k b c")).then_inc(s_ld, 16)
            sp.wait_ge(s_ones, 1)
            sp.wait_ge(s_zero, 3)
            att.sync(sp)


def block_experts0(core):
    with ExitStack() as mem, Block(core, "e0") as b:
        sb = core.sb(mem, b.name + "_")
        raw = sb("w1_raw", [P, 2, 4 * F0])
        wl = sb("w1_lo", [P, 2 * E0 * F0], F32R)
        wh = sb("w1_hi", [P, 2 * E0 * F0], F32R)
        w2 = sb("w2", [P, 2 * E0, D])
        b2 = sb("b2", [E0, D])
        bv = sb("b_value", [P, E0, 2])
        lg = sb("logits", [P, PAIR * NT, E0])
        gate = Gate(core, sb, E0)
        wt = sb("w_turned", [E0, PAIR * NT, P])
        gc = sb("gate_clipped", [P, 3, T])
        sg = sb("gate_sigmoid", [P, 3, T])
        vc = sb("value", [P, 3, T])
        h = sb("hidden", [P, 3, T])
        acc = sb("acc", [P, NT, D])
        diff = sb("logit_diff", [P, PAIR * NT])
        w01 = sb("weights01", [P, 2, PAIR * NT])
        comb = sb("combine", [P, PAIR * NT, E0])
        part = sb("combine_part", [P, PAIR * NT, E0])
        norm = Norm(b, "norm", core.x, core.n)
        turn = Turn(b, "turn", norm)
        s_ld = [b.sem(f"load{i}") for i in range(3)]
        s_wh = b.sem("w_hi")
        s_wl = b.sem("w_lo")
        s_diff = b.sem("diff")
        s_w01 = b.sem("w01")
        s_comb = b.sem("comb")
        s_wt = b.sem("wt")
        s_gc = b.D.free
        s_bv = b.sem("bv")
        s_sg = b.sem("sg")
        s_t = b.sem("t")
        s_h = b.sem("h")
        s_y = b.sem("y")
        units = [(u, e, s) for u in range(PAIR) for e in range(E0) for s in range(2)]
        b1, _ = COL["b1"]

        def bias1(e, what, s):
            k = b1 + 4 * e + 2 * what + s
            return core.col[:, k:k + 1]

        def w1(w, e, what, s):
            k = (2 * e + what) * F0 + s * P
            return w[:, k:k + P]

        def chunk(c):
            return slice(4 * F0 * c, 4 * F0 * (c + 1))

        def wait_y(eng, j):
            u, e, s = units[j]
            if s:
                b.O.read(eng, ("y", u, e))
            else:
                eng.wait_ge(s_y, j // 2 + 1)

        @b.block.tensor
        def _(pe):
            turn.tensor(pe)
            bank = b.S.fill(pe, "logits")
            for u in range(PAIR):
                turn.ready(pe, u)
                for i in range(NT):
                    k = E0 * (NT * u + i)
                    mm = product_rows(pe, core, bank[:, k:k + E0], "g0", u, i)
            mm.then_inc(b.S.full, 1)
            def hidden(j):
                u, e, s = units[j]
                if u == 0 and s == 0:
                    pe.wait_ge(s_wl, e // 2 + 1)
                for what, ring in ((0, b.D), (1, b.A)):
                    bank = ring.fill(pe, ("h", j))
                    pe.matmul(bank, w1(wh, e, what, s), core.nh[:, u, :], start=True, stop=False)
                    pe.matmul(bank, w1(wh, e, what, s), core.nl[:, u, :], start=False, stop=False)
                    pe.matmul(bank, w1(wl, e, what, s), core.nh[:, u, :], start=False, stop=True).then_inc(ring.full, 1)

            def down(j):
                u, e, s = units[j]
                if s == 0:
                    self_bank[0] = b.O.fill(pe, ("y", u, e))
                pe.wait_ge(s_h, j + 1)
                for i in range(NT):
                    mm = pe.matmul(self_bank[0][:, i * P:i * P + P], h[:, j % 3, i * P:i * P + P], w2[:, 2 * e + s, :],
                                   start=s == 0 and i == 0, stop=s == 1, skip_group_check=True)
                mm.then_inc(b.O.full if s else s_y, 1)

            self_bank = [None]
            hidden(0)
            hidden(1)
            pe.wait_ge(s_comb, 1)
            pe.wait_ge(s_ld[2], 32)
            for u in range(PAIR):
                bank = b.S.fill(pe, ("wt", u))
                for i in range(NT):
                    mm = pe.transpose(bank[0:E0, i * P:i * P + P], comb[:, NT * u + i, :], core.K("ident"))
                mm.then_inc(b.S.full, 1)
            for u in range(PAIR):
                b.S.done(pe, ("wt", u))
                bank = b.S.fill(pe, ("bias", u))
                for i in range(NT):
                    mm = pe.matmul(bank[:, i * P:i * P + P], wt[:, NT * u + i, :], b2[:, :], start=True, stop=True)
                mm.then_inc(b.S.full, 1)
            for j in range(2, len(units)):
                hidden(j)
                down(j - 2)
            down(len(units) - 2)
            down(len(units) - 1)

        @b.block.scalar
        def _(a):
            turn.scalar(a)
            for c in range(E0 // 2):
                a.wait_ge(s_ld[c % 2], 16 * (c // 2 + 1))
                a.activation(wh[:, chunk(c)], raw[:, c % 2, :], ACT.Copy).then_inc(s_wh, 1)
            a.wait_ge(s_diff, 1)
            a.activation(w01[:, 0, :], diff[:, :], ACT.Sigmoid)
            a.activation(w01[:, 1, :], diff[:, :], ACT.Sigmoid, scale=-1.0).then_inc(s_w01, 1)
            a.wait_ge(s_bv, 1)
            for j, (u, e, s) in enumerate(units):
                bank = b.A.read(a, ("h", j))
                if j >= 3:
                    a.wait_ge(s_h, j - 2)
                a.activation(vc[:, j % 3, :], bank, ACT.Identity, bias=bv[:, e, s:s + 1]).then_inc(b.A.free, 1)
                b.D.done(a, ("h", j))
                a.activation(sg[:, j % 3, :], gc[:, j % 3, :], ACT.Sigmoid, scale=1.702).then_inc(s_sg, 1)

        @b.block.gpsimd
        def _(g):
            norm.gpsimd(g)
            for c in range(E0 // 2):
                g.wait_ge(s_wh, c + 1)
                g.tensor_tensor(wl[:, chunk(c)], raw[:, c % 2, :], f32(wh[:, chunk(c)]), ALU.subtract).then_inc(s_wl, 1)
            for j, (u, e, s) in enumerate(units):
                b.A.done(g, ("h", j))
                g.tensor_scalar(vc[:, j % 3, :], vc[:, j % 3, :], -8.0, 10.0, ALU.max, ALU.min)
                g.wait_ge(s_sg, j + 1)
                g.tensor_tensor(sg[:, j % 3, :], sg[:, j % 3, :], gc[:, j % 3, :], ALU.mult).then_inc(s_t, 1)

        @b.block.vector
        def _(v):
            ch = Chain(v, b.sem("chain"))
            norm.vector_stats(v, ch)
            norm.vector_apply(v)
            v.tensor_scalar(bv[:, :, :], core.col[:, b1:b1 + 4 * E0].rearrange("p (e w s) -> p e w s", e=E0, w=2)[:, :, 1, :],
                            1.0, None, ALU.add).then_inc(s_bv, 1)
            turn.vector(v)
            bank = b.S.read(v, "logits")
            ins = v.tensor_copy(lg[:, :, :], bank[:, 0:PAIR * NT * E0].rearrange("p (t e) -> p t e", e=E0))
            ins.then_inc(b.S.free, 1)
            b.S.done(v, "logits")
            gate.largest(v, ch, lg)
            v.tensor_tensor(diff[:, :], gate.mx[:, :, 0], gate.mx[:, :, 1], ALU.subtract).then_inc(s_diff, 1)
            v.wait_ge(s_w01, 1)
            for k, out in ((0, comb), (1, part)):
                ch.link(gate.one_hot(v, out[:, :, :], k))
                ch.link(v.tensor_tensor(out[:, :, :], out[:, :, :], w01[:, k, :].unsqueeze(2).to_broadcast([P, PAIR * NT, E0]),
                                        ALU.mult))
            ins = v.tensor_tensor(comb[:, :, :], comb[:, :, :], part[:, :, :], ALU.add)
            ins.then_inc(s_comb, 1)
            v.wait_ge(s_comb, 1)

            def clip(j):
                u, e, s = units[j]
                bank = b.D.read(v, ("h", j))
                v.tensor_scalar(gc[:, j % 3, :], bank, bias1(e, 0, s), 9.0, ALU.add, ALU.min).then_inc(b.D.free, 1)

            def combine(u, e):
                bank = b.O.read(v, ("y", u, e))
                if e == 0:
                    src = b.S.read(v, ("bias", u))
                    ins = v.tensor_copy(acc[:, :, :], src.rearrange("p (t d) -> p t d", t=NT))
                    ins.then_inc(b.S.free, 1)
                    b.S.done(v, ("bias", u))
                for i in range(NT):
                    ins = v.scalar_tensor_tensor(acc[:, i, :], bank[:, i * P:i * P + P], comb[:, NT * u + i, e:e + 1],
                                                 acc[:, i, :], ALU.mult, ALU.add)
                ins.then_inc(b.O.free, 1)
                b.O.done(v, ("y", u, e))
                if e == E0 - 1:
                    x = core.toks(core.x, u)
                    ch.link(v.scalar_tensor_tensor(x, acc[:, :, :], core.tg[:, 4:5], x, ALU.mult, ALU.add))

            clip(0)
            clip(1)
            for u in range(PAIR):
                bank = b.S.read(v, ("wt", u))
                v.tensor_copy(wt[:, NT * u:NT * u + NT, :], bank[0:E0, :].rearrange("p (t d) -> p t d", t=NT))\
                    .then_inc(b.S.free, 1)
            n = len(units)
            for j in range(n + 2):
                if 2 <= j < n:
                    clip(j)
                if j < n:
                    v.wait_ge(s_t, j + 1)
                    if j >= 3:
                        wait_y(v, j - 3)
                    v.tensor_tensor(h[:, j % 3, :], sg[:, j % 3, :], vc[:, j % 3, :], ALU.mult).then_inc(s_h, 1)
                k = j - 3
                if k >= 0 and units[k][2]:
                    combine(*units[k][:2])
            combine(*units[n - 1][:2])

        @b.block.sync
        def _(sp):
            for c in range(E0 // 2):
                if c >= 2:
                    sp.wait_ge(s_wl, c - 1)
                sp.dma_start(raw[:, c % 2, :], core.io["w1"][:, chunk(c)]).then_inc(s_ld[c % 2], 16)
                if c == 1:
                    sp.dma_start(w2[:, :, :], core.io["w2"]).then_inc(s_ld[2], 16)
                    sp.dma_start(b2[:, :], core.io["b2"]).then_inc(s_ld[2], 16)


class Gate:

    def __init__(self, core, sb, experts):
        n = PAIR * NT
        self.core, self.experts = core, experts
        self.mx = sb("largest", [P, n, 8])
        self.ix = sb("largest_at", [P, n, 8], U32)
        self.ixf = sb("largest_at_f", [P, n, 8])

    def largest(self, v, ch, scores):
        for t in range(PAIR * NT):
            last = v.max(self.mx[:, t, :], scores[:, t, :])
        ch.link(last)
        for t in range(PAIR * NT):
            last = v.max_index(self.ix[:, t, :], self.mx[:, t, :], scores[:, t, :])
        ch.link(last)
        ch.link(v.tensor_copy(self.ixf[:, :, :], self.ix[:, :, :]))

    def one_hot(self, v, out, k):
        n = PAIR * NT
        return v.tensor_tensor(out, self.core.K("iota", 0, self.experts).unsqueeze(1).to_broadcast([P, n, self.experts]),
                               self.ixf[:, :, k:k + 1].to_broadcast([P, n, self.experts]), ALU.is_equal)


class Tail:

    def __init__(self, b, a, att, xo, k_bias):
        self.b, self.core, self.a, self.att, self.xo, self.k_bias = b, b.core, a, att, xo, k_bias
        self.s_xb = b.sem("t_xb")
        self.s_xo = b.sem("t_xo")
        self.s_r = b.sem("t_r")
        self.norm = Norm(b, "t_norm", xo, b.core.n)
        self.turn = Turn(b, "t_turn", self.norm)

    def hidden(self, u, m):
        t = self.att.t
        return t.p[:, 0, m, :] if u else t.ot[:, m, :]

    def tensor_out(self, pe, u):
        b, att = self.b, self.att
        b.O.done(pe, att.sums(4 * u + 3))
        bank = b.D.fill(pe, ("li1", u))
        for i in range(NT):
            tok = slice(i * P, i * P + P)
            for m in range(4):
                mm = pe.matmul(bank[:, tok], att.t.ot[:, m, tok], self.core.F(self.a + "li1", m * P, m * P + P),
                               start=m == 0, stop=m == 3)
        mm.then_inc(b.D.full, 1)

    def vector_out(self, v, u):
        bank = self.b.D.read(v, ("li1", u))
        if u == 0:
            v.wait_ge(self.s_xb, 1)
        x = self.core.toks(self.xo, u).rearrange("p t d -> p (t d)")
        v.tensor_tensor(x, bank, x, ALU.add).then_inc(self.b.D.free, 1)

    def gpsimd_bias(self, g):
        c = self.core
        g.tensor_tensor(self.xo[:, :, :], c.x1[:, :, :], c.rows(self.a + "li1b", PAIR * NT), ALU.add)\
            .then_inc(self.s_xb, 1)

    def tensor(self, pe):
        b, c = self.b, self.core
        self.turn.tensor(pe)
        for u in range(PAIR):
            self.turn.ready(pe, u)
            for m in range(4):
                bank = b.A.fill(pe, ("li2", u, m))
                product(pe, c, bank, self.a + "li2", u, m * P, m * P + P).then_inc(b.A.full, 1)
            if u:
                self.tensor_last(pe, 0)
        self.tensor_last(pe, 1)

    def tensor_last(self, pe, u):
        b, c = self.b, self.core
        bank = b.D.fill(pe, ("li3", u))
        b.A.done(pe, ("li2", u, 3))
        for i in range(NT):
            tok = slice(i * P, i * P + P)
            for m in range(4):
                mm = pe.matmul(bank[:, tok], self.hidden(u, m)[:, tok], c.F(self.a + "li3", m * P, m * P + P),
                               start=m == 0, stop=m == 3)
        mm.then_inc(b.D.full, 1)

    def scalar(self, a):
        self.turn.scalar(a)
        for u in range(PAIR):
            for m in range(4):
                bank = self.b.A.read(a, ("li2", u, m))
                k = self.k_bias + m
                a.activation(self.hidden(u, m), bank, ACT.Gelu, bias=self.core.bias[:, k:k + 1])\
                    .then_inc(self.b.A.free, 1)

    def gpsimd(self, g):
        c = self.core
        self.norm.gpsimd(g)
        s = self.b.sem("t_g")
        g.tensor_tensor(c.x1[:, :, :], c.x1[:, :, :], c.rows(self.a + "li3b", PAIR * NT), ALU.add).then_inc(s, 1)
        g.wait_ge(s, 1)
        g.tensor_tensor(c.x1[:, :, :], c.x1[:, :, :], self.xo[:, :, :], ALU.add).then_inc(self.s_r, 1)

    def vector(self, v, ch):
        self.b.D.done(v, ("li1", 1))
        self.norm.vector_stats(v, ch)
        self.norm.vector_apply(v)
        self.turn.vector(v)
        for u in range(PAIR):
            bank = self.b.D.read(v, ("li3", u))
            v.wait_ge(self.s_r, 1)
            x = self.core.toks(self.core.x1, u).rearrange("p t d -> p (t d)")
            v.tensor_tensor(x, bank, x, ALU.add).then_inc(self.b.D.free, 1)
        self.b.D.done(v, ("li3", 1))


def gains(v, core, ch, name):
    ch.link(v.tensor_tensor(core.x1[:, :, :], core.n[:, :, :], core.rows(name + "g", PAIR * NT), ALU.mult))
    ch.link(v.tensor_tensor(core.x1[:, :, :], core.x1[:, :, :], core.rows(name + "b", PAIR * NT), ALU.add))


def block_self(core):
    with ExitStack() as mem, Block(core, "s1", attention=True) as b:
        sb = core.sb(mem, b.name + "_")
        t = attention_tensors(core, sb, "self")
        xo = sb("x_out", [P, PAIR * NT, D])
        outer = Norm(b, "outer", core.x, core.n)
        first = Norm(b, "first", core.n, core.n)
        norm = Norm(b, "norm", core.x1, core.n)
        turn = Turn(b, "turn", norm)
        col = lambda k: (lambda m: core.bias[:, k + m:k + m + 1])
        att = Attention(b, "att", "self", t, DH ** -0.5, "a1q", col(0), "a1k", col(4))
        tail = Tail(b, "a1", att, xo, 8)
        last = Norm(b, "last", core.x1, core.n)
        s_ones = b.sem("ones")

        @b.block.tensor
        def _(pe):
            turn.tensor(pe)
            for u in range(PAIR):
                att.tensor_project(pe, turn, u)
                for kt in range(NT):
                    bank = b.D.fill(pe, ("v", u, kt))
                    product_rows(pe, core, bank, "a1v", u, kt).then_inc(b.D.full, 1)
            b.D.done(pe, ("v", 1, NT - 1))
            att.tensor(pe, tail.tensor_out)
            tail.tensor(pe)

        @b.block.scalar
        def _(a):
            turn.scalar(a)
            for u in range(PAIR):
                att.scalar_project(a, u)
            att.staging_done(a, len(att.items))
            att.scalar(a)
            tail.scalar(a)

        @b.block.gpsimd
        def _(g):
            outer.gpsimd(g)
            first.gpsimd(g)
            norm.gpsimd(g)
            tail.gpsimd_bias(g)
            att.gpsimd_mask(g)
            tail.gpsimd(g)
            last.gpsimd(g)

        @b.block.vector
        def _(v):
            ch = Chain(v, b.sem("chain"))
            outer.vector_stats(v, ch)
            outer.vector_apply(v)
            v.wait_ge(outer.s_n, PAIR)
            first.vector_stats(v, ch)
            first.vector_apply(v)
            v.wait_ge(first.s_n, PAIR)
            gains(v, core, ch, "ln1")
            norm.vector_stats(v, ch)
            norm.vector_apply(v)
            fill_key_ones(v, core, t.ks, "self").then_inc(s_ones, 1)
            turn.vector(v)
            for u in range(PAIR):
                att.vector_project(v, u)
                for kt in range(NT):
                    bank = b.D.read(v, ("v", u, kt))
                    v.tensor_tensor(t.vv[:, u, kt, :], bank, core.vb1[:, :], ALU.add).then_inc(b.D.free, 1)
            att.vector(v, ch, tail.vector_out)
            tail.vector(v, ch)
            last.vector_stats(v, ch)
            last.vector_apply(v)
            v.wait_ge(last.s_n, PAIR)
            gains(v, core, ch, "ln2")

        @b.block.sync
        def _(sp):
            sp.wait_ge(s_ones, 1)
            att.sync(sp)


def block_wide(core):
    with ExitStack() as mem, Block(core, "w1", attention=True) as b:
        sb = core.sb(mem, b.name + "_")
        t = attention_tensors(core, sb, "wide")
        t.ctx = sb("ctxT_norm", [NC, PAIR, NKE])
        cn = sb("ctx_norm", [NK, PAIR, NC])
        xo = sb("x_out", [P, PAIR * NT, D])
        cnorm = Norm(b, "cnorm", core.ctxr, cn, parts=NK, tiles=PAIR)
        norm = Norm(b, "norm", core.x1, core.n)
        turn = Turn(b, "turn", norm)
        col = lambda k: (lambda m: core.bias[:, k + m:k + m + 1])
        att = Attention(b, "att", "wide", t, DH ** -0.5, "a2q", col(12), "a2k", col(20))
        tail = Tail(b, "a2", att, xo, 16)
        s_zero = b.sem("zero")
        s_ones = b.sem("ones")

        @b.block.tensor
        def _(pe):
            for u in range(PAIR):
                pe.wait_ge(cnorm.s_n, u + 1)
                bank = b.D.fill(pe, ("ctx", u))
                pe.transpose(bank[0:NC, 0:NK], cn[:, u, :], core.K("ident", 0, NK, NK)).then_inc(b.D.full, 1)
            turn.tensor(pe)
            b.D.done(pe, ("ctx", 1))
            for u in range(PAIR):
                att.tensor_project(pe, turn, u)
                bank = b.D.fill(pe, ("v", u))
                pe.matmul(bank[0:NK, :], t.ctx[:, u, 0:NK], core.X("a2v"), start=True, stop=True).then_inc(b.D.full, 1)
            b.D.done(pe, ("v", 1))
            att.tensor(pe, tail.tensor_out)
            tail.tensor(pe)

        @b.block.scalar
        def _(a):
            turn.scalar(a)
            for u in range(PAIR):
                att.scalar_project(a, u)
            a.wait_ge(s_zero, 3)
            att.scalar(a)
            tail.scalar(a)

        @b.block.gpsimd
        def _(g):
            g.memset(t.ctx[:, :, :], 0.0).then_inc(s_zero, 1)
            cnorm.gpsimd(g)
            norm.gpsimd(g)
            g.memset(t.vv[:, :, :], 0.0).then_inc(s_zero, 1)
            g.memset(t.p[:, :, :, :], 0.0).then_inc(s_zero, 1)
            tail.gpsimd_bias(g)
            tail.gpsimd(g)

        @b.block.vector
        def _(v):
            ch = Chain(v, b.sem("chain"))
            cnorm.vector_stats(v, ch)
            cnorm.vector_apply(v)
            norm.vector_stats(v, ch)
            norm.vector_apply(v)
            v.wait_ge(s_zero, 1)
            for u in range(PAIR):
                bank = b.D.read(v, ("ctx", u))
                v.tensor_copy(t.ctx[:, u, 0:NK], bank[0:NC, 0:NK]).then_inc(b.D.free, 1)
            fill_key_ones(v, core, t.ks, "wide").then_inc(s_ones, 1)
            turn.vector(v)
            for u in range(PAIR):
                att.vector_project(v, u)
                bank = b.D.read(v, ("v", u))
                if u == 0:
                    v.wait_ge(s_zero, 2)
                v.tensor_tensor(t.vv[0:NK, u, :], bank[0:NK, :], core.vb2[0:NK, :], ALU.add).then_inc(b.D.free, 1)
            att.vector(v, ch, tail.vector_out)
            tail.vector(v, ch)
            v.scalar_tensor_tensor(core.x[:, :, :], core.x1[:, :, :], core.tg[:, 1:2], core.x[:, :, :], ALU.mult, ALU.add)

        @b.block.sync
        def _(sp):
            sp.wait_ge(s_ones, 1)
            att.sync(sp)


def block_experts1(core):
    TILES = E1 // 2
    with ExitStack() as mem, Block(core, "e1") as b:
        sb = core.sb(mem, "e1_")
        n = PAIR * NT
        down = sb("w_down", [P, TILES + 1, D])
        gate = Gate(core, sb, E1)
        score = sb("scores", [P, n, E1])
        comb = sb("combine", [P, n, E1])
        hot = sb("one_hot", [P, n, E1])
        total = sb("top_sum", [P, n])
        c3 = sb("combine_parts", [P, n, 3, E1], BF16)
        ct = sb("combine_turned", [3 * E1, PAIR, T], BF16)
        sg = sb("gate_silu", [P, 3, T])
        up = sb("hidden_raw", [P, 3, T])
        h = sb("hidden", [P, 3, T])
        norm = Norm(b, "norm", core.x, core.n)
        turn = Turn(b, "turn", norm)
        s_ld = b.sem("load")
        s_score = b.sem("score")
        s_comb = b.sem("comb")
        s_y = b.sem("y")
        units = [(u, j) for u in range(PAIR) for j in range(TILES + 1)]

        def wait_y(eng, i):
            u, j = units[i]
            if j == TILES:
                b.O.read(eng, ("y", u))
            else:
                eng.wait_ge(s_y, i + 1 - u)

        @b.block.tensor
        def _(pe):
            turn.tensor(pe)
            bank = b.S.fill(pe, "logits")
            for u in range(PAIR):
                turn.ready(pe, u)
                for i in range(NT):
                    k = E1 * (NT * u + i)
                    mm = product_rows(pe, core, bank[:, k:k + E1], "g1", u, i)
            mm.then_inc(b.S.full, 1)

            def hidden(i):
                u, j = units[i]
                for what, ring in ((0, b.A), (1, b.D)):
                    bank = ring.fill(pe, ("h", i))
                    if j < TILES:
                        product(pe, core, bank, ("eg", "eu")[what], u, j * P, j * P + P).then_inc(ring.full, 1)
                    else:
                        product(pe, core, bank, ("sg", "su")[what], u).then_inc(ring.full, 1)
                if j < TILES:
                    bank = b.S.fill(pe, ("c", i))
                    pe.matmul(bank, core.sel48[:, j * P:j * P + P], ct[:, u, :], start=True, stop=True).then_inc(b.S.full, 1)

            def down_sum(i):
                u, j = units[i]
                if j == 0:
                    y[0] = b.O.fill(pe, ("y", u))
                if i == 0:
                    pe.wait_ge(s_ld, 16)
                if j < TILES:
                    b.S.done(pe, ("c", i))
                else:
                    b.D.done(pe, ("h", i))
                for t in range(NT):
                    mm = pe.matmul(y[0][:, t * P:t * P + P], h[:, i % 3, t * P:t * P + P], down[:, j, :],
                                   start=j == 0 and t == 0, stop=j == TILES, skip_group_check=True)
                mm.then_inc(b.O.full if j == TILES else s_y, 1)

            y = [None]
            pe.wait_ge(s_comb, 1)
            for u in range(PAIR):
                bank = b.S.fill(pe, ("ct", u)).bitcast(BF16)
                for t in range(NT):
                    mm = pe.transpose(bank[0:3 * E1, t * P:t * P + P], c3[:, NT * u + t, :, :].rearrange("p k e -> p (k e)"),
                                      core.identb[:, :])
                mm.then_inc(b.S.full, 1)
            b.S.done(pe, ("ct", 1))
            for i in range(len(units)):
                hidden(i)
                if i >= 2:
                    down_sum(i - 2)
            down_sum(len(units) - 2)
            down_sum(len(units) - 1)

        @b.block.scalar
        def _(a):
            turn.scalar(a)
            bank = b.S.read(a, "logits")
            a.activation(score[:, :, :], bank[:, 0:n * E1].rearrange("p (t e) -> p t e", e=E1), ACT.Sigmoid)\
                .then_inc(b.S.free, 1)
            for i in range(len(units)):
                bank = b.A.read(a, ("h", i))
                if i >= 3:
                    b.D.done(a, ("h", i - 3))
                a.activation(sg[:, i % 3, :], bank, ACT.Silu).then_inc(b.A.free, 1)

        @b.block.gpsimd
        def _(g):
            norm.gpsimd(g)

        @b.block.vector
        def _(v):
            ch = Chain(v, b.sem("chain"))
            norm.vector_stats(v, ch)
            norm.vector_apply(v)
            turn.vector(v)
            b.S.done(v, "logits")
            gate.largest(v, ch, score)
            ch.link(v.tensor_reduce(total[:, :], gate.mx[:, :, 0:4], AX, ALU.add))
            ch.link(v.tensor_scalar(total[:, :], total[:, :], 1e-20, None, ALU.add))
            ch.link(v.reciprocal(total[:, :], total[:, :]))
            ch.link(gate.one_hot(v, comb[:, :, :], 0))
            for k in range(1, 4):
                ch.link(gate.one_hot(v, hot[:, :, :], k))
                ch.link(v.tensor_tensor(comb[:, :, :], comb[:, :, :], hot[:, :, :], ALU.add))
            ch.link(v.tensor_tensor(comb[:, :, :], comb[:, :, :], score[:, :, :], ALU.mult))
            ch.link(v.tensor_tensor(comb[:, :, :], comb[:, :, :], total[:, :].unsqueeze(2).to_broadcast([P, n, E1]), ALU.mult))
            for k in range(3):
                ins = v.tensor_copy(c3[:, :, k, :], comb[:, :, :])
                if k < 2:
                    ch.link(ins)
                    ch.link(v.tensor_tensor(comb[:, :, :], comb[:, :, :], c3[:, :, k, :], ALU.subtract))
            ins.then_inc(s_comb, 1)
            for u in range(PAIR):
                bank = b.S.read(v, ("ct", u)).bitcast(BF16)
                v.tensor_copy(ct[:, u, :], bank[0:3 * E1, 0:T]).then_inc(b.S.free, 1)

            def add(u):
                bank = b.O.read(v, ("y", u))
                x = core.toks(core.x, u).rearrange("p t d -> p (t d)")
                v.scalar_tensor_tensor(x, bank, core.tg[:, 5:6], x, ALU.mult, ALU.add).then_inc(b.O.free, 1)

            for i, (u, j) in enumerate(units):
                bank = b.D.read(v, ("h", i))
                b.A.done(v, ("h", i))
                if i >= 3:
                    wait_y(v, i - 3)
                out = up if j < TILES else h
                v.tensor_tensor(out[:, i % 3, :], bank, sg[:, i % 3, :], ALU.mult).then_inc(b.D.free, 1)
                if j < TILES:
                    b.D.done(v, ("h", i))
                    bank = b.S.read(v, ("c", i))
                    v.tensor_tensor(h[:, i % 3, :], bank, up[:, i % 3, :], ALU.mult).then_inc(b.S.free, 1)
                if j == 2 and u:
                    add(0)
            add(1)

        @b.block.sync
        def _(sp):
            sp.dma_start(down[:, :, :], core.io["down"]).then_inc(s_ld, 16)


def block_single(core):
    with ExitStack() as mem, Block(core, "L2x") as b:
        sb = core.sb(mem, "L2x_")
        qh = sb("q_hi", [P, PAIR, T], F32R)
        ql = sb("q_lo", [P, PAIR, T], F32R)
        kh = sb("k_hi", [P, PAIR, NKE], F32R)
        kl = sb("k_lo", [P, PAIR, NKE], F32R)
        vv = sb("v", [NK, PAIR, D])
        mx = sb("score_max", [P, PAIR, NT])
        nm = sb("neg_max", [P, PAIR, NT, 2], BF16)
        nmt = sb("neg_max_turned", [2, PAIR, T], BF16)
        p = sb("weights", [NK, PAIR, T])
        rs = sb("inv_sums", [P, PAIR, NT])
        norm = Norm(b, "norm", core.x, core.n)
        turn = Turn(b, "turn", norm)
        s_hi = b.sem("hi")
        s_nm = b.sem("nm")
        s_sum = b.sem("sum")

        @b.block.tensor
        def _(pe):
            for u in range(PAIR):
                bank = b.S.fill(pe, ("k", u))
                pe.matmul(bank[:, 0:NKE], core.X("L2k"), core.ctxp[:, u, :], start=True, stop=True).then_inc(b.S.full, 1)
            for u in range(PAIR):
                bank = b.S.fill(pe, ("v", u))
                pe.matmul(bank[0:NK, 0:D], core.ctxp[:, u, 0:NK], core.X("L2v"), start=True, stop=True)\
                    .then_inc(b.S.full, 1)
            turn.tensor(pe)
            for u in range(PAIR):
                turn.ready(pe, u)
                bank = b.D.fill(pe, ("q", u))
                product(pe, core, bank, "L2q", u).then_inc(b.D.full, 1)
            for u in range(PAIR):
                b.D.done(pe, ("q", u))
                b.S.done(pe, ("k", u))
                bank = b.D.fill(pe, ("s", u))
                for t in range(NT):
                    tok = slice(t * P, t * P + P)
                    out = bank[:, t * KSLOT:t * KSLOT + NKE]
                    pe.matmul(out, qh[:, u, tok], kh[:, u, :], start=True, stop=False)
                    pe.matmul(out, qh[:, u, tok], kl[:, u, :], start=False, stop=False)
                    mm = pe.matmul(out, ql[:, u, tok], kh[:, u, :], start=False, stop=True)
                mm.then_inc(b.D.full, 1)
            for u in range(PAIR):
                pe.wait_ge(s_nm, u + 1)
                bank = b.S.fill(pe, ("nm", u)).bitcast(BF16)
                for t in range(NT):
                    mm = pe.transpose(bank[0:2, t * P:t * P + P], nm[:, u, t, :], core.identb[:, :])
                mm.then_inc(b.S.full, 1)
            for u in range(PAIR):
                bank = b.A.fill(pe, ("st", u))
                out = bank[0:NK, :]
                pe.matmul(out, kh[:, u, 0:NK], qh[:, u, :], start=True, stop=False)
                pe.matmul(out, kh[:, u, 0:NK], ql[:, u, :], start=False, stop=False)
                pe.matmul(out, kl[:, u, 0:NK], qh[:, u, :], start=False, stop=False)
                b.S.done(pe, ("nm", u))
                pe.matmul(out, core.ones2[:, 0:NK], nmt[:, u, :], start=False, stop=True).then_inc(b.A.full, 1)
            for u in range(PAIR):
                b.A.done(pe, ("st", u))
                b.S.done(pe, ("v", u))
                bank = b.O.fill(pe, ("y", u))
                sums = b.S.fill(pe, ("sum", u))
                for t in range(NT):
                    tok = slice(t * P, t * P + P)
                    pe.matmul(sums[:, 2 * t:2 * t + 2], p[:, u, tok], core.K("ones", 0, 2, NK), start=True, stop=True)
                    mm = pe.matmul(bank[:, tok], p[:, u, tok], vv[:, u, :], start=True, stop=True)
                mm.then_inc(b.O.full, 1)

        @b.block.scalar
        def _(a):
            for u in range(PAIR):
                bank = b.S.read(a, ("k", u))
                a.activation(kh[:, u, :], bank[:, 0:NKE], ACT.Identity, bias=core.Cc("L2bk")).then_inc(s_hi, 1)
            turn.scalar(a)
            for u in range(PAIR):
                bank = b.D.read(a, ("q", u))
                a.activation(qh[:, u, :], bank, ACT.Identity, bias=core.Cc("L2bq")).then_inc(s_hi, 1)
            for u in range(PAIR):
                bank = b.A.read(a, ("st", u))
                a.activation(p[:, u, :], bank[0:NK, :], ACT.Exp).then_inc(b.A.free, 1)

        @b.block.gpsimd
        def _(g):
            norm.gpsimd(g)

        @b.block.vector
        def _(v):
            ch = Chain(v, b.sem("chain"))
            for u in range(PAIR):
                bank = b.S.read(v, ("k", u))
                v.wait_ge(s_hi, u + 1)
                v.scalar_tensor_tensor(kl[:, u, :], bank[:, 0:NKE], core.Cc("L2bk"), f32(kh[:, u, :]), ALU.add,
                                       ALU.subtract).then_inc(b.S.free, 1)
            for u in range(PAIR):
                bank = b.S.read(v, ("v", u))
                v.tensor_tensor(vv[:, u, :], bank[0:NK, 0:D], core.R("L2bv")[0:NK], ALU.add).then_inc(b.S.free, 1)
            norm.vector_stats(v, ch)
            norm.vector_apply(v)
            turn.vector(v)
            for u in range(PAIR):
                bank = b.D.read(v, ("q", u))
                v.wait_ge(s_hi, PAIR + u + 1)
                v.scalar_tensor_tensor(ql[:, u, :], bank, core.Cc("L2bq"), f32(qh[:, u, :]), ALU.add, ALU.subtract)\
                    .then_inc(b.D.free, 1)
            for u in range(PAIR):
                bank = b.D.read(v, ("s", u))
                v.tensor_reduce(mx[:, u, :], bank[:, 0:NT * KSLOT].rearrange("p (t k) -> p t k", t=NT)[:, :, 0:NK], AX,
                                ALU.max).then_inc(b.D.free, 1)
                b.D.done(v, ("s", u))
                hi, lo = nm[:, u, :, 0], nm[:, u, :, 1]
                ch.link(v.tensor_scalar(hi, mx[:, u, :], -1.0, None, ALU.mult))
                v.scalar_tensor_tensor(lo, mx[:, u, :], -1.0, hi, ALU.mult, ALU.subtract).then_inc(s_nm, 1)
            for u in range(PAIR):
                bank = b.S.read(v, ("nm", u)).bitcast(BF16)
                v.tensor_copy(nmt[:, u, :], bank[0:2, 0:T]).then_inc(b.S.free, 1)
            for u in range(PAIR):
                bank = b.O.read(v, ("y", u))
                sums = b.S.banks[b.S.number[("sum", u)] % 2]
                ins = v.reciprocal(rs[:, u, :], sums[:, 0:2 * NT].rearrange("p (t e) -> p t e", e=2)[:, :, 0])
                ins.then_inc(b.S.free, 1)
                b.S.done(v, ("sum", u))
                ch.link(v.tensor_scalar(rs[:, u, :], rs[:, u, :], core.tg[:, 2:3], None, ALU.mult))
                for t in range(NT):
                    x = core.x[:, NT * u + t, :]
                    ins = v.scalar_tensor_tensor(x, bank[:, t * P:t * P + P], rs[:, u, t:t + 1], x, ALU.mult, ALU.add)
                ins.then_inc(b.O.free, 1)


def block_signs(core):
    with ExitStack() as mem, Block(core, "sg") as b:
        sb = core.sb(mem, "sg_")
        words = [sb("k0", [P, 2, T // 4], U32), sb("k1", [P, T], U32), sb("k2", [P, D], U32)]
        k0, k1, k2 = words[0][:, :, :].bitcast(U8), words[1][:, :].bitcast(U8), words[2][:, :].bitcast(U8)
        half = sb("w0_half", [P, 2, T])
        w0 = sb("w0", [P, T], F32R)
        w1 = sb("w1", [P, 4 * T], F32R)
        w2 = sb("w2", [P, 4 * D], F32R)
        s2x = sb("scales", [P, 3])
        r = sb("relu", [P, 3, T])
        hh = sb("h_hi", [P, PAIR, 2, 4, T], F32R)
        hl = sb("h_lo", [P, PAIR, 4, T], F32R)
        norm = Norm(b, "norm", core.x, core.n)
        turn = Turn(b, "turn", norm)
        s_ld = b.sem("load")
        s_w = b.sem("w")
        s_s = b.sem("scale")
        s_r = b.sem("r")
        s_hi = b.sem("hi")
        s_lo = b.sem("lo")
        units = [(layer, u, m) for layer in range(2) for u in range(PAIR) for m in range(4)]

        @b.block.tensor
        def _(pe):
            turn.tensor(pe)
            for i, (layer, u, m) in enumerate(units):
                if m == 0:
                    if layer == 0:
                        turn.ready(pe, u)
                    if u == 0:
                        pe.wait_ge(s_w, 1 + layer)
                    if layer == 1:
                        pe.wait_ge(s_lo, 4 * u + 4)
                bank = b.A.fill(pe, i)
                cols = slice(m * P, m * P + P)
                if layer == 0:
                    pe.matmul(bank, w0[:, cols], core.nh[:, u, :], start=True, stop=False)
                    mm = pe.matmul(bank, w0[:, cols], core.nl[:, u, :], start=False, stop=True)
                else:
                    for k in range(4):
                        w = w1[:, k * T + m * P:k * T + m * P + P]
                        pe.matmul(bank, w, hh[:, u, 0, k, :], start=k == 0, stop=False)
                        mm = pe.matmul(bank, w, hl[:, u, k, :], start=False, stop=k == 3)
                mm.then_inc(b.A.full, 1)
            pe.wait_ge(s_w, 3)
            for u in range(PAIR):
                pe.wait_ge(s_lo, 8 + 4 * u + 4)
                bank = b.D.fill(pe, ("y", u))
                for t in range(NT):
                    tok = slice(t * P, t * P + P)
                    for k in range(4):
                        w = w2[:, k * D:k * D + D]
                        pe.matmul(bank[:, tok], hh[:, u, 1, k, tok], w, start=k == 0, stop=False)
                        mm = pe.matmul(bank[:, tok], hl[:, u, k, tok], w, start=False, stop=k == 3)
                mm.then_inc(b.D.full, 1)

        @b.block.scalar
        def _(a):
            turn.scalar(a)
            a.wait_ge(s_s, 1)
            for i, (layer, u, m) in enumerate(units):
                bank = b.A.read(a, i)
                if i >= 3:
                    a.wait_ge(s_lo, i - 2)
                a.activation(r[:, i % 3, :], bank, ACT.Relu, scale=s2x[:, layer:layer + 1]).then_inc(b.A.free, 1)
                b.A.done(a, i)
                a.activation(hh[:, u, layer, m, :], r[:, i % 3, :], ACT.Copy).then_inc(s_hi, 1)

        @b.block.gpsimd
        def _(g):
            norm.gpsimd(g)
            g.wait_ge(s_ld, 48)
            s = b.sem("half")
            g.tensor_scalar(half[:, 0, :], k0[:, 0, :], 2.0, None, ALU.mult)
            g.tensor_scalar(half[:, 1, :], k0[:, 1, :], 2.0, None, ALU.mult).then_inc(s, 1)
            g.wait_ge(s, 1)
            g.tensor_tensor(w0[:, :], half[:, 0, :], half[:, 1, :], ALU.subtract).then_inc(s_w, 1)
            g.tensor_scalar(w1[:, :], k1[:, :], 2.0, 1.0, ALU.mult, ALU.subtract).then_inc(s_w, 1)
            g.tensor_scalar(w2[:, :], k2[:, :], 2.0, 1.0, ALU.mult, ALU.subtract).then_inc(s_w, 1)

        @b.block.vector
        def _(v):
            ch = Chain(v, b.sem("chain"))
            s, _ = COL["s"]
            v.tensor_scalar(s2x[:, 0:2], core.col[:, s:s + 2], 2.0, None, ALU.mult)
            v.tensor_tensor(s2x[:, 2:3], core.col[:, s + 2:s + 3], core.tg[:, 6:7], ALU.mult).then_inc(s_s, 1)
            norm.vector_stats(v, ch)
            norm.vector_apply(v)
            turn.vector(v)
            for i, (layer, u, m) in enumerate(units):
                v.wait_ge(s_hi, i + 1)
                if layer == 1 and m == 0:
                    b.A.read(v, 8 + 4 * u + 3)
                v.tensor_tensor(hl[:, u, m, :], r[:, i % 3, :], f32(hh[:, u, layer, m, :]), ALU.subtract)\
                    .then_inc(s_lo, 1)
            for u in range(PAIR):
                bank = b.D.read(v, ("y", u))
                x = core.toks(core.x, u).rearrange("p t d -> p (t d)")
                v.scalar_tensor_tensor(x, bank, s2x[:, 2:3], x, ALU.mult, ALU.add).then_inc(b.D.free, 1)

        @b.block.sync
        def _(sp):
            sp.dma_start(words[0][:, :, :], core.io["k0"].rearrange("h p n -> p h n")).then_inc(s_ld, 16)
            sp.dma_start(words[1][:, :], core.io["k1"]).then_inc(s_ld, 16)
            sp.dma_start(words[2][:, :], core.io["k2"]).then_inc(s_ld, 16)


def block_setup(core):
    nc, io = core.nc, core.io
    with ExitStack() as mem, Block(core, "setup") as b:
        sb = core.sb(mem, b.name + "_")
        raw = sb("raw", [P, N_STAGED])
        cst = sb("cst_all", [P, N_CST])
        sel = sb("sel_raw", [3 * E1, E1 // 2 * P])
        freq = sb("freq", [P, 2, D])
        at = sb("at", [P, 2, D])
        rep = sb("rep", [P, P])
        rep64 = sb("rep64", [NC, P])
        s_ld = b.sem("load")
        s_ones = b.sem("rep")
        s_pe = b.sem("pe")
        s_at = b.sem("at")
        s_th = b.sem("tanh")
        loads = 10
        R = lambda name: raw[:, SPLIT[name][0]:SPLIT[name][0] + SPLIT[name][1]]
        columns = [("a1q", "a1bx"), ("a1k", "a1by"), ("a1li2", "a1b3"), ("a2q", "a2bx"), ("a2li2", "a2b3")]
        bank = lambda i: core.psum[:, i, :]
        C = lambda name: cst[:, CST[name][0]:CST[name][0] + P]

        @b.block.sync
        def _(sp):
            for dst, name in ((raw, "wsplit"), (core.wf, "wf"), (core.w64, "w64"), (core.row, "row"), (core.col, "col"),
                              (cst, "cst"), (sel, "sel48")):
                sp.dma_start(dst[:, :], io[name]).then_inc(s_ld, 16)
            sp.dma_start(core.cst[:, :], io["cst"][:, 0:N_CST_KEPT]).then_inc(s_ld, 16)
            sp.dma_start(freq[:, 0, :], io["freq_re"]).then_inc(s_ld, 16)
            sp.dma_start(freq[:, 1, :], io["freq_im"]).then_inc(s_ld, 16)

        @b.block.gpsimd
        def _(g):
            g.memset(f32(core.qs[:, :, :, :]), 0.0)

        @b.block.tensor
        def _(pe):
            pe.wait_ge(s_ld, 16 * loads)
            k = 0
            for w, shift in columns:
                for m in range(4):
                    pe.matmul(bank(0)[:, k:k + 1], R(w)[:, m * P:m * P + P], core.Cc(shift), start=True, stop=True)
                    k += 1
            for m in range(4):
                mm = pe.matmul(bank(0)[:, k:k + 1], core.X("a2k", m * P, m * P + P), core.Cc("a2by", 0, NC),
                               start=True, stop=True)
                k += 1
            mm.then_inc(s_pe, 1)
            re, im = freq[:, 0, :], freq[:, 1, :]
            pe.matmul(bank(3)[:, 0:D], re, C("C"), start=True, stop=False)
            pe.matmul(bank(3)[:, 0:D], im, C("S"), start=False, stop=True)
            pe.matmul(bank(4)[:, 0:D], im, C("C"), start=True, stop=False)
            pe.matmul(bank(4)[:, 0:D], re, C("nS"), start=False, stop=True).then_inc(s_pe, 1)
            pe.wait_ge(s_ones, 1)
            pe.matmul(bank(1), rep[:, :], R("a1v"), start=True, stop=True)
            pe.matmul(bank(2)[:, :], rep64[:, :], core.X("a2v"), start=True, stop=True).then_inc(s_pe, 1)
            pe.wait_ge(s_at, 1)
            pe.matmul(bank(5)[:, 0:D], at[:, 0, :], C("Cn"), start=True, stop=False)
            pe.matmul(bank(5)[:, 0:D], at[:, 1, :], C("nSn"), start=False, stop=True).then_inc(s_pe, 1)

        @b.block.scalar
        def _(a):
            a.wait_ge(s_ld, 16 * loads)
            s, _ = COL["gx"]
            a.activation(core.tg[:, :], core.col[:, s:s + 8], ACT.Tanh).then_inc(s_th, 1)

        @b.block.vector
        def _(v):
            ch = Chain(v, b.sem("chain"))
            v.memset(core.ones2[:, :], 1.0)
            v.wait_ge(s_ld, 16 * loads)
            v.tensor_copy(core.identb[:, :], core.K("ident"))
            v.tensor_copy(core.sel48[:, :], sel[:, :])
            v.tensor_scalar(rep[:, :], C("ones128"), core.Cc("a1by"), None, ALU.mult)
            v.tensor_scalar(rep64[:, :], cst[0:NC, CST["ones128"][0]:CST["ones128"][0] + P], core.Cc("a2by", 0, NC), None,
                            ALU.mult).then_inc(s_ones, 1)
            v.wait_ge(s_pe, 2)
            v.tensor_copy(at[:, 0, :], bank(3)[:, 0:D])
            v.tensor_copy(at[:, 1, :], bank(4)[:, 0:D]).then_inc(s_at, 1)
            ch.link(v.tensor_copy(core.bias[:, :], bank(0)[:, 0:24]))
            for k, name in ((8, "a1li2b"), (16, "a2li2b")):
                s, w = COL[name]
                v.tensor_tensor(core.bias[:, k:k + 4], core.bias[:, k:k + 4], core.col[:, s:s + w], ALU.add)
            v.wait_ge(s_pe, 3)
            v.tensor_copy(core.vb1[:, :], bank(1))
            v.tensor_copy(core.vb2[:, :], bank(2))
            for w, gain in (("a1q", "a1gx"), ("a1k", "a1gy"), ("a1v", "a1gy"), ("a1li2", "a1g3"), ("a2q", "a2gx"),
                            ("a2li2", "a2g3")):
                last = v.tensor_scalar(R(w), R(w), core.Cc(gain), None, ALU.mult)
            s, _ = W64["a2k"]
            both = core.w64[:, s:s + 1024]
            last = v.tensor_scalar(both, both, core.Cc("a2gy", 0, NC), None, ALU.mult)
            ch.link(last)
            ch.link(v.tensor_copy(core.wh[:, 0:N_STAGED], raw[:, :]))
            v.tensor_tensor(core.wl[:, 0:N_STAGED], raw[:, :], f32(core.wh[:, 0:N_STAGED]), ALU.subtract)
            v.wait_ge(s_pe, 4)
            ch.link(v.tensor_copy(core.W("M", 1), bank(5)[:, 0:D]))
            v.tensor_tensor(core.W("M", 0), bank(5)[:, 0:D], f32(core.W("M", 1)), ALU.subtract)
            v.wait_ge(s_th, 1)
            for name, k in (("L0bo", 0), ("L3bo", 3), ("L3fb", 7)):
                v.tensor_scalar(core.R(name), core.R(name), core.tg[:, k:k + 1], None, ALU.mult)


def block_last(core, pair):
    with ExitStack() as mem, Block(core, "last") as b:
        norm = Norm(b, "norm", core.x, core.n)
        turn = Turn(b, "turn", norm)
        s_xb = b.sem("xb")
        s_out = b.sem("out")

        @b.block.tensor
        def _(pe):
            turn.tensor(pe)
            for u in range(PAIR):
                turn.ready(pe, u)
                bank = b.D.fill(pe, ("y", u))
                for i in range(NT):
                    mm = product_rows(pe, core, bank[:, i * P:i * P + P], "M", u, i)
                mm.then_inc(b.D.full, 1)

        @b.block.vector
        def _(v):
            ch = Chain(v, b.sem("chain"))
            norm.vector_stats(v, ch)
            norm.vector_apply(v)
            turn.vector(v)
            v.wait_ge(s_xb, 1)
            for u in range(PAIR):
                x = core.toks(core.x, u).rearrange("p t d -> p (t d)")
                bank = b.D.read(v, ("y", u))
                v.scalar_tensor_tensor(x, bank, core.tg[:, 7:8], x, ALU.mult, ALU.add).then_inc(b.D.free, 1)

        @b.block.scalar
        def _(a):
            turn.scalar(a)

        @b.block.gpsimd
        def _(g):
            norm.gpsimd(g)
            g.wait_ge(norm.s_n, PAIR)
            g.tensor_tensor(core.x[:, :, :], core.x[:, :, :], core.rows("L3fb", PAIR * NT), ALU.add).then_inc(s_xb, 1)

        @b.block.sync
        def _(sp):
            for u in range(PAIR):
                b.D.done(sp, ("y", u))
                sp.dma_start(core.io["out"][bass.ds(pair * PAIR + u, 1)].rearrange("b (t p) d -> p (b t) d", p=P),
                             core.toks(core.x, u)).then_inc(s_out, 16)
            sp.wait_ge(s_out, 16 * PAIR)


IN = ["x", "ctxT", "ctx", "wsplit", "wf", "w64", "row", "col", "cst", "sel48", "freq_re", "freq_im",
      "w1", "w2", "b2", "down", "k0", "k1", "k2"]


def build(nc, io):
    with ExitStack() as ctx:
        core = Core(nc, io, ctx)
        block_setup(core)
        with nc.Fori(0, B // PAIR) as pair:
            block_narrow(core, 0, pair, True)
            block_experts0(core)
            block_self(core)
            block_wide(core)
            block_experts1(core)
            block_single(core)
            block_signs(core)
            block_narrow(core, 3, pair, False)
            block_last(core, pair)


def packed(layout, width, parts, given):
    out = np.zeros((parts, width), np.float32)
    for name, (at, w) in layout.items():
        if name in given:
            a = given[name]
            out[:a.shape[0], at:at + w] = a
    return out


def constants():
    i = np.arange(P)
    turn = 2 * np.pi * ((i[:, None] * i[None, :]) % D) / D
    c, s = np.cos(turn), np.sin(turn)
    onesm = np.zeros((P, 4, 40))
    onesm[:, :, 0:8] = 1
    ksel = np.zeros((P, 4))
    for q in range(4):
        ksel[STK + 2 * q:STK + 2 * q + 2, q] = 1
    given = {"ident": np.eye(P), "mask": i[:, None] > i[None, :], "ones": np.ones((P, 32)), "ones128": np.ones((P, P)), "onesm": onesm.reshape(P, 160),
             "ksel": ksel, "iota": np.tile(np.arange(16), (P, 1)), "half": np.full((P, 8), -0.5),
             "C": c, "S": s, "nS": -s, "Cn": c / D, "nSn": -s / D}
    sel = np.zeros((3, E1, E1 // 2, 2, F1), np.float32)
    for e in range(E1):
        sel[:, e, e // 2, e % 2] = 1
    return packed(CST, N_CST, P, given), sel.reshape(3 * E1, E1 // 2 * P)


def arrays(i):
    tile = lambda a, n: a.reshape(n, P, -1).transpose(1, 0, 2).reshape(P, -1)
    heads = lambda a: a.transpose(1, 0, 2).reshape(a.shape[1], -1)
    cols = lambda a: a.reshape(-1, P).T
    words = lambda a: np.ascontiguousarray(a).view(np.uint32)
    a1, a2 = "L1_xattn_a1_", "L1_xattn_a2_"
    split = {"L0q": i["L0_xattn_Wq"], "L3q": i["L3_xattn_Wq"], "L2q": i["L2_xattn_Wq"], "g0": i["L0_ffn_gate_w"],
             "g1": i["L1_ffn_gate_w"].T, "a1q": heads(i[a1 + "wq"]), "a1k": heads(i[a1 + "wk"]),
             "a1v": heads(i[a1 + "wv"]), "a1li2": i[a1 + "li2_w"], "a2q": heads(i[a2 + "wq"]), "a2li2": i[a2 + "li2_w"],
             "eg": heads(i["L1_ffn_expert_gate"]), "sg": i["L1_ffn_shared_gate"],
             "eu": heads(i["L1_ffn_expert_up"]), "su": i["L1_ffn_shared_up"]}
    wf = {"L0o": i["L0_xattn_Wo"], "L3o": i["L3_xattn_Wo"], "a1li1": tile(i[a1 + "li1_w"], 4),
          "a1li3": tile(i[a1 + "li3_w"], 4), "a2li1": tile(i[a2 + "li1_w"], 4), "a2li3": tile(i[a2 + "li3_w"], 4)}
    w64 = {f"L{n}{k}": i[f"L{n}_xattn_W{k}"] for n in (0, 2, 3) for k in "kv"}
    w64 |= {"a2k": heads(i[a2 + "wk"]), "a2v": heads(i[a2 + "wv"])}
    rows = {"L0bv": "L0_xattn_bv", "L2bv": "L2_xattn_bv", "L3bv": "L3_xattn_bv", "L0bo": "L0_xattn_bo",
            "L3bo": "L3_xattn_bo", "L3fb": "L3_ffn_bias", "a1li1b": a1 + "li1_b", "a1li3b": a1 + "li3_b",
            "a2li1b": a2 + "li1_b", "a2li3b": a2 + "li3_b", "ln1g": "L1_xattn_ln1_g", "ln1b": "L1_xattn_ln1_b",
            "ln2g": "L1_xattn_ln2_g", "ln2b": "L1_xattn_ln2_b"}
    row = {k: np.broadcast_to(i[v], (P, D)) for k, v in rows.items()}
    col = {f"L{n}b{k}": cols(i[f"L{n}_xattn_b{k}"]) for n in (0, 2, 3) for k in "qk"}
    for a, full in (("a1", a1), ("a2", a2)):
        for short, long in (("gx", "lnx_g"), ("bx", "lnx_b"), ("gy", "lny_g"), ("by", "lny_b"), ("g3", "ln3_g"),
                            ("b3", "ln3_b")):
            col[a + short] = i[full + long].reshape(-1, 1)
        col[a + "li2b"] = cols(i[full + "li2_b"])
    col["b1"] = cols(i["L0_ffn_dense_1_b"].reshape(E0, F0, 2).transpose(0, 2, 1).reshape(-1))
    col["gx"] = np.broadcast_to(i["g_xattn"], (P, 4))
    col["gf"] = np.broadcast_to(i["g_ffn"], (P, 4))
    col["s"] = np.broadcast_to(np.stack([i["L2_ffn_s0"], i["L2_ffn_s1"], i["L2_ffn_s2"]]), (P, 3))
    ctxT = np.zeros((NC, B, NKE), np.float32)
    ctxT[:, :, :NK] = i["ctx_512"].transpose(2, 0, 1)
    cst, sel = constants()
    return {
        "x": i["x"], "ctxT": ctxT, "ctx": i["ctx_512"],
        "wsplit": packed(SPLIT, N_STAGED, P, split), "wf": packed(WF, N_WF, P, wf), "w64": packed(W64, N_W64, NC, w64),
        "row": packed(ROW, N_ROW, P, row), "col": packed(COL, N_COL, P, col), "cst": cst, "sel48": sel,
        "freq_re": i["L3_ffn_w_freq_real"], "freq_im": i["L3_ffn_w_freq_imag"],
        "w1": i["L0_ffn_dense_1_w"].reshape(E0, F0, 2, D).transpose(3, 0, 2, 1).reshape(D, -1),
        "w2": i["L0_ffn_dense_2_w"].transpose(0, 2, 1).reshape(E0 * F0 // P, P, D).transpose(1, 0, 2),
        "b2": i["L0_ffn_dense_2_b"],
        "down": np.concatenate([i["L1_ffn_expert_down"].reshape(E1 * F1, D), i["L1_ffn_shared_down"]])
        .reshape(-1, P, D).transpose(1, 0, 2),
        "k0": words(i["L2_ffn_k0"].reshape(2, P, 512)), "k1": words(tile(i["L2_ffn_k1"], 4)),
        "k2": words(tile(i["L2_ffn_k2"], 4)),
    }


def kernel(**inputs):
    from concourse import bacc
    from concourse.bass_utils import run_bass_kernel_spmd

    given = arrays({k: np.asarray(v) for k, v in inputs.items()})
    nc = bacc.Bacc("TRN2", target_bir_lowering=False, num_devices=1)
    feed, io = {}, {}
    for name in IN:
        a = np.ascontiguousarray(given[name])
        feed["in_" + name] = a
        io[name] = nc.dram_tensor("in_" + name, a.shape, mybir.dt.from_np(a.dtype), kind="ExternalInput").ap()
    io["out"] = nc.dram_tensor("out_x", (B, T, D), F32, kind="ExternalOutput").ap()
    build(nc, io)
    r = run_bass_kernel_spmd(nc, [feed], core_ids=[0])
    return r.results[0]["out_x"]
```

```python
from contextlib import ExitStack

import numpy as np

import concourse.bass as bass
from concourse import mybir

F32 = mybir.dt.float32
F32R = mybir.dt.float32r
BF16 = mybir.dt.bfloat16
U32 = mybir.dt.uint32
U8 = mybir.dt.uint8
ALU = mybir.AluOpType
ACT = mybir.ActivationFunctionType
AX = mybir.AxisListType.X

P = 128
B, T, D = 4, 512, 128
NT = T // P
PAIR = 2
NK, NKE = 77, 78
NC = 64
H = 16
DH = 32
KSLOT = 80
STK = 96
STKM = STK + 8
E0, F0 = 8, 256
E1, F1 = 16, 64
EPS = 1e-5



def _layout(items):
    out, at = {}, 0
    for name, width in items:
        out[name] = (at, width)
        at += width
    return out, at


SPLIT, N_SPLIT = _layout([
    ("L0q", 128), ("L3q", 128), ("L2q", 128), ("g0", E0), ("g1", E1),
    ("a1q", 512), ("a1k", 512), ("a1v", 512), ("a1li2", 512), ("a2q", 512), ("a2li2", 512),
    ("eg", 1024), ("sg", 128), ("eu", 1024), ("su", 128), ("M", 128)])
N_STAGED = SPLIT["M"][0]
WF, N_WF = _layout([("L0o", 128), ("L3o", 128), ("a1li1", 512), ("a1li3", 512), ("a2li1", 512), ("a2li3", 512)])
W64, N_W64 = _layout([("L0k", 128), ("L0v", 128), ("L2k", 128), ("L2v", 128), ("L3k", 128), ("L3v", 128),
                      ("a2k", 512), ("a2v", 512)])
ROW, N_ROW = _layout([(n, 128) for n in (
    "L0bv", "L2bv", "L3bv", "L0bo", "L3bo", "L3fb", "a1li1b", "a1li3b", "a2li1b", "a2li3b",
    "ln1g", "ln1b", "ln2g", "ln2b")])
COL, N_COL = _layout([
    ("L0bq", 1), ("L0bk", 1), ("L2bq", 1), ("L2bk", 1), ("L3bq", 1), ("L3bk", 1),
    ("a1gx", 1), ("a1bx", 1), ("a1gy", 1), ("a1by", 1), ("a1g3", 1), ("a1b3", 1), ("a1li2b", 4),
    ("a2gx", 1), ("a2bx", 1), ("a2gy", 1), ("a2by", 1), ("a2g3", 1), ("a2b3", 1), ("a2li2b", 4),
    ("b1", 4 * E0), ("gx", 4), ("gf", 4), ("s", 3)])
CST, N_CST = _layout([
    ("ident", 128), ("mask", 128), ("ones", 32), ("onesm", 160), ("ksel", 4), ("kblock", 4), ("iota", 16), ("half", 8),
    ("C", 128), ("ones128", 128), ("S", 128), ("nS", 128), ("Cn", 128), ("nSn", 128)])
N_CST_KEPT = CST["C"][0]


class Ring:

    def __init__(self, banks, full, free):
        self.banks, self.full, self.free = banks, full, free
        self.n, self.number = 0, {}

    def fill(self, pe, name):
        n = self.number[name] = self.n
        self.n += 1
        if n >= len(self.banks):
            pe.wait_ge(self.free, n - len(self.banks) + 1)
        return self.banks[n % len(self.banks)]

    def read(self, eng, name):
        n = self.number[name]
        eng.wait_ge(self.full, n + 1)
        return self.banks[n % len(self.banks)]

    def done(self, eng, name):
        eng.wait_ge(self.free, self.number[name] + 1)


class Chain:

    def __init__(self, eng, sem):
        self.eng, self.sem, self.n = eng, sem, 0

    def link(self, ins):
        ins.then_inc(self.sem, 1)
        self.n += 1
        self.eng.wait_ge(self.sem, self.n)


def f32(ap):
    return ap.bitcast(F32)


class Core:

    def __init__(self, nc, io, ctx):
        self.nc, self.io = nc, io
        self.ctx = ctx
        self.psum = ctx.enter_context(nc.psum_tensor("banks", [P, 8, T], F32))
        sb = self.sb(ctx)
        self.x = sb("x_res", [P, PAIR * NT, D])
        self.n = sb("x_norm", [P, PAIR * NT, D])
        self.nh = sb("normT_hi", [P, PAIR, T], F32R)
        self.nl = sb("normT_lo", [P, PAIR, T], F32R)
        self.wh = sb("w_hi", [P, N_SPLIT], F32R)
        self.wl = sb("w_lo", [P, N_SPLIT], F32R)
        self.wf = sb("w_f32", [P, N_WF])
        self.w64 = sb("w_ctx", [NC, N_W64])
        self.row = sb("rows", [P, N_ROW])
        self.col = sb("cols", [P, N_COL])
        self.cst = sb("consts", [P, N_CST_KEPT])
        self.identb = sb("ident_bf", [P, P], BF16)
        self.ones2 = sb("ones2_bf", [2, NKE], BF16)
        self.sel48 = sb("sel48_bf", [3 * E1, E1 // 2 * P], BF16)
        self.ctxp = sb("ctxT_pair", [NC, PAIR, NKE])
        self.ctxn = sb("ctxT_norm", [NC, PAIR, NKE])
        self.tg = sb("tanh_g", [P, 8])
        self.bias = sb("proj_bias", [P, 24])
        self.vb1 = sb("a1_vbias", [P, 512])
        self.vb2 = sb("a2_vbias", [P, 512])
        self.qs = sb("q_stack", [P, 3, 4, T], F32R)
        self.x1 = sb("x_inner", [P, PAIR * NT, D])
        self.st = sb("bn_stats", [P, PAIR * NT, 6])
        self.mv = sb("mean_var", [P, PAIR * NT, 2])
        self.ve = sb("var_eps", [P, PAIR * NT])
        self.rstd = sb("rstd", [P, PAIR * NT])
        self.qkd = nc.dram_tensor("qk_scratch", (PAIR, 2, 4, 2, P, T), F32).ap()
        self.kd = nc.dram_tensor("k_scratch", (PAIR, 2, 1, P, NKE), F32).ap()
        self.kw = nc.dram_tensor("k_scratch_wide", (PAIR, 2, DH, H, NKE), F32).ap()

    def sb(self, ctx, prefix=""):
        nc = self.nc
        return lambda name, shape, dt=F32: ctx.enter_context(nc.sbuf_tensor(prefix + name, shape, dt))

    def W(self, name, hi, a=0, b=None):
        s, w = SPLIT[name]
        return (self.wh if hi else self.wl)[:, s + a:s + (w if b is None else b)]

    def F(self, name, a=0, b=None):
        s, w = WF[name]
        return self.wf[:, s + a:s + (w if b is None else b)]

    def X(self, name, a=0, b=None):
        s, w = W64[name]
        return self.w64[:, s + a:s + (w if b is None else b)]

    def R(self, name):
        s, w = ROW[name]
        return self.row[:, s:s + w]

    def rows(self, name, n):
        s, w = ROW[name]
        return self.row[:, s:s + w].unsqueeze(1).to_broadcast([P, n, w])

    def Cc(self, name, k=0, p=P):
        s, _ = COL[name]
        return self.col[0:p, s + k:s + k + 1]

    def K(self, name, a=0, b=None, p=P):
        s, w = CST[name]
        return self.cst[0:p, s + a:s + (w if b is None else b)]

    def toks(self, t, u):
        return t[:, NT * u:NT * u + NT, :]


class Block:

    def __init__(self, core, name, attention=False):
        self.core, self.name, self.nc, self.attention = core, name, core.nc, attention

    def __enter__(self):
        self.stack = ExitStack()
        self.sems = []
        bk = self.core.psum
        one = lambda i: bk[:, i, :]
        self.A = Ring([one(0), one(1)], self.sem("A_full"), self.sem("A_free"))
        self.D = Ring([one(2), one(3)], self.sem("D_full"), self.sem("D_free"))
        self.O = Ring([one(4), one(6)], self.sem("O_full"), self.sem("O_free"))
        if self.attention:
            self.S = Ring([one(5)], self.sem("S_full"), self.sem("S_free"))
            self.N = Ring([one(7)], self.sem("N_full"), self.sem("N_free"))
        else:
            self.S = Ring([one(5), one(7)], self.sem("S_full"), self.sem("S_free"))
        self.block = self.stack.enter_context(self.nc.Block())
        return self

    def sem(self, name):
        s = self.stack.enter_context(self.nc.semaphore(f"{self.name}_{name}"))
        self.sems.append(s.num)
        return s

    def __exit__(self, *_):
        self.stack.close()
        self.nc.all_engine_barrier(sems_to_clear=range(min(self.sems), max(self.sems) + 1))
        return False


class Norm:

    def __init__(self, b, name, src, dst, parts=P, tiles=PAIR * NT):
        self.core, self.src, self.dst = b.core, src, dst
        self.parts, self.each = parts, tiles // PAIR
        self.s_st = b.sem(name + "_st")
        self.s_mv = b.sem(name + "_mv")
        self.s_var = b.sem(name + "_var")
        self.s_rstd = b.sem(name + "_rstd")
        self.s_n = b.sem(name + "_n")

    def tiles(self, u):
        return range(self.each * u, self.each * (u + 1))

    def sums(self, v, u):
        for t in self.tiles(u):
            ins = v.bn_stats(self.core.st[0:self.parts, t, :], self.src[:, t, :])
        ins.then_inc(self.s_st, 1)

    def means(self, v, u):
        c, p = self.core, self.parts
        v.wait_ge(self.s_st, u + 1)
        for t in self.tiles(u):
            ins = v.bn_aggr(c.mv[0:p, t, :], c.st[0:p, t, :])
        ins.then_inc(self.s_mv, 1)

    def variances(self, v, u):
        c, p = self.core, self.parts
        a = slice(self.each * u, self.each * (u + 1))
        v.wait_ge(self.s_mv, u + 1)
        v.tensor_scalar(c.ve[0:p, a], c.mv[0:p, a, 1], EPS, None, ALU.add).then_inc(self.s_var, 1)

    def vector_stats(self, v, after=None, us=range(PAIR)):
        for u in us:
            if after:
                v.wait_ge(after.s_n, u + 1)
            self.sums(v, u)
        for u in us:
            self.means(v, u)
        for u in us:
            self.variances(v, u)

    def gpsimd(self, g, us=range(PAIR)):
        c, p = self.core, self.parts
        for u in us:
            a = slice(self.each * u, self.each * (u + 1))
            g.wait_ge(self.s_var, u + 1)
            g.tensor_tensor(c.rstd[0:p, a], c.ve[0:p, a], c.K("half", 0, self.each, p), ALU.pow).then_inc(self.s_rstd, 1)

    def vector_apply(self, v, us=range(PAIR)):
        c, p = self.core, self.parts
        for u in us:
            v.wait_ge(self.s_rstd, u + 1)
            for t in self.tiles(u):
                ins = v.tensor_scalar(self.dst[:, t, :], self.src[:, t, :], c.mv[0:p, t, 0:1], c.rstd[0:p, t:t + 1],
                                      ALU.subtract, ALU.mult)
            ins.then_inc(self.s_n, 1)


class Turn:

    def __init__(self, b, name, norm):
        self.b, self.core, self.name, self.norm = b, b.core, name, norm
        self.s_hi = b.sem(name + "_hi")

    def tensor(self, pe, us=range(PAIR)):
        for u in us:
            pe.wait_ge(self.norm.s_n, u + 1)
            bank = self.b.D.fill(pe, (self.name, u))
            for t in range(NT):
                mm = pe.transpose(bank[:, t * P:(t + 1) * P], self.core.n[:, NT * u + t, :], self.core.K("ident"))
            mm.then_inc(self.b.D.full, 1)

    def scalar(self, a, us=range(PAIR)):
        for u in us:
            bank = self.b.D.read(a, (self.name, u))
            a.activation(self.core.nh[:, u, :], bank, ACT.Copy).then_inc(self.s_hi, 1)

    def vector(self, v, us=range(PAIR)):
        for u in us:
            bank = self.b.D.read(v, (self.name, u))
            v.wait_ge(self.s_hi, u + 1)
            v.tensor_tensor(self.core.nl[:, u, :], bank, f32(self.core.nh[:, u, :]), ALU.subtract)\
                .then_inc(self.b.D.free, 1)

    def ready(self, pe, u):
        self.b.D.done(pe, (self.name, u))


def product(pe, core, out, w, u, a=0, b=None):
    pe.matmul(out, core.W(w, 1, a, b), core.nh[:, u, :], start=True, stop=False)
    pe.matmul(out, core.W(w, 1, a, b), core.nl[:, u, :], start=False, stop=False)
    return pe.matmul(out, core.W(w, 0, a, b), core.nh[:, u, :], start=False, stop=True)


def product_rows(pe, core, out, w, u, t, a=0, b=None):
    tok = slice(t * P, (t + 1) * P)
    pe.matmul(out, core.nh[:, u, tok], core.W(w, 1, a, b), start=True, stop=False)
    pe.matmul(out, core.nl[:, u, tok], core.W(w, 1, a, b), start=False, stop=False)
    return pe.matmul(out, core.nh[:, u, tok], core.W(w, 0, a, b), start=False, stop=True)


class Attention:

    def __init__(self, b, name, kind, t, scale, wq, bq, wk, bk):
        self.b, self.core, self.name, self.kind, self.t, self.scale = b, b.core, name, kind, t, scale
        self.wq, self.bq, self.wk, self.bk = wq, bq, wk, bk
        self.own = kind == "self"
        self.narrow = kind == "narrow"
        self.wide = kind == "wide"
        self.nkt = NT if self.own else 1
        self.keys = P if self.own else NK
        self.slots = 3 if self.own else 8 if self.narrow else 4
        self.steps = [(u, m) for u in range(PAIR) for m in range(4)]
        self.units = len(self.steps) * self.nkt
        self.tiles = 1 if self.narrow else 4
        self.out_unit = 4 * self.nkt + (3 if self.own else 2)
        self.items = [(u, kind, m) for u in range(PAIR) for m in range(self.tiles) for kind in (0, 1)]
        if not self.own:
            self.items.sort(key=lambda item: -item[1])
        self.s_hi = b.sem("a_hi")
        self.s_out = [b.sem(f"a_out{i}") for i in range(4)]
        self.s_kout = b.sem("a_kout")
        self.s_q = [b.sem(f"a_q{i}") for i in range(self.slots)]
        self.s_k = [b.sem(f"a_k{u}") for u in range(PAIR)]
        self.s_kb = b.sem("a_kb")
        self.s_nm = b.sem("a_nm")
        self.s_mr = b.sem("a_mr")
        self.s_pm = b.sem("a_pm")
        self.s_pv = b.sem("a_pv")
        self.s_rs = b.sem("a_rs")
        self.s_nw = b.sem("a_nw")

    def last_of_unit(self, i):
        n, kt = divmod(i, self.nkt)
        return kt == self.nkt - 1 and (not self.narrow or self.steps[n][1] == 3)

    def sums(self, n):
        u, m = self.steps[n]
        return (self.name, "sum", u) if self.narrow else (self.name, "sum", u, m)

    def wait_pv(self, eng, i):
        if self.last_of_unit(i):
            self.b.O.read(eng, self.sums(i // self.nkt))
        else:
            eng.wait_ge(self.s_pv, sum(not self.last_of_unit(j) for j in range(i + 1)))

    def head(self, m, lane):
        return 4 * lane + m if self.narrow else 4 * m + lane

    def n_keys(self, kind):
        return T if (self.own or not kind) else NKE

    def q(self, n):
        slot = n % self.slots
        if self.narrow:
            return self.core.qs[:, slot // 4, slot % 4, :].unsqueeze(1)
        return self.core.qs[:, slot, :, :] if slot < 3 else self.t.q4[:, :, :]

    def ring(self, j):
        return (self.b.D, self.b.A)[j % 2]

    def staged(self, j, part):
        return self.t.stage[:, part, j % 4, 0:self.n_keys(self.items[j][1])]

    def of(self, u, kinds):
        return [(j, item) for j, item in enumerate(self.items) if item[0] == u and item[1] in kinds]

    @property
    def late(self):
        return (0, 1) if self.own else (0,)

    def staging_done(self, eng, n_items):
        if self.wide:
            eng.wait_ge(self.s_kout, 32 * min(n_items // 4, PAIR))
            n_items -= 4 * PAIR
        for i in range(4):
            k = len(range(i, n_items, 4))
            if k:
                eng.wait_ge(self.s_out[i], 32 * k)

    def slot_free(self, eng, j):
        if self.wide and 4 <= j < 4 + 4 * PAIR:
            eng.wait_ge(self.s_kout, 32 * (j // 4))
        elif j >= 4:
            eng.wait_ge(self.s_out[j % 4], 32 * ((j // 4) - (PAIR if self.wide else 0)))

    def tensor_project(self, pe, u, kinds):
        c = self.core
        for j, (_, kind, m) in self.of(u, kinds):
            ring = self.ring(j)
            bank = ring.fill(pe, (self.name, "p", j))
            cols = (m * P, m * P + P)
            if kind == 0 or self.own:
                mm = product(pe, c, bank, self.wk if kind else self.wq, u, *cols)
            else:
                mm = pe.matmul(bank[:, 0:NKE], c.X(self.wk, *cols), self.t.ctx[:, u, :], start=True, stop=True)
            mm.then_inc(ring.full, 1)

    def query_item(self, u):
        return self.items.index((u, 0, 0))

    def key_blocks(self, eng, ready):
        s, _ = CST["kblock"]
        for u in range(PAIR):
            eng.wait_ge(self.s_k[u], 16 * 3)
            out = self.t.ks[0:STKM, u, :, :].rearrange("p (q m) n -> p q m n", q=4)
            for q in range(4):
                ins = eng.tensor_scalar(out[:, q], f32(self.t.kc[0:STKM, u, :, :]), self.core.cst[0:STKM, s + q:s + q + 1],
                                        None, ALU.mult)
            ins.then_inc(ready, 1)

    def staged_all(self, pe, u):
        j, _ = self.of(u, self.late)[-1]
        self.ring(j).done(pe, (self.name, "p", j))
        self.ring(j - 1).done(pe, (self.name, "p", j - 1))

    def scalar_project(self, a, u, kinds):
        for j, (_, kind, m) in self.of(u, kinds):
            bank = self.ring(j).read(a, (self.name, "p", j))
            w = self.n_keys(kind)
            self.slot_free(a, j)
            a.activation(self.staged(j, 0).bitcast(F32R), bank[:, 0:w], ACT.Identity,
                         bias=(self.bk if kind else self.bq)(m)).then_inc(self.s_hi, 1)

    def vector_project(self, v, u, kinds):
        for j, (_, kind, m) in self.of(u, kinds):
            ring = self.ring(j)
            bank = ring.read(v, (self.name, "p", j))
            w = self.n_keys(kind)
            v.wait_ge(self.s_hi, j + 1)
            self.slot_free(v, j)
            v.scalar_tensor_tensor(self.staged(j, 1).bitcast(F32R), bank[:, 0:w], (self.bk if kind else self.bq)(m),
                                   self.staged(j, 0), ALU.add, ALU.subtract).then_inc(ring.free, 1)

    def sync_project(self, sp, u, kinds):
        c = self.core
        for j, (_, kind, m) in self.of(u, kinds):
            self.ring(j).done(sp, (self.name, "p", j))
            if self.wide and kind:
                if m == 3:
                    for part in range(2):
                        sp.dma_start(c.kw[u, part].rearrange("d (m q) n -> q d m n", q=4),
                                     self.t.stage[:, part, :, 0:NKE]).then_inc(self.s_kout, 16)
                continue
            for part in range(2):
                dst = c.qkd[u, kind, m, part] if (self.own or not kind) else c.kd[u, part, m]
                sp.dma_start(dst, self.staged(j, part)).then_inc(self.s_out[j % 4], 16)
            if u == 0 and m >= 1 and kind == kinds[-1] and 0 in kinds:
                self.staging_done(sp, j + 1 - len(kinds))
                self.sync_stacks(sp, [m - 1])
        self.staging_done(sp, j + 1)

    def sync_keys(self, sp, u):
        c = self.core
        for g, part in enumerate((0, 1, 0)):
            if self.narrow:
                dst, src = self.t.kc[32 * g:32 * g + 32, u, :, :], c.kd[u, part, 0].rearrange("(m r) n -> r m n", m=4)
            else:
                dst = self.t.ks[32 * g:32 * g + 32, u, :, :]
                src = c.kw[u, part]
            sp.dma_start(f32(dst), src).then_inc(self.s_k[u], 16)

    def sync_stacks(self, sp, steps):
        c = self.core
        for n in steps:
            u, m = self.steps[n]
            if n >= self.slots:
                self.b.A.read(sp, (self.name, "st", n - self.slots, self.nkt - 1, 3))
            for kind in range(2 if self.own else 1):
                for g, part in enumerate((0, 1, 0) if kind else (0, 0, 1)):
                    if self.narrow:
                        src = self.staged(self.query_item(u), part)[32 * m:32 * m + 32]
                        dst = self.q(n)[32 * g:32 * g + 32, 0, :]
                    else:
                        src = c.qkd[u, kind, m, part].rearrange("(q d) n -> d q n", q=4)
                        dst = (self.t.ks[:, n % 3, :, :] if kind else self.q(n))[32 * g:32 * g + 32]
                    sp.dma_start(f32(dst), src).then_inc(self.s_q[n % self.slots], 16)

    def sync(self, sp, ones):
        if not self.own:
            for u in range(PAIR):
                self.sync_project(sp, u, (1,))
            if not self.narrow:
                ones(sp)
            for u in range(PAIR if self.narrow else 1):
                self.sync_keys(sp, u)
        else:
            ones(sp)
        if self.narrow:
            for u in range(PAIR):
                j = self.query_item(u)
                self.ring(j).done(sp, (self.name, "p", j))
                self.sync_stacks(sp, range(4 * u, 4 * u + 4))
            return
        for u in range(PAIR):
            self.sync_project(sp, u, self.late)
            if u == 0:
                self.sync_stacks(sp, range(self.tiles - 1, self.slots))
                if not self.own:
                    self.sync_keys(sp, 1)
        self.sync_stacks(sp, range(self.slots, len(self.steps)))

    def key_stack(self, n, lane, rows, cols):
        u, m = self.steps[n]
        if self.own:
            return self.t.ks[0:rows, n % 3, lane, cols]
        return self.t.ks[0:rows, u, self.head(m, lane), cols]

    def scores(self, n):
        if n > 7:
            return []
        return [(n, t, lane) for t in range(NT) for lane in (range(4) if self.own else (None,))]

    def tensor_scores(self, pe, piece):
        n, t, lane = piece
        u, m = self.steps[n]
        tok = slice(t * P, (t + 1) * P)
        if t == 0 and not lane:
            pe.wait_ge(self.s_q[n % self.slots], 16 * (6 if self.own else 3) * (n // self.slots + 1))
            if m == 0 and self.narrow:
                pe.wait_ge(self.s_kb, u + 1)
            elif m == 0 and not self.own:
                pe.wait_ge(self.s_k[u], 16 * 3)
        bank = self.b.D.fill(pe, (self.name, "s", piece))
        if self.own:
            mm = pe.matmul(bank, self.q(n)[0:STK, lane, tok], self.key_stack(n, lane, STK, slice(0, T)),
                           start=True, stop=True)
        elif self.narrow:
            keys = self.t.ks[0:STK, u, :, :].rearrange("p (q m) n -> p m q n", q=4)[:, m]
            mm = pe.matmul(bank[:, 0:4 * NKE], self.q(n)[0:STK, 0, tok], keys, start=True, stop=True)
        else:
            for q in range(4):
                mm = pe.matmul(bank[:, KSLOT * q:KSLOT * q + NKE], self.q(n)[0:STK, q, tok],
                               self.key_stack(n, q, STK, slice(0, NKE)), start=True, stop=True)
        mm.then_inc(self.b.D.full, 1)

    def vector_max(self, v, piece):
        n, t, lane = piece
        bank = self.b.D.read(v, (self.name, "s", piece))
        if self.own:
            ins = v.tensor_reduce(self.t.mx[:, n % 2, t, lane:lane + 1], bank, AX, ALU.max)
        else:
            each = NKE if self.narrow else KSLOT
            ins = v.tensor_reduce(self.t.mx[:, n % 2, t, :], bank[:, 0:4 * each].rearrange("p (q k) -> p q k", q=4)[:, :, 0:NK],
                                  AX, ALU.max)
        ins.then_inc(self.b.D.free, 1)

    def vector_negate(self, v, ch, n):
        self.b.D.done(v, (self.name, "s", self.scores(n)[-1]))
        hi, lo = self.t.nm[:, :, :, 0], self.t.nm[:, :, :, 1]
        if n >= 1:
            self.b.N.read(v, (self.name, "nm", n - 1))
        ch.link(v.tensor_scalar(hi, self.t.mx[:, n % 2, :, :], -1.0, None, ALU.mult))
        v.scalar_tensor_tensor(lo, self.t.mx[:, n % 2, :, :], -1.0, hi, ALU.mult, ALU.subtract).then_inc(self.s_nm, 1)

    def tensor_turn_max(self, pe, n):
        c = self.core
        if n > 7:
            return
        pe.wait_ge(self.s_nm, n + 1)
        bank = self.b.N.fill(pe, (self.name, "nm", n)).bitcast(BF16)
        for t in range(NT):
            mm = pe.transpose(bank[STK:STKM, t * P:(t + 1) * P], self.t.nm[:, t, :, :].rearrange("p q e -> p (q e)"),
                              c.identb[:, :])
        mm.then_inc(self.b.N.full, 1)

    def scalar_max(self, a, n):
        if n <= 7:
            bank = self.b.N.read(a, (self.name, "nm", n)).bitcast(BF16)
            a.activation(self.q(n)[STK:STKM, 0, :], bank[STK:STKM, 0:T], ACT.Copy).then_inc(self.b.N.free, 1)

    def vector_max_rows(self, v, n):
        if n <= 7 and not self.narrow:
            self.b.N.done(v, (self.name, "nm", n))
            rows = self.q(n)[STK:STKM]
            for lane in range(1, 4):
                ins = v.tensor_copy(rows[:, lane, :], f32(rows[:, 0, :]))
            ins.then_inc(self.s_mr, 1)

    def tensor_exps(self, pe, i, lane):
        n, kt = divmod(i, self.nkt)
        if kt == 0 and lane == 0:
            if self.narrow:
                self.b.N.done(pe, (self.name, "nm", n))
            else:
                pe.wait_ge(self.s_mr, n + 1)
        bank = self.b.A.fill(pe, (self.name, "st", n, kt, lane))
        cols = slice(kt * P, kt * P + self.keys)
        pe.matmul(bank[0:self.keys, :], self.key_stack(n, lane, STKM, cols), self.q(n)[0:STKM, 0 if self.narrow else lane, :],
                  start=True, stop=True).then_inc(self.b.A.full, 1)

    def scalar_exps(self, a, i, lane):
        n, kt = divmod(i, self.nkt)
        if i >= 3 and lane == 0:
            self.wait_pv(a, i - 3)
            if self.own:
                a.wait_ge(self.s_pm, i - 2)
        bank = self.b.A.read(a, (self.name, "st", n, kt, lane))
        a.activation(self.t.p[0:self.keys, i % 3, lane, :], bank[0:self.keys, :], ACT.Exp, scale=self.scale)\
            .then_inc(self.b.A.free, 1)

    def gpsimd(self, g):
        for i in range(self.units):
            n, kt = divmod(i, self.nkt)
            if i and self.last_of_unit(i - 1):
                if not self.own:
                    self.newton(g, (i - 1) // self.nkt)
            if not self.own:
                continue
            if kt == 1 and n:
                self.newton(g, n - 1)
            self.b.A.done(g, (self.name, "st", n, kt, 3))
            if i >= 2:
                self.wait_pv(g, i - 2)
            g.tensor_tensor(self.t.pm[:, i % 2, :, :], self.t.p[:, i % 3, :, kt * P:(kt + 1) * P],
                            self.core.K("mask").unsqueeze(1).to_broadcast([P, 4, P]), ALU.mult).then_inc(self.s_pm, 1)

    def first_of_sums(self, i):
        n, kt = divmod(i, self.nkt)
        return kt == 0 and (not self.narrow or self.steps[n][1] == 0)

    def lanes(self, pe, i, bank, stationary, moving, cols, start):
        for q in range(4):
            mm = pe.matmul(bank[32 * q:32 * q + 32, cols], stationary(q), moving(q), start=start,
                           stop=self.last_of_unit(i), skip_group_check=True)
        return mm

    def tensor_sums(self, pe, i):
        n, kt = divmod(i, self.nkt)
        m = self.steps[n][1]
        first = self.first_of_sums(i)
        if first:
            self.sbank = self.b.S.fill(pe, self.sums(n))
        self.b.A.done(pe, (self.name, "st", n, kt, 3))
        ones = self.core.K("onesm", 32 * m, 32 * m + 32) if self.narrow else self.core.K("ones", 0, 32)
        mm = self.lanes(pe, i, self.sbank, lambda q: ones, lambda q: self.t.p[:, i % 3, q, :], slice(0, T), first)
        if self.last_of_unit(i):
            mm.then_inc(self.b.S.full, 1)

    def tensor_values(self, pe, i):
        n, kt = divmod(i, self.nkt)
        u, m = self.steps[n]
        first = self.first_of_sums(i)
        if first:
            self.obank = self.b.O.fill(pe, self.sums(n))
        v = lambda q: self.t.v(u, kt, m, q)
        if self.own:
            pe.wait_ge(self.s_pm, i + 1)
            mm = self.lanes(pe, i, self.obank, v, lambda q: self.t.pm[:, i % 2, q, :], slice(kt * P, kt * P + P), first)
            if kt:
                mm = self.lanes(pe, i, self.obank, v, lambda q: self.t.p[:, i % 3, q, 0:kt * P], slice(0, kt * P), False)
        else:
            mm = self.lanes(pe, i, self.obank, v, lambda q: self.t.p[:, i % 3, q, :], slice(0, T), first)
        mm.then_inc(self.b.O.full if self.last_of_unit(i) else self.s_pv, 1)

    def scalar_inverse(self, a, n):
        key = self.sums(n)
        k = self.b.S.number[key]
        bank = self.b.S.read(a, key)
        if k:
            a.wait_ge(self.b.O.free, k)
        a.activation(self.t.sm[:, :], bank, ACT.Copy)
        a.activation(self.t.rs[:, :], bank, ACT.Ln).then_inc(self.b.S.free, 1)
        a.wait_ge(self.b.S.free, k + 1)
        a.activation(self.t.rs[:, :], self.t.rs[:, :], ACT.Exp, scale=-1.0).then_inc(self.s_rs, 1)

    def newton(self, eng, n):
        k = self.b.S.number[self.sums(n)]
        sm, rs = self.t.sm[:, :], self.t.rs[:, :]
        eng.wait_ge(self.s_rs, k + 1)
        eng.tensor_tensor(sm, sm, rs, ALU.mult).then_inc(self.s_nw, 1)
        eng.wait_ge(self.s_nw, 3 * k + 1)
        eng.tensor_scalar(sm, sm, -1.0, 2.0, ALU.mult, ALU.add).then_inc(self.s_nw, 1)
        eng.wait_ge(self.s_nw, 3 * k + 2)
        eng.tensor_tensor(sm, sm, rs, ALU.mult).then_inc(self.s_nw, 1)

    def vector_divide(self, v, n):
        key = self.sums(n)
        if n == len(self.steps) - 1:
            self.newton(v, n)
        bank = self.b.O.read(v, key)
        v.wait_ge(self.s_nw, 3 * self.b.O.number[key] + 3)
        v.tensor_tensor(self.t.o(*self.steps[n]), bank, self.t.sm[:, :], ALU.mult).then_inc(self.b.O.free, 1)

    def ahead(self, i):
        n, kt = divmod(i, self.nkt)
        if not self.own:
            s = self.scores(n + 2)
            return s[:2], s[2:]
        s = self.scores(n + 2)[0:4] if kt == 3 else self.scores(n + 1)[4 * kt + 4:4 * kt + 8]
        return s[:2], s[2:]

    def turns(self, i):
        n, kt = divmod(i, self.nkt)
        return n + 1 if kt == self.nkt - 1 else None

    def divided(self, i):
        ends = i - (3 if self.own else 2)
        return ends // self.nkt if 0 <= ends < self.units and self.last_of_unit(ends) else None

    def tensor(self, pe, second, out, end=lambda pe: None):
        for piece in self.scores(0):
            self.tensor_scores(pe, piece)
        second(pe)
        self.tensor_turn_max(pe, 0)
        for piece in self.scores(1)[0:4]:
            self.tensor_scores(pe, piece)
        for i in range(self.units):
            for half in range(2):
                pieces = list(self.ahead(i)[half])
                for lane in (2 * half, 2 * half + 1):
                    self.tensor_exps(pe, i, lane)
                    if pieces:
                        self.tensor_scores(pe, pieces.pop(0))
                for piece in pieces:
                    self.tensor_scores(pe, piece)
                if half == 0 and self.turns(i):
                    self.tensor_turn_max(pe, self.turns(i))
                if i and half == 0:
                    self.tensor_sums(pe, i - 1)
                if i and half == 1:
                    self.tensor_values(pe, i - 1)
            if i == self.out_unit:
                out(pe, 0)
        self.tensor_sums(pe, self.units - 1)
        self.tensor_values(pe, self.units - 1)
        end(pe)
        out(pe, 1)

    def scalar(self, a, second):
        second(a)
        a.preload_act_table_set("natural_log_exp_and_others")
        self.scalar_max(a, 0)
        for i in range(self.units):
            for lane in range(4):
                self.scalar_exps(a, i, lane)
                if lane == 1 and self.turns(i):
                    self.scalar_max(a, self.turns(i))
            if i and self.last_of_unit(i - 1):
                self.scalar_inverse(a, (i - 1) // self.nkt)
        self.scalar_inverse(a, len(self.steps) - 1)

    def vector(self, v, ch, second, out, end=(lambda v: None, lambda v: None)):
        for piece in self.scores(0):
            self.vector_max(v, piece)
        self.vector_negate(v, ch, 0)
        second(v)
        self.vector_max_rows(v, 0)
        for piece in self.scores(1)[0:4]:
            self.vector_max(v, piece)
        if not self.own:
            self.vector_negate(v, ch, 1)
        for i in range(self.units):
            first, second = self.ahead(i)
            if not self.own:
                for piece in first:
                    self.vector_max(v, piece)
                self.vector_max_rows(v, self.turns(i))
                for piece in second:
                    self.vector_max(v, piece)
                if i + 2 <= 7:
                    self.vector_negate(v, ch, i + 2)
            else:
                n, kt = divmod(i, self.nkt)
                for piece in first:
                    self.vector_max(v, piece)
                if kt == 3:
                    self.vector_max_rows(v, n + 1)
                for piece in second:
                    self.vector_max(v, piece)
                if kt == 2 and n < 7:
                    self.vector_negate(v, ch, n + 1)
            if i == self.out_unit:
                out(v, 0)
            if self.divided(i) is not None:
                self.vector_divide(v, self.divided(i))
        end[0](v)
        for i in range(self.units, self.units + 3):
            if self.divided(i) is not None:
                self.vector_divide(v, self.divided(i))
        end[1](v)
        out(v, 1)


def fill_key_ones(a, core, ks, kind):
    s, _ = CST["ksel"]
    one = core.cst[STK:STKM, s:s + 4]
    for i in range(3 if kind == "self" else PAIR):
        if kind == "self":
            out, src = ks[STK:STKM, i, :, :], one.unsqueeze(2).to_broadcast([8, 4, T])
        else:
            out = ks[STK:STKM, i, :, :].rearrange("p (m q) n -> p m q n", q=4)
            src = one.unsqueeze(1).unsqueeze(3).to_broadcast([8, 4, 4, NKE])
        last = a.activation(out, src, ACT.Copy)
    return last


class Space:
    pass


def attention_tensors(core, sb, kind):
    t = Space()
    t.mx = sb("score_max", [P, 2, NT, 4])
    t.nm = sb("neg_max", [P, NT, 4, 2], BF16)
    t.p = sb("weights", [P, 3, 4, T])
    t.rs = sb("inv_sums", [P, T])
    t.sm = sb("sums", [P, T])
    t.stage = t.p if kind == "self" else sb("proj_parts", [P, 2, 4, T])
    if kind == "self":
        t.pm = sb("masked", [P, 2, 4, P])
        t.ks = sb("k_stack", [P, 3, 4, T], F32R)
        t.vv = sb("v_self", [P, PAIR, NT, T])
        t.v = lambda u, kt, m, q: t.vv[:, u, kt, DH * (4 * m + q):DH * (4 * m + q) + DH]
    else:
        t.ks = sb("k_stack", [P, PAIR, H, NKE], F32R)
    if kind == "narrow":
        t.kc = sb("k_compact", [P, PAIR, 4, NKE], F32R)
    if kind == "wide":
        t.q4 = sb("q_stack4", [P, 4, T], F32R)
        t.vv = sb("v_wide", [P, PAIR, T])
        t.v = lambda u, kt, m, q: t.vv[:, u, DH * (4 * m + q):DH * (4 * m + q) + DH]
    if kind == "narrow":
        t.vv = sb("v_narrow", [P, PAIR, 4, 160])
        t.v = lambda u, kt, m, q: t.vv[:, u, q, 32 * m:32 * m + 32]
        t.ot = sb("heads_out", [P, PAIR, T])
        t.o = lambda u, m: t.ot[:, u, :]
    else:
        t.ot = sb("heads_out", [P, 4, T])
        t.o = lambda u, m: t.ot[:, m, :]
    return t


def block_narrow(core, layer, pair, load):
    L = f"L{layer}"
    with ExitStack() as mem, Block(core, f"{L}x", attention=True) as b:
        sb = core.sb(mem, b.name + "_")
        t = attention_tensors(core, sb, "narrow")
        t.ctx = core.ctxp
        norm = Norm(b, "norm", core.x, core.n)
        turn = Turn(b, "turn", norm)
        if load:
            raw = sb("ctx_raw", [NK, PAIR, NC])
            cn = sb("ctx_norm", [NK, PAIR, NC])
            cnorm = Norm(b, "cnorm", raw, cn, parts=NK, tiles=PAIR)
        col = lambda name: (lambda m: core.Cc(name))
        att = Attention(b, "att", "narrow", t, (D // H) ** -0.5, L + "q", col(L + "bq"), L + "k", col(L + "bk"))
        s_ld = b.sem("load")
        s_xb = b.sem("xb")
        s_zero = b.sem("zero")
        s_ones = b.sem("ones")
        D_ = b.D

        @b.block.tensor
        def _(pe):
            if load:
                pe.wait_ge(s_ld, 48)
            for u in range(PAIR):
                att.tensor_project(pe, u, (1,))
                bank = D_.fill(pe, ("v", u))
                pe.matmul(bank[0:NK, 0:P], core.ctxp[:, u, 0:NK], core.X(L + "v"), start=True, stop=True)\
                    .then_inc(D_.full, 1)
            turn.tensor(pe)
            for u in range(PAIR):
                turn.ready(pe, u)
                att.tensor_project(pe, u, (0,))
            if load:
                for u in range(PAIR):
                    pe.wait_ge(cnorm.s_n, u + 1)
                    bank = D_.fill(pe, ("ctx", u))
                    pe.transpose(bank[0:NC, 0:NK], cn[:, u, :], core.K("ident", 0, NK, NK)).then_inc(D_.full, 1)
            for u in range(PAIR):
                D_.done(pe, ("v", u))
                att.staged_all(pe, u)

            def out(pe, u):
                b.O.done(pe, att.sums(4 * u + 3))
                bank = D_.fill(pe, ("o", u))
                for i in range(NT):
                    tok = slice(i * P, i * P + P)
                    mm = pe.matmul(bank[:, tok], t.ot[:, u, tok], core.F(L + "o"), start=True, stop=True)
                mm.then_inc(D_.full, 1)

            att.tensor(pe, lambda pe: None, out)

        @b.block.vector
        def _(v):
            ch = Chain(v, b.sem("chain"))
            if load:
                v.wait_ge(s_ld, 48)
            norm.vector_stats(v)
            for u in range(PAIR):
                att.vector_project(v, u, (1,))
                bank = D_.read(v, ("v", u))
                v.wait_ge(s_zero, 1)
                v.tensor_tensor(t.vv[0:NK, u, :, :].rearrange("p q (m e) -> p q m e", e=40)[:, :, :, 0:8],
                                bank[0:NK, 0:P].rearrange("p (q m e) -> p q m e", q=4, m=4),
                                core.R(L + "bv")[0:NK].rearrange("p (q m e) -> p q m e", q=4, m=4),
                                ALU.add).then_inc(D_.free, 1)
            norm.vector_apply(v)
            if load:
                v.wait_ge(norm.s_n, PAIR)
                cnorm.vector_stats(v)
            turn.vector(v)
            if load:
                cnorm.vector_apply(v)
            for u in range(PAIR):
                att.vector_project(v, u, (0,))
            if load:
                for u in range(PAIR):
                    bank = D_.read(v, ("ctx", u))
                    v.tensor_copy(core.ctxn[:, u, 0:NK], bank[0:NC, 0:NK]).then_inc(D_.free, 1)
            att.key_blocks(v, att.s_kb)

            def out(v, u):
                bank = D_.read(v, ("o", u))
                v.wait_ge(s_xb, 1)
                x = core.toks(core.x, u).rearrange("p t d -> p (t d)")
                v.scalar_tensor_tensor(x, bank, core.tg[:, layer:layer + 1], x, ALU.mult, ALU.add)\
                    .then_inc(D_.free, 1)

            att.vector(v, ch, lambda v: None, out)

        @b.block.scalar
        def _(a):
            for u in range(PAIR):
                att.scalar_project(a, u, (1,))
            turn.scalar(a)
            for u in range(PAIR):
                att.scalar_project(a, u, (0,))
            a.wait_ge(s_zero, 2)
            att.scalar(a, lambda a: None)

        @b.block.gpsimd
        def _(g):
            g.memset(f32(t.kc[:, :, :, :]), 1.0).then_inc(s_ones, 1)
            g.memset(t.vv[:, :, :, :], 0.0).then_inc(s_zero, 1)
            norm.gpsimd(g)
            if load:
                cnorm.gpsimd(g)
            g.memset(t.p[:, :, :, :], 0.0).then_inc(s_zero, 1)
            g.wait_ge(norm.s_n, PAIR)
            g.tensor_tensor(core.x[:, :, :], core.x[:, :, :], core.rows(L + "bo", PAIR * NT), ALU.add).then_inc(s_xb, 1)
            att.gpsimd(g)

        @b.block.sync
        def _(sp):
            if load:
                sp.dma_start(core.x[:, :, :], core.io["x"][bass.ds(pair * PAIR, PAIR)]
                             .rearrange("b (t p) d -> p (b t) d", p=P)).then_inc(s_ld, 16)
                sp.dma_start(core.ctxp[:, :, :], core.io["ctxT"][:, bass.ds(pair * PAIR, PAIR), :]).then_inc(s_ld, 16)
                sp.dma_start(raw[:, :, :], core.io["ctx"][bass.ds(pair * PAIR, PAIR)]
                             .rearrange("b k c -> k b c")).then_inc(s_ld, 16)
            sp.wait_ge(s_ones, 1)
            att.sync(sp, None)


def block_experts0(core):
    with ExitStack() as mem, Block(core, "e0") as b:
        sb = core.sb(mem, b.name + "_")
        raw = sb("w1_raw", [P, 2, 4 * F0])
        wl = sb("w1_lo", [P, 2 * E0 * F0], F32R)
        wh = sb("w1_hi", [P, 2 * E0 * F0], F32R)
        w2 = sb("w2", [P, 2 * E0, D])
        b2 = sb("b2", [E0, D])
        bv = sb("b_value", [P, E0, 2])
        lg = sb("logits", [P, PAIR * NT, E0])
        gate = Gate(core, sb, E0)
        wt = sb("w_turned", [E0, PAIR * NT, P])
        gc = sb("gate_clipped", [P, 4, T])
        sg = sb("gate_sigmoid", [P, 4, T])
        vc = sb("value", [P, 4, T])
        h = sb("hidden", [P, 3, T])
        acc = core.x1
        diff = sb("logit_diff", [P, PAIR * NT])
        w01 = sb("weights01", [P, 2, PAIR * NT])
        comb = sb("combine", [P, PAIR * NT, E0])
        part = sb("combine_part", [P, PAIR * NT, E0])
        norm = Norm(b, "norm", core.x, core.n)
        turn = Turn(b, "turn", norm)
        s_ld = [b.sem(f"load{i}") for i in range(3)]
        s_wh = b.sem("w_hi")
        s_wl = b.sem("w_lo")
        s_diff = b.sem("diff")
        s_w01 = b.sem("w01")
        s_comb = b.sem("comb")
        s_wt = b.sem("wt")
        s_gc = b.D.free
        s_bv = b.sem("bv")
        s_sg = b.sem("sg")
        s_vc = b.sem("vc")
        s_t = b.sem("t")
        s_h = b.sem("h")
        s_y = b.sem("y")
        units = [(u, e, s) for u in range(PAIR) for e in range(E0) for s in range(2)]
        b1, _ = COL["b1"]

        def bias1(e, what, s):
            k = b1 + 4 * e + 2 * what + s
            return core.col[:, k:k + 1]

        def w1(w, e, what, s):
            k = (2 * e + what) * F0 + s * P
            return w[:, k:k + P]

        def chunk(c):
            return slice(4 * F0 * c, 4 * F0 * (c + 1))

        def wait_y(eng, j):
            u, e, s = units[j]
            if s:
                b.O.read(eng, ("y", u, e))
            else:
                eng.wait_ge(s_y, j // 2 + 1)

        @b.block.tensor
        def _(pe):
            turn.tensor(pe)
            bank = b.S.fill(pe, "logits")
            for u in range(PAIR):
                turn.ready(pe, u)
                for i in range(NT):
                    k = E0 * (NT * u + i)
                    mm = product_rows(pe, core, bank[:, k:k + E0], "g0", u, i)
            mm.then_inc(b.S.full, 1)
            def hidden(j):
                u, e, s = units[j]
                if u == 0 and s == 0:
                    pe.wait_ge(s_wl, e // 2 + 1)
                for what, ring in ((0, b.D), (1, b.A)):
                    bank = ring.fill(pe, ("h", j))
                    pe.matmul(bank, w1(wh, e, what, s), core.nh[:, u, :], start=True, stop=False)
                    pe.matmul(bank, w1(wh, e, what, s), core.nl[:, u, :], start=False, stop=False)
                    pe.matmul(bank, w1(wl, e, what, s), core.nh[:, u, :], start=False, stop=True).then_inc(ring.full, 1)

            def down(j):
                u, e, s = units[j]
                if s == 0:
                    self_bank[0] = b.O.fill(pe, ("y", u, e))
                pe.wait_ge(s_h, j + 1)
                for i in range(NT):
                    mm = pe.matmul(self_bank[0][:, i * P:i * P + P], h[:, j % 3, i * P:i * P + P], w2[:, 2 * e + s, :],
                                   start=s == 0 and i == 0, stop=s == 1, skip_group_check=True)
                mm.then_inc(b.O.full if s else s_y, 1)

            def second_biases(pe):
                for u in range(PAIR):
                    b.S.done(pe, ("wt", u))
                    bank = b.S.fill(pe, ("bias", u))
                    for i in range(NT):
                        mm = pe.matmul(bank[:, i * P:i * P + P], wt[:, NT * u + i, :], b2[:, :], start=True, stop=True)
                    mm.then_inc(b.S.full, 1)

            self_bank = [None]
            hidden(0)
            hidden(1)
            hidden(2)
            pe.wait_ge(s_comb, 1)
            pe.wait_ge(s_ld[2], 32)
            for u in range(PAIR):
                bank = b.S.fill(pe, ("wt", u))
                for i in range(NT):
                    mm = pe.transpose(bank[0:E0, i * P:i * P + P], comb[:, NT * u + i, :], core.K("ident"))
                mm.then_inc(b.S.full, 1)
            for j in range(3, len(units) + 3):
                if j < len(units):
                    hidden(j)
                if j == 3:
                    second_biases(pe)
                down(j - 3)

        @b.block.scalar
        def _(a):
            turn.scalar(a)
            for c in range(E0 // 2):
                a.wait_ge(s_ld[c % 2], 16 * (c // 2 + 1))
                a.activation(wh[:, chunk(c)], raw[:, c % 2, :], ACT.Copy).then_inc(s_wh, 1)
                if c == E0 // 2 - 2:
                    a.wait_ge(s_diff, 1)
                    a.activation(w01[:, 0, :], diff[:, :], ACT.Sigmoid)
                    a.activation(w01[:, 1, :], diff[:, :], ACT.Sigmoid, scale=-1.0).then_inc(s_w01, 1)
            a.wait_ge(s_bv, 1)
            for j, (u, e, s) in enumerate(units):
                if j >= 4:
                    a.wait_ge(s_h, j - 3)
                b.D.done(a, ("h", j))
                a.activation(sg[:, j % 4, :], gc[:, j % 4, :], ACT.Sigmoid, scale=1.702).then_inc(s_sg, 1)
                bank = b.A.read(a, ("h", j))
                a.activation(vc[:, j % 4, :], bank, ACT.Identity, bias=bv[:, e, s:s + 1]).then_inc(b.A.free, 1)

        @b.block.gpsimd
        def _(g):
            norm.gpsimd(g)
            for c in range(E0 // 2):
                g.wait_ge(s_wh, c + 1)
                g.tensor_tensor(wl[:, chunk(c)], raw[:, c % 2, :], f32(wh[:, chunk(c)]), ALU.subtract).then_inc(s_wl, 1)
            for j, (u, e, s) in enumerate(units):
                g.wait_ge(s_sg, j + 1)
                g.tensor_tensor(sg[:, j % 4, :], sg[:, j % 4, :], gc[:, j % 4, :], ALU.mult).then_inc(s_t, 1)

        @b.block.vector
        def _(v):
            ch = Chain(v, b.sem("chain"))
            norm.vector_stats(v)
            norm.vector_apply(v)
            v.tensor_scalar(bv[:, :, :], core.col[:, b1:b1 + 4 * E0].rearrange("p (e w s) -> p e w s", e=E0, w=2)[:, :, 1, :],
                            1.0, None, ALU.add).then_inc(s_bv, 1)
            turn.vector(v)
            bank = b.S.read(v, "logits")
            ins = v.tensor_copy(lg[:, :, :], bank[:, 0:PAIR * NT * E0].rearrange("p (t e) -> p t e", e=E0))
            ins.then_inc(b.S.free, 1)
            b.S.done(v, "logits")
            gate.largest(v, ch, lg)
            v.tensor_tensor(diff[:, :], gate.mx[:, :, 0], gate.mx[:, :, 1], ALU.subtract).then_inc(s_diff, 1)
            def clip(j):
                u, e, s = units[j]
                bank = b.D.read(v, ("h", j))
                v.tensor_scalar(gc[:, j % 4, :], bank, bias1(e, 0, s), 9.0, ALU.add, ALU.min).then_inc(b.D.free, 1)

            clip(0)
            clip(1)
            v.wait_ge(s_w01, 1)
            for k, out in ((0, comb), (1, part)):
                ch.link(gate.one_hot(v, out[:, :, :], k))
                ch.link(v.tensor_tensor(out[:, :, :], out[:, :, :], w01[:, k, :].unsqueeze(2).to_broadcast([P, PAIR * NT, E0]),
                                        ALU.mult))
            ins = v.tensor_tensor(comb[:, :, :], comb[:, :, :], part[:, :, :], ALU.add)
            ins.then_inc(s_comb, 1)
            v.wait_ge(s_comb, 1)

            def combine(u, e):
                bank = b.O.read(v, ("y", u, e))
                if e == 0:
                    src = b.S.read(v, ("bias", u))
                    ins = v.tensor_copy(acc[:, 0:NT, :], src.rearrange("p (t d) -> p t d", t=NT))
                    ins.then_inc(b.S.free, 1)
                    b.S.done(v, ("bias", u))
                for i in range(NT):
                    ins = v.scalar_tensor_tensor(acc[:, i, :], bank[:, i * P:i * P + P], comb[:, NT * u + i, e:e + 1],
                                                 acc[:, i, :], ALU.mult, ALU.add)
                ins.then_inc(b.O.free, 1)
                b.O.done(v, ("y", u, e))
                if e == E0 - 1:
                    x = core.toks(core.x, u)
                    ch.link(v.scalar_tensor_tensor(x, acc[:, 0:NT, :], core.tg[:, 4:5], x, ALU.mult, ALU.add))

            for u in range(PAIR):
                bank = b.S.read(v, ("wt", u))
                v.tensor_copy(wt[:, NT * u:NT * u + NT, :], bank[0:E0, :].rearrange("p (t d) -> p t d", t=NT))\
                    .then_inc(b.S.free, 1)
            n = len(units)
            for j in range(n + 3):
                if j >= 4 and units[j - 4][2]:
                    combine(*units[j - 4][:2])
                if j + 2 < n:
                    clip(j + 2)
                if j < n:
                    b.A.done(v, ("h", j))
                    v.tensor_scalar(vc[:, j % 4, :], vc[:, j % 4, :], -8.0, 10.0, ALU.max, ALU.min).then_inc(s_vc, 1)
                    v.wait_ge(s_vc, j + 1)
                    v.wait_ge(s_t, j + 1)
                    if j >= 3:
                        wait_y(v, j - 3)
                    v.tensor_tensor(h[:, j % 3, :], sg[:, j % 4, :], vc[:, j % 4, :], ALU.mult).then_inc(s_h, 1)
            combine(*units[n - 1][:2])

        @b.block.sync
        def _(sp):
            for c in range(E0 // 2):
                if c >= 2:
                    sp.wait_ge(s_wl, c - 1)
                sp.dma_start(raw[:, c % 2, :], core.io["w1"][:, chunk(c)]).then_inc(s_ld[c % 2], 16)
                if c == 1:
                    sp.dma_start(w2[:, :, :], core.io["w2"]).then_inc(s_ld[2], 16)
                    sp.dma_start(b2[:, :], core.io["b2"]).then_inc(s_ld[2], 16)


class Gate:

    def __init__(self, core, sb, experts):
        n = PAIR * NT
        self.core, self.experts = core, experts
        self.mx = sb("largest", [P, n, 8])
        self.ix = sb("largest_at", [P, n, 8], U32)
        self.ixf = sb("largest_at_f", [P, n, 8])

    def largest(self, v, ch, scores):
        for t in range(PAIR * NT):
            last = v.max(self.mx[:, t, :], scores[:, t, :])
        ch.link(last)
        for t in range(PAIR * NT):
            last = v.max_index(self.ix[:, t, :], self.mx[:, t, :], scores[:, t, :])
        ch.link(last)
        ch.link(v.tensor_copy(self.ixf[:, :, :], self.ix[:, :, :]))

    def one_hot(self, v, out, k):
        n = PAIR * NT
        return v.tensor_tensor(out, self.core.K("iota", 0, self.experts).unsqueeze(1).to_broadcast([P, n, self.experts]),
                               self.ixf[:, :, k:k + 1].to_broadcast([P, n, self.experts]), ALU.is_equal)


class Tail:

    def __init__(self, b, a, att, xo, k_bias):
        self.b, self.core, self.a, self.att, self.xo, self.k_bias = b, b.core, a, att, xo, k_bias
        self.s_xb = b.sem("t_xb")
        self.s_xo = b.sem("t_xo")
        self.s_r = b.sem("t_r")
        self.norm = Norm(b, "t_norm", xo, b.core.n)
        self.turn = Turn(b, "t_turn", self.norm)

    def hidden(self, u, m):
        return self.att.t.p[:, (2, 0)[u], m, :]

    def tensor_out(self, pe, u):
        b, att = self.b, self.att
        b.O.done(pe, att.sums(4 * u + 3))
        bank = b.D.fill(pe, ("li1", u))
        for i in range(NT):
            tok = slice(i * P, i * P + P)
            for m in range(4):
                mm = pe.matmul(bank[:, tok], att.t.ot[:, m, tok], self.core.F(self.a + "li1", m * P, m * P + P),
                               start=m == 0, stop=m == 3)
        mm.then_inc(b.D.full, 1)

    def vector_out(self, v, u):
        bank = self.b.D.read(v, ("li1", u))
        if u == 0:
            v.wait_ge(self.s_xb, 1)
        x = self.core.toks(self.xo, u).rearrange("p t d -> p (t d)")
        v.tensor_tensor(x, bank, x, ALU.add).then_inc(self.b.D.free, 1)

    def gpsimd_bias(self, g):
        c = self.core
        g.tensor_tensor(self.xo[:, :, :], c.x1[:, :, :], c.rows(self.a + "li1b", PAIR * NT), ALU.add)\
            .then_inc(self.s_xb, 1)

    def tensor_end(self, pe):
        self.turn.tensor(pe, (0,))

    def tensor(self, pe):
        b, c = self.b, self.core
        for u in range(PAIR):
            self.turn.ready(pe, u)
            for m in range(4):
                bank = b.A.fill(pe, ("li2", u, m))
                product(pe, c, bank, self.a + "li2", u, m * P, m * P + P).then_inc(b.A.full, 1)
            if u == 0:
                self.turn.tensor(pe, (1,))
            self.tensor_last(pe, u)

    def tensor_last(self, pe, u):
        b, c = self.b, self.core
        bank = b.D.fill(pe, ("li3", u))
        b.A.done(pe, ("li2", u, 3))
        for i in range(NT):
            tok = slice(i * P, i * P + P)
            for m in range(4):
                mm = pe.matmul(bank[:, tok], self.hidden(u, m)[:, tok], c.F(self.a + "li3", m * P, m * P + P),
                               start=m == 0, stop=m == 3)
        mm.then_inc(b.D.full, 1)

    def scalar(self, a):
        for u in range(PAIR):
            self.turn.scalar(a, (u,))
            if u == 0:
                self.att.wait_pv(a, self.att.units - 3)
            for m in range(4):
                bank = self.b.A.read(a, ("li2", u, m))
                k = self.k_bias + m
                a.activation(self.hidden(u, m), bank, ACT.Gelu, bias=self.core.bias[:, k:k + 1])\
                    .then_inc(self.b.A.free, 1)

    def gpsimd(self, g):
        c = self.core
        s = self.b.sem("t_g")
        self.norm.gpsimd(g, (0,))
        g.tensor_tensor(c.x1[:, :, :], c.x1[:, :, :], c.rows(self.a + "li3b", PAIR * NT), ALU.add).then_inc(s, 1)
        g.wait_ge(s, 1)
        for u in range(PAIR):
            if u:
                self.norm.gpsimd(g, (u,))
            self.b.D.done(g, ("li1", u))
            g.tensor_tensor(c.toks(c.x1, u), c.toks(c.x1, u), c.toks(self.xo, u), ALU.add).then_inc(self.s_r, 1)

    def vector_begin(self, v):
        self.b.D.done(v, ("li1", 0))
        self.norm.vector_stats(v, us=(0,))
        self.norm.vector_apply(v, (0,))

    def vector_turn(self, v):
        self.turn.vector(v, (0,))

    def vector(self, v, last):
        self.b.D.done(v, ("li1", 1))
        self.norm.vector_stats(v, us=(1,))
        self.norm.vector_apply(v, (1,))
        self.turn.vector(v, (1,))
        for u in range(PAIR):
            bank = self.b.D.read(v, ("li3", u))
            v.wait_ge(self.s_r, u + 1)
            x = self.core.toks(self.core.x1, u).rearrange("p t d -> p (t d)")
            v.tensor_tensor(x, bank, x, ALU.add).then_inc(self.b.D.free, 1)
            self.b.D.done(v, ("li3", u))
            last(v, u)


def gains(v, core, ch, name, u):
    x1, n = core.toks(core.x1, u), core.toks(core.n, u)
    ch.link(v.tensor_tensor(x1, n, core.rows(name + "g", NT), ALU.mult))
    ch.link(v.tensor_tensor(x1, x1, core.rows(name + "b", NT), ALU.add))


def block_self(core):
    with ExitStack() as mem, Block(core, "s1", attention=True) as b:
        sb = core.sb(mem, b.name + "_")
        t = attention_tensors(core, sb, "self")
        xo = sb("x_out", [P, PAIR * NT, D])
        outer = Norm(b, "outer", core.x, core.n)
        first = Norm(b, "first", core.n, core.n)
        norm = Norm(b, "norm", core.x1, core.n)
        turn = Turn(b, "turn", norm)
        col = lambda k: (lambda m: core.bias[:, k + m:k + m + 1])
        att = Attention(b, "att", "self", t, DH ** -0.5, "a1q", col(0), "a1k", col(4))
        tail = Tail(b, "a1", att, xo, 8)
        last = Norm(b, "last", core.x1, core.n)
        s_ones = b.sem("ones")

        @b.block.tensor
        def _(pe):
            turn.tensor(pe, (0,))

            def project(pe, u):
                turn.ready(pe, u)
                att.tensor_project(pe, u, att.late)
                if u == 0:
                    turn.tensor(pe, (1,))
                for kt in range(NT):
                    bank = b.D.fill(pe, ("v", u, kt))
                    product_rows(pe, core, bank, "a1v", u, kt).then_inc(b.D.full, 1)
                b.D.done(pe, ("v", u, NT - 1))

            project(pe, 0)
            att.tensor(pe, lambda pe: project(pe, 1), tail.tensor_out, tail.tensor_end)
            tail.tensor(pe)

        @b.block.scalar
        def _(a):
            fill_key_ones(a, core, t.ks, "self").then_inc(s_ones, 1)
            turn.scalar(a, (0,))
            att.scalar_project(a, 0, att.late)
            turn.scalar(a, (1,))

            def second(a):
                att.scalar_project(a, 1, att.late)
                att.staging_done(a, len(att.items))

            att.scalar(a, second)
            tail.scalar(a)

        @b.block.gpsimd
        def _(g):
            outer.gpsimd(g)
            for u in range(PAIR):
                first.gpsimd(g, (u,))
                norm.gpsimd(g, (u,))
            tail.gpsimd_bias(g)
            att.gpsimd(g)
            tail.gpsimd(g)
            last.gpsimd(g)

        @b.block.vector
        def _(v):
            ch = Chain(v, b.sem("chain"))

            def to_norm(v, u):
                first.vector_apply(v, (u,))
                v.wait_ge(first.s_n, u + 1)
                gains(v, core, ch, "ln1", u)
                if u:
                    turn.vector(v, (0,))
                norm.vector_stats(v, us=(u,))

            for u in range(PAIR):
                outer.vector_stats(v, us=(u,))
            outer.vector_apply(v, (0,))
            first.vector_stats(v, outer, (0,))
            outer.vector_apply(v, (1,))
            to_norm(v, 0)
            first.vector_stats(v, outer, (1,))
            norm.vector_apply(v, (0,))
            to_norm(v, 1)
            norm.vector_apply(v, (1,))

            def project(v, u):
                att.vector_project(v, u, att.late)
                if u == 0:
                    turn.vector(v, (1,))
                for kt in range(NT):
                    bank = b.D.read(v, ("v", u, kt))
                    v.tensor_tensor(t.vv[:, u, kt, :], bank, core.vb1[:, :], ALU.add).then_inc(b.D.free, 1)

            project(v, 0)
            att.vector(v, ch, lambda v: project(v, 1), tail.vector_out, (tail.vector_begin, tail.vector_turn))

            def finish(v, u):
                last.vector_stats(v, us=(u,))
                last.vector_apply(v, (u,))
                v.wait_ge(last.s_n, u + 1)
                gains(v, core, ch, "ln2", u)

            tail.vector(v, finish)

        @b.block.sync
        def _(sp):
            att.sync(sp, lambda sp: sp.wait_ge(s_ones, 1))


def block_wide(core):
    with ExitStack() as mem, Block(core, "w1", attention=True) as b:
        sb = core.sb(mem, b.name + "_")
        t = attention_tensors(core, sb, "wide")
        t.ctx = core.ctxn
        xo = sb("x_out", [P, PAIR * NT, D])
        norm = Norm(b, "norm", core.x1, core.n)
        turn = Turn(b, "turn", norm)
        col = lambda k: (lambda m: core.bias[:, k + m:k + m + 1])
        att = Attention(b, "att", "wide", t, DH ** -0.5, "a2q", col(12), "a2k", col(20))
        tail = Tail(b, "a2", att, xo, 16)
        s_zero = b.sem("zero")
        s_ones = b.sem("ones")

        @b.block.tensor
        def _(pe):
            def values(u):
                bank = b.D.fill(pe, ("v", u))
                pe.matmul(bank[0:NK, :], t.ctx[:, u, 0:NK], core.X("a2v"), start=True, stop=True).then_inc(b.D.full, 1)

            att.tensor_project(pe, 0, (1,))
            values(0)
            att.tensor_project(pe, 1, (1,))
            turn.tensor(pe, (0,))

            def project(pe, u):
                turn.ready(pe, u)
                att.tensor_project(pe, u, (0,))
                if u == 0:
                    values(1)
                    turn.tensor(pe, (1,))
                att.staged_all(pe, u)

            project(pe, 0)
            att.tensor(pe, lambda pe: project(pe, 1), tail.tensor_out, tail.tensor_end)
            tail.tensor(pe)

        @b.block.scalar
        def _(a):
            for u in range(PAIR):
                att.scalar_project(a, u, (1,))
            fill_key_ones(a, core, t.ks, "wide").then_inc(s_ones, 1)
            turn.scalar(a, (0,))
            att.scalar_project(a, 0, (0,))
            turn.scalar(a, (1,))
            a.wait_ge(s_zero, 2)
            att.scalar(a, lambda a: att.scalar_project(a, 1, (0,)))
            tail.scalar(a)

        @b.block.gpsimd
        def _(g):
            g.memset(t.vv[:, :, :], 0.0).then_inc(s_zero, 1)
            norm.gpsimd(g)
            g.memset(t.p[:, :, :, :], 0.0).then_inc(s_zero, 1)
            tail.gpsimd_bias(g)
            att.gpsimd(g)
            tail.gpsimd(g)

        @b.block.vector
        def _(v):
            ch = Chain(v, b.sem("chain"))
            def values(u):
                bank = b.D.read(v, ("v", u))
                v.tensor_tensor(t.vv[0:NK, u, :], bank[0:NK, :], core.vb2[0:NK, :], ALU.add).then_inc(b.D.free, 1)

            att.vector_project(v, 0, (1,))
            v.wait_ge(s_zero, 1)
            values(0)
            norm.vector_stats(v, us=(0,))
            att.vector_project(v, 1, (1,))
            norm.vector_apply(v, (0,))
            norm.vector_stats(v, us=(1,))
            turn.vector(v, (0,))
            norm.vector_apply(v, (1,))
            att.vector_project(v, 0, (0,))
            values(1)
            turn.vector(v, (1,))
            att.vector(v, ch, lambda v: att.vector_project(v, 1, (0,)), tail.vector_out, (tail.vector_begin, tail.vector_turn))

            def finish(v, u):
                x, x1 = core.toks(core.x, u), core.toks(core.x1, u)
                v.scalar_tensor_tensor(x, x1, core.tg[:, 1:2], x, ALU.mult, ALU.add)

            tail.vector(v, finish)

        @b.block.sync
        def _(sp):
            att.sync(sp, lambda sp: sp.wait_ge(s_ones, 1))


def block_experts1(core):
    TILES = E1 // 2
    with ExitStack() as mem, Block(core, "e1") as b:
        sb = core.sb(mem, "e1_")
        n = PAIR * NT
        down = sb("w_down", [P, TILES + 1, D])
        gate = Gate(core, sb, E1)
        score = sb("scores", [P, n, E1])
        comb = sb("combine", [P, n, E1])
        hot = sb("one_hot", [P, n, E1])
        total = sb("top_sum", [P, n])
        c3 = sb("combine_parts", [P, n, 3, E1], BF16)
        ct = sb("combine_turned", [3 * E1, PAIR, T], BF16)
        sg = sb("gate_silu", [P, 3, T])
        up = sb("hidden_raw", [P, 3, T])
        h = sb("hidden", [P, 3, T])
        norm = Norm(b, "norm", core.x, core.n)
        turn = Turn(b, "turn", norm)
        s_ld = b.sem("load")
        s_score = b.sem("score")
        s_comb = b.sem("comb")
        s_y = b.sem("y")
        units = [(u, j) for u in range(PAIR) for j in range(TILES + 1)]

        def wait_y(eng, i):
            u, j = units[i]
            if j == TILES:
                b.O.read(eng, ("y", u))
            else:
                eng.wait_ge(s_y, i + 1 - u)

        @b.block.tensor
        def _(pe):
            turn.tensor(pe)
            bank = b.S.fill(pe, "logits")
            for u in range(PAIR):
                turn.ready(pe, u)
                for i in range(NT):
                    k = E1 * (NT * u + i)
                    mm = product_rows(pe, core, bank[:, k:k + E1], "g1", u, i)
            mm.then_inc(b.S.full, 1)

            def hidden(i):
                u, j = units[i]
                for what, ring in ((0, b.A), (1, b.D)):
                    bank = ring.fill(pe, ("h", i))
                    if j < TILES:
                        product(pe, core, bank, ("eg", "eu")[what], u, j * P, j * P + P).then_inc(ring.full, 1)
                    else:
                        product(pe, core, bank, ("sg", "su")[what], u).then_inc(ring.full, 1)

            def weights(i):
                u, j = units[i]
                if j < TILES:
                    bank = b.S.fill(pe, ("c", i))
                    pe.matmul(bank, core.sel48[:, j * P:j * P + P], ct[:, u, :], start=True, stop=True).then_inc(b.S.full, 1)

            def down_sum(i):
                u, j = units[i]
                if j == 0:
                    y[0] = b.O.fill(pe, ("y", u))
                if i == 0:
                    pe.wait_ge(s_ld, 16)
                if j < TILES:
                    b.S.done(pe, ("c", i))
                else:
                    b.D.done(pe, ("h", i))
                for t in range(NT):
                    mm = pe.matmul(y[0][:, t * P:t * P + P], h[:, i % 3, t * P:t * P + P], down[:, j, :],
                                   start=j == 0 and t == 0, stop=j == TILES, skip_group_check=True)
                mm.then_inc(b.O.full if j == TILES else s_y, 1)

            y = [None]
            hidden(0)
            hidden(1)
            pe.wait_ge(s_comb, 1)
            for u in range(PAIR):
                bank = b.S.fill(pe, ("ct", u)).bitcast(BF16)
                for t in range(NT):
                    mm = pe.transpose(bank[0:3 * E1, t * P:t * P + P], c3[:, NT * u + t, :, :].rearrange("p k e -> p (k e)"),
                                      core.identb[:, :])
                mm.then_inc(b.S.full, 1)
            b.S.done(pe, ("ct", 1))
            weights(0)
            weights(1)
            for i in range(2, len(units)):
                hidden(i)
                weights(i)
                down_sum(i - 2)
            down_sum(len(units) - 2)
            down_sum(len(units) - 1)

        @b.block.scalar
        def _(a):
            turn.scalar(a)
            bank = b.S.read(a, "logits")
            a.activation(score[:, :, :], bank[:, 0:n * E1].rearrange("p (t e) -> p t e", e=E1), ACT.Sigmoid)\
                .then_inc(b.S.free, 1)
            for i in range(len(units)):
                bank = b.A.read(a, ("h", i))
                if i >= 3:
                    b.D.done(a, ("h", i - 3))
                a.activation(sg[:, i % 3, :], bank, ACT.Silu).then_inc(b.A.free, 1)

        @b.block.gpsimd
        def _(g):
            norm.gpsimd(g)

        @b.block.vector
        def _(v):
            ch = Chain(v, b.sem("chain"))
            norm.vector_stats(v)
            norm.vector_apply(v)
            turn.vector(v)
            b.S.done(v, "logits")
            gate.largest(v, ch, score)
            ch.link(v.tensor_reduce(total[:, :], gate.mx[:, :, 0:4], AX, ALU.add))
            ch.link(v.tensor_scalar(total[:, :], total[:, :], 1e-20, None, ALU.add))
            ch.link(v.reciprocal(total[:, :], total[:, :]))
            ch.link(gate.one_hot(v, comb[:, :, :], 0))
            for k in range(1, 4):
                ch.link(gate.one_hot(v, hot[:, :, :], k))
                ch.link(v.tensor_tensor(comb[:, :, :], comb[:, :, :], hot[:, :, :], ALU.add))
            ch.link(v.tensor_tensor(comb[:, :, :], comb[:, :, :], score[:, :, :], ALU.mult))
            ch.link(v.tensor_tensor(comb[:, :, :], comb[:, :, :], total[:, :].unsqueeze(2).to_broadcast([P, n, E1]), ALU.mult))
            for k in range(3):
                ins = v.tensor_copy(c3[:, :, k, :], comb[:, :, :])
                if k < 2:
                    ch.link(ins)
                    ch.link(v.tensor_tensor(comb[:, :, :], comb[:, :, :], c3[:, :, k, :], ALU.subtract))
            ins.then_inc(s_comb, 1)
            for u in range(PAIR):
                bank = b.S.read(v, ("ct", u)).bitcast(BF16)
                v.tensor_copy(ct[:, u, :], bank[0:3 * E1, 0:T]).then_inc(b.S.free, 1)

            def add(u):
                bank = b.O.read(v, ("y", u))
                x = core.toks(core.x, u).rearrange("p t d -> p (t d)")
                v.scalar_tensor_tensor(x, bank, core.tg[:, 5:6], x, ALU.mult, ALU.add).then_inc(b.O.free, 1)

            for i, (u, j) in enumerate(units):
                bank = b.D.read(v, ("h", i))
                b.A.done(v, ("h", i))
                if i >= 3:
                    wait_y(v, i - 3)
                out = up if j < TILES else h
                v.tensor_tensor(out[:, i % 3, :], bank, sg[:, i % 3, :], ALU.mult).then_inc(b.D.free, 1)
                if j < TILES:
                    b.D.done(v, ("h", i))
                    bank = b.S.read(v, ("c", i))
                    v.tensor_tensor(h[:, i % 3, :], bank, up[:, i % 3, :], ALU.mult).then_inc(b.S.free, 1)
                if j == 2 and u:
                    add(0)
            add(1)

        @b.block.sync
        def _(sp):
            sp.dma_start(down[:, :, :], core.io["down"]).then_inc(s_ld, 16)


def block_single(core):
    with ExitStack() as mem, Block(core, "L2x") as b:
        sb = core.sb(mem, "L2x_")
        qh = sb("q_hi", [P, PAIR, T], F32R)
        ql = sb("q_lo", [P, PAIR, T], F32R)
        kh = sb("k_hi", [P, PAIR, NKE], F32R)
        kl = sb("k_lo", [P, PAIR, NKE], F32R)
        vv = sb("v", [NK, PAIR, D])
        mx = sb("score_max", [P, PAIR, NT])
        nm = sb("neg_max", [P, PAIR, NT, 2], BF16)
        nmt = sb("neg_max_turned", [2, PAIR, T], BF16)
        p = sb("weights", [NK, PAIR, T])
        rs = sb("inv_sums", [P, PAIR, NT])
        norm = Norm(b, "norm", core.x, core.n)
        turn = Turn(b, "turn", norm)
        s_hi = b.sem("hi")
        s_nm = b.sem("nm")
        s_sum = b.sem("sum")

        @b.block.tensor
        def _(pe):
            for u in range(PAIR):
                bank = b.S.fill(pe, ("k", u))
                pe.matmul(bank[:, 0:NKE], core.X("L2k"), core.ctxp[:, u, :], start=True, stop=True).then_inc(b.S.full, 1)
            for u in range(PAIR):
                bank = b.S.fill(pe, ("v", u))
                pe.matmul(bank[0:NK, 0:D], core.ctxp[:, u, 0:NK], core.X("L2v"), start=True, stop=True)\
                    .then_inc(b.S.full, 1)
            turn.tensor(pe)
            for u in range(PAIR):
                turn.ready(pe, u)
                bank = b.D.fill(pe, ("q", u))
                product(pe, core, bank, "L2q", u).then_inc(b.D.full, 1)
            for u in range(PAIR):
                b.D.done(pe, ("q", u))
                b.S.done(pe, ("k", u))
                bank = b.D.fill(pe, ("s", u))
                for t in range(NT):
                    tok = slice(t * P, t * P + P)
                    out = bank[:, t * KSLOT:t * KSLOT + NKE]
                    pe.matmul(out, qh[:, u, tok], kh[:, u, :], start=True, stop=False)
                    pe.matmul(out, qh[:, u, tok], kl[:, u, :], start=False, stop=False)
                    mm = pe.matmul(out, ql[:, u, tok], kh[:, u, :], start=False, stop=True)
                mm.then_inc(b.D.full, 1)
            for u in range(PAIR):
                pe.wait_ge(s_nm, u + 1)
                bank = b.S.fill(pe, ("nm", u)).bitcast(BF16)
                for t in range(NT):
                    mm = pe.transpose(bank[0:2, t * P:t * P + P], nm[:, u, t, :], core.identb[:, :])
                mm.then_inc(b.S.full, 1)
            for u in range(PAIR):
                bank = b.A.fill(pe, ("st", u))
                out = bank[0:NK, :]
                pe.matmul(out, kh[:, u, 0:NK], qh[:, u, :], start=True, stop=False)
                pe.matmul(out, kh[:, u, 0:NK], ql[:, u, :], start=False, stop=False)
                pe.matmul(out, kl[:, u, 0:NK], qh[:, u, :], start=False, stop=False)
                b.S.done(pe, ("nm", u))
                pe.matmul(out, core.ones2[:, 0:NK], nmt[:, u, :], start=False, stop=True).then_inc(b.A.full, 1)
            for u in range(PAIR):
                b.A.done(pe, ("st", u))
                b.S.done(pe, ("v", u))
                bank = b.O.fill(pe, ("y", u))
                sums = b.S.fill(pe, ("sum", u))
                for t in range(NT):
                    tok = slice(t * P, t * P + P)
                    pe.matmul(sums[:, 2 * t:2 * t + 2], p[:, u, tok], core.K("ones", 0, 2, NK), start=True, stop=True)
                    mm = pe.matmul(bank[:, tok], p[:, u, tok], vv[:, u, :], start=True, stop=True)
                mm.then_inc(b.O.full, 1)

        @b.block.scalar
        def _(a):
            for u in range(PAIR):
                bank = b.S.read(a, ("k", u))
                a.activation(kh[:, u, :], bank[:, 0:NKE], ACT.Identity, bias=core.Cc("L2bk")).then_inc(s_hi, 1)
            turn.scalar(a)
            for u in range(PAIR):
                bank = b.D.read(a, ("q", u))
                a.activation(qh[:, u, :], bank, ACT.Identity, bias=core.Cc("L2bq")).then_inc(s_hi, 1)
            for u in range(PAIR):
                bank = b.A.read(a, ("st", u))
                a.activation(p[:, u, :], bank[0:NK, :], ACT.Exp).then_inc(b.A.free, 1)

        @b.block.gpsimd
        def _(g):
            norm.gpsimd(g)

        @b.block.vector
        def _(v):
            ch = Chain(v, b.sem("chain"))
            for u in range(PAIR):
                bank = b.S.read(v, ("k", u))
                v.wait_ge(s_hi, u + 1)
                v.scalar_tensor_tensor(kl[:, u, :], bank[:, 0:NKE], core.Cc("L2bk"), f32(kh[:, u, :]), ALU.add,
                                       ALU.subtract).then_inc(b.S.free, 1)
            for u in range(PAIR):
                bank = b.S.read(v, ("v", u))
                v.tensor_tensor(vv[:, u, :], bank[0:NK, 0:D], core.R("L2bv")[0:NK], ALU.add).then_inc(b.S.free, 1)
            norm.vector_stats(v)
            norm.vector_apply(v)
            turn.vector(v)
            for u in range(PAIR):
                bank = b.D.read(v, ("q", u))
                v.wait_ge(s_hi, PAIR + u + 1)
                v.scalar_tensor_tensor(ql[:, u, :], bank, core.Cc("L2bq"), f32(qh[:, u, :]), ALU.add, ALU.subtract)\
                    .then_inc(b.D.free, 1)
            for u in range(PAIR):
                bank = b.D.read(v, ("s", u))
                v.tensor_reduce(mx[:, u, :], bank[:, 0:NT * KSLOT].rearrange("p (t k) -> p t k", t=NT)[:, :, 0:NK], AX,
                                ALU.max).then_inc(b.D.free, 1)
                b.D.done(v, ("s", u))
                hi, lo = nm[:, u, :, 0], nm[:, u, :, 1]
                ch.link(v.tensor_scalar(hi, mx[:, u, :], -1.0, None, ALU.mult))
                v.scalar_tensor_tensor(lo, mx[:, u, :], -1.0, hi, ALU.mult, ALU.subtract).then_inc(s_nm, 1)
            for u in range(PAIR):
                bank = b.S.read(v, ("nm", u)).bitcast(BF16)
                v.tensor_copy(nmt[:, u, :], bank[0:2, 0:T]).then_inc(b.S.free, 1)
            for u in range(PAIR):
                bank = b.O.read(v, ("y", u))
                sums = b.S.banks[b.S.number[("sum", u)] % 2]
                ins = v.reciprocal(rs[:, u, :], sums[:, 0:2 * NT].rearrange("p (t e) -> p t e", e=2)[:, :, 0])
                ins.then_inc(b.S.free, 1)
                b.S.done(v, ("sum", u))
                ch.link(v.tensor_scalar(rs[:, u, :], rs[:, u, :], core.tg[:, 2:3], None, ALU.mult))
                for t in range(NT):
                    x = core.x[:, NT * u + t, :]
                    ins = v.scalar_tensor_tensor(x, bank[:, t * P:t * P + P], rs[:, u, t:t + 1], x, ALU.mult, ALU.add)
                ins.then_inc(b.O.free, 1)


def block_signs(core):
    with ExitStack() as mem, Block(core, "sg") as b:
        sb = core.sb(mem, "sg_")
        words = [sb("k0", [P, 2, T // 4], U32), sb("k1", [P, T], U32), sb("k2", [P, D], U32)]
        k0, k1, k2 = words[0][:, :, :].bitcast(U8), words[1][:, :].bitcast(U8), words[2][:, :].bitcast(U8)
        half = sb("w0_half", [P, 2, T])
        w0 = sb("w0", [P, T], F32R)
        w1 = sb("w1", [P, 4 * T], F32R)
        w2 = sb("w2", [P, 4 * D], F32R)
        s2x = sb("scales", [P, 3])
        r = sb("relu", [P, 3, T])
        hh = sb("h_hi", [P, PAIR, 2, 4, T], F32R)
        hl = sb("h_lo", [P, PAIR, 4, T], F32R)
        norm = Norm(b, "norm", core.x, core.n)
        turn = Turn(b, "turn", norm)
        s_ld = b.sem("load")
        s_half = b.sem("half")
        s_w0 = b.sem("w0")
        s_w1 = b.sem("w1")
        s_s = b.sem("scale")
        s_r = b.sem("r")
        s_hi = b.sem("hi")
        s_lo = b.sem("lo")
        units = [(layer, u, m) for layer in range(2) for u in range(PAIR) for m in range(4)]

        @b.block.tensor
        def _(pe):
            turn.tensor(pe)
            for i, (layer, u, m) in enumerate(units):
                if m == 0:
                    if layer == 0:
                        turn.ready(pe, u)
                    if u == 0:
                        pe.wait_ge((s_w0, s_w1)[layer], 1)
                    if layer == 1:
                        pe.wait_ge(s_lo, 4 * u + 4)
                bank = b.A.fill(pe, i)
                cols = slice(m * P, m * P + P)
                if layer == 0:
                    pe.matmul(bank, w0[:, cols], core.nh[:, u, :], start=True, stop=False)
                    mm = pe.matmul(bank, w0[:, cols], core.nl[:, u, :], start=False, stop=True)
                else:
                    for k in range(4):
                        w = w1[:, k * T + m * P:k * T + m * P + P]
                        pe.matmul(bank, w, hh[:, u, 0, k, :], start=k == 0, stop=False)
                        mm = pe.matmul(bank, w, hl[:, u, k, :], start=False, stop=k == 3)
                mm.then_inc(b.A.full, 1)
            pe.wait_ge(s_w1, 2)
            for u in range(PAIR):
                pe.wait_ge(s_lo, 8 + 4 * u + 4)
                bank = b.D.fill(pe, ("y", u))
                for t in range(NT):
                    tok = slice(t * P, t * P + P)
                    for k in range(4):
                        w = w2[:, k * D:k * D + D]
                        pe.matmul(bank[:, tok], hh[:, u, 1, k, tok], w, start=k == 0, stop=False)
                        mm = pe.matmul(bank[:, tok], hl[:, u, k, tok], w, start=False, stop=k == 3)
                mm.then_inc(b.D.full, 1)

        @b.block.scalar
        def _(a):
            a.wait_ge(s_ld, 48)
            a.activation(half[:, :, :], k0, ACT.Copy, scale=2.0).then_inc(s_half, 1)
            a.activation(w1[:, :], k1, ACT.Copy, scale=2.0, bias=-1.0).then_inc(s_w1, 1)
            a.activation(w2[:, :], k2, ACT.Copy, scale=2.0, bias=-1.0).then_inc(s_w1, 1)
            turn.scalar(a)
            a.wait_ge(s_s, 1)
            for i, (layer, u, m) in enumerate(units):
                bank = b.A.read(a, i)
                if i >= 3:
                    a.wait_ge(s_lo, i - 2)
                a.activation(r[:, i % 3, :], bank, ACT.Relu, scale=s2x[:, layer:layer + 1]).then_inc(b.A.free, 1)

        @b.block.gpsimd
        def _(g):
            norm.gpsimd(g)

        @b.block.vector
        def _(v):
            ch = Chain(v, b.sem("chain"))
            s, _ = COL["s"]
            v.tensor_scalar(s2x[:, 0:2], core.col[:, s:s + 2], 2.0, None, ALU.mult)
            v.tensor_tensor(s2x[:, 2:3], core.col[:, s + 2:s + 3], core.tg[:, 6:7], ALU.mult).then_inc(s_s, 1)
            norm.vector_stats(v)
            norm.vector_apply(v)
            v.wait_ge(s_half, 1)
            v.tensor_tensor(w0[:, :], half[:, 0, :], half[:, 1, :], ALU.subtract).then_inc(s_w0, 1)
            turn.vector(v)
            for i, (layer, u, m) in enumerate(units):
                b.A.done(v, i)
                v.tensor_copy(hh[:, u, layer, m, :], r[:, i % 3, :]).then_inc(s_hi, 1)
                v.wait_ge(s_hi, i + 1)
                if layer == 1 and m == 0:
                    b.A.read(v, 8 + 4 * u + 3)
                v.tensor_tensor(hl[:, u, m, :], r[:, i % 3, :], f32(hh[:, u, layer, m, :]), ALU.subtract)\
                    .then_inc(s_lo, 1)
            for u in range(PAIR):
                bank = b.D.read(v, ("y", u))
                x = core.toks(core.x, u).rearrange("p t d -> p (t d)")
                v.scalar_tensor_tensor(x, bank, s2x[:, 2:3], x, ALU.mult, ALU.add).then_inc(b.D.free, 1)

        @b.block.sync
        def _(sp):
            sp.dma_start(words[0][:, :, :], core.io["k0"].rearrange("h p n -> p h n")).then_inc(s_ld, 16)
            sp.dma_start(words[1][:, :], core.io["k1"]).then_inc(s_ld, 16)
            sp.dma_start(words[2][:, :], core.io["k2"]).then_inc(s_ld, 16)


def block_setup(core):
    nc, io = core.nc, core.io
    with ExitStack() as mem, Block(core, "setup") as b:
        sb = core.sb(mem, b.name + "_")
        raw = sb("raw", [P, N_STAGED])
        cst = sb("cst_all", [P, N_CST])
        sel = sb("sel_raw", [3 * E1, E1 // 2 * P])
        freq = sb("freq", [P, 2, D])
        at = sb("at", [P, 2, D])
        rep = sb("rep", [P, P])
        rep64 = sb("rep64", [NC, P])
        s_plain = b.sem("load_plain")
        s_ld = b.sem("load")
        s_rest = b.sem("load_rest")
        s_ones = b.sem("rep")
        s_pe = b.sem("pe")
        s_at = b.sem("at")
        s_th = b.sem("tanh")
        s_wh = b.sem("w_hi")
        gained = (("a1q", "a1gx"), ("a1k", "a1gy"), ("a1v", "a1gy"), ("a1li2", "a1g3"), ("a2q", "a2gx"), ("a2li2", "a2g3"))
        first = SPLIT["a1q"][0]
        k = SPLIT["eg"][0]
        halves = slice(k, N_STAGED), slice(0, k)
        loads = 6
        R = lambda name: raw[:, SPLIT[name][0]:SPLIT[name][0] + SPLIT[name][1]]
        columns = [("a1q", "a1bx"), ("a1k", "a1by"), ("a1li2", "a1b3"), ("a2q", "a2bx"), ("a2li2", "a2b3")]
        bank = lambda i: core.psum[:, i, :]
        C = lambda name: cst[:, CST[name][0]:CST[name][0] + P]

        @b.block.sync
        def _(sp):
            sp.dma_start(raw[:, halves[0]], io["wsplit"][:, halves[0]]).then_inc(s_plain, 16)
            for dst, name in ((core.col, "col"), (core.w64, "w64"), (cst, "cst")):
                sp.dma_start(dst[:, :], io[name]).then_inc(s_ld, 16)
            sp.dma_start(freq[:, 0, :], io["freq_re"]).then_inc(s_ld, 16)
            sp.dma_start(freq[:, 1, :], io["freq_im"]).then_inc(s_ld, 16)
            sp.dma_start(raw[:, halves[1]], io["wsplit"][:, halves[1]]).then_inc(s_ld, 16)
            sp.dma_start(core.cst[:, :], io["cst"][:, 0:N_CST_KEPT]).then_inc(s_rest, 16)
            for dst, name in ((sel, "sel48"), (core.row, "row"), (core.wf, "wf")):
                sp.dma_start(dst[:, :], io[name]).then_inc(s_rest, 16)

        @b.block.gpsimd
        def _(g):
            g.memset(core.ones2[:, :], 1.0)
            g.memset(core.ctxn[:, :, :], 0.0)

        @b.block.tensor
        def _(pe):
            pe.wait_ge(s_ld, 16 * loads)
            k = 0
            for w, shift in columns:
                for m in range(4):
                    pe.matmul(bank(0)[:, k:k + 1], R(w)[:, m * P:m * P + P], core.Cc(shift), start=True, stop=True)
                    k += 1
            for m in range(4):
                mm = pe.matmul(bank(0)[:, k:k + 1], core.X("a2k", m * P, m * P + P), core.Cc("a2by", 0, NC),
                               start=True, stop=True)
                k += 1
            mm.then_inc(s_pe, 1)
            re, im = freq[:, 0, :], freq[:, 1, :]
            pe.matmul(bank(3)[:, 0:D], re, C("C"), start=True, stop=False)
            pe.matmul(bank(3)[:, 0:D], im, C("S"), start=False, stop=True)
            pe.matmul(bank(4)[:, 0:D], im, C("C"), start=True, stop=False)
            pe.matmul(bank(4)[:, 0:D], re, C("nS"), start=False, stop=True).then_inc(s_pe, 1)
            pe.wait_ge(s_ones, 1)
            pe.matmul(bank(1), rep[:, :], R("a1v"), start=True, stop=True)
            pe.matmul(bank(2)[:, :], rep64[:, :], core.X("a2v"), start=True, stop=True).then_inc(s_pe, 1)
            pe.wait_ge(s_at, 1)
            pe.matmul(bank(5)[:, 0:D], at[:, 0, :], C("Cn"), start=True, stop=False)
            pe.matmul(bank(5)[:, 0:D], at[:, 1, :], C("nSn"), start=False, stop=True).then_inc(s_pe, 1)

        @b.block.scalar
        def _(a):
            a.wait_ge(s_plain, 16)
            a.activation(core.wh[:, halves[0]], raw[:, halves[0]], ACT.Copy).then_inc(s_wh, 1)
            a.wait_ge(s_ld, 16 * loads)
            s, _ = COL["gx"]
            a.activation(core.tg[:, :], core.col[:, s:s + 8], ACT.Tanh).then_inc(s_th, 1)
            for w, gain in gained:
                a.activation(core.W(w, 1), R(w), ACT.Copy, scale=core.Cc(gain)).then_inc(s_wh, 1)
            a.activation(core.wh[:, 0:first], raw[:, 0:first], ACT.Copy).then_inc(s_wh, 1)

        @b.block.vector
        def _(v):
            ch = Chain(v, b.sem("chain"))
            v.wait_ge(s_wh, 1)
            v.tensor_tensor(core.wl[:, halves[0]], raw[:, halves[0]], f32(core.wh[:, halves[0]]), ALU.subtract)
            v.wait_ge(s_ld, 16 * loads)
            v.tensor_scalar(rep[:, :], C("ones128"), core.Cc("a1by"), None, ALU.mult)
            v.tensor_scalar(rep64[:, :], cst[0:NC, CST["ones128"][0]:CST["ones128"][0] + P], core.Cc("a2by", 0, NC), None,
                            ALU.mult).then_inc(s_ones, 1)
            for k, (w, gain) in enumerate(gained):
                v.wait_ge(s_wh, k + 2)
                v.scalar_tensor_tensor(core.W(w, 0), R(w), core.Cc(gain), f32(core.W(w, 1)), ALU.mult, ALU.subtract)
            v.wait_ge(s_wh, len(gained) + 2)
            v.tensor_tensor(core.wl[:, 0:first], raw[:, 0:first], f32(core.wh[:, 0:first]), ALU.subtract)
            v.wait_ge(s_pe, 2)
            v.tensor_copy(at[:, 0, :], bank(3)[:, 0:D])
            v.tensor_copy(at[:, 1, :], bank(4)[:, 0:D]).then_inc(s_at, 1)
            ch.link(v.tensor_copy(core.bias[:, :], bank(0)[:, 0:24]))
            for k, name in ((8, "a1li2b"), (16, "a2li2b")):
                s, w = COL[name]
                v.tensor_tensor(core.bias[:, k:k + 4], core.bias[:, k:k + 4], core.col[:, s:s + w], ALU.add)
            v.wait_ge(s_pe, 3)
            v.tensor_copy(core.vb1[:, :], bank(1))
            v.tensor_copy(core.vb2[:, :], bank(2))
            s, _ = W64["a2k"]
            both = core.w64[:, s:s + 1024]
            v.tensor_scalar(both, both, core.Cc("a2gy", 0, NC), None, ALU.mult)
            v.wait_ge(s_rest, 16 * 4)
            v.tensor_copy(core.identb[:, :], core.K("ident"))
            v.tensor_copy(core.sel48[:, :], sel[:, :])
            v.wait_ge(s_pe, 4)
            ch.link(v.tensor_copy(core.W("M", 1), bank(5)[:, 0:D]))
            v.tensor_tensor(core.W("M", 0), bank(5)[:, 0:D], f32(core.W("M", 1)), ALU.subtract)
            v.wait_ge(s_th, 1)
            for name, k in (("L0bo", 0), ("L3bo", 3), ("L3fb", 7)):
                v.tensor_scalar(core.R(name), core.R(name), core.tg[:, k:k + 1], None, ALU.mult)


def block_last(core, pair):
    with ExitStack() as mem, Block(core, "last") as b:
        norm = Norm(b, "norm", core.x, core.n)
        turn = Turn(b, "turn", norm)
        s_xb = b.sem("xb")
        s_out = b.sem("out")

        @b.block.tensor
        def _(pe):
            turn.tensor(pe)
            for u in range(PAIR):
                turn.ready(pe, u)
                bank = b.D.fill(pe, ("y", u))
                for i in range(NT):
                    mm = product_rows(pe, core, bank[:, i * P:i * P + P], "M", u, i)
                mm.then_inc(b.D.full, 1)

        @b.block.vector
        def _(v):
            ch = Chain(v, b.sem("chain"))
            norm.vector_stats(v)
            norm.vector_apply(v)
            turn.vector(v)
            v.wait_ge(s_xb, 1)
            for u in range(PAIR):
                x = core.toks(core.x, u).rearrange("p t d -> p (t d)")
                bank = b.D.read(v, ("y", u))
                v.scalar_tensor_tensor(x, bank, core.tg[:, 7:8], x, ALU.mult, ALU.add).then_inc(b.D.free, 1)

        @b.block.scalar
        def _(a):
            turn.scalar(a)

        @b.block.gpsimd
        def _(g):
            norm.gpsimd(g)
            g.wait_ge(norm.s_n, PAIR)
            g.tensor_tensor(core.x[:, :, :], core.x[:, :, :], core.rows("L3fb", PAIR * NT), ALU.add).then_inc(s_xb, 1)

        @b.block.sync
        def _(sp):
            for u in range(PAIR):
                b.D.done(sp, ("y", u))
                sp.dma_start(core.io["out"][bass.ds(pair * PAIR + u, 1)].rearrange("b (t p) d -> p (b t) d", p=P),
                             core.toks(core.x, u)).then_inc(s_out, 16)
            sp.wait_ge(s_out, 16 * PAIR)


IN = ["x", "ctxT", "ctx", "wsplit", "wf", "w64", "row", "col", "cst", "sel48", "freq_re", "freq_im",
      "w1", "w2", "b2", "down", "k0", "k1", "k2"]


def build(nc, io):
    with ExitStack() as ctx:
        core = Core(nc, io, ctx)
        block_setup(core)
        with nc.Fori(0, B // PAIR) as pair:
            block_narrow(core, 0, pair, True)
            block_experts0(core)
            block_self(core)
            block_wide(core)
            block_experts1(core)
            block_single(core)
            block_signs(core)
            block_narrow(core, 3, pair, False)
            block_last(core, pair)


def packed(layout, width, parts, given):
    out = np.zeros((parts, width), np.float32)
    for name, (at, w) in layout.items():
        if name in given:
            a = given[name]
            out[:a.shape[0], at:at + w] = a
    return out


def constants():
    i = np.arange(P)
    turn = 2 * np.pi * ((i[:, None] * i[None, :]) % D) / D
    c, s = np.cos(turn), np.sin(turn)
    onesm = np.zeros((P, 4, 40))
    onesm[:, :, 0:8] = 1
    ksel = np.zeros((P, 4))
    for q in range(4):
        ksel[STK + 2 * q:STK + 2 * q + 2, q] = 1
    kblock = ksel + (((i[:, None] % 32) // 8 == np.arange(4)) & (i[:, None] < STK))
    given = {"ident": np.eye(P), "mask": i[:, None] > i[None, :], "ones": np.ones((P, 32)), "ones128": np.ones((P, P)), "onesm": onesm.reshape(P, 160),
             "ksel": ksel, "kblock": kblock, "iota": np.tile(np.arange(16), (P, 1)), "half": np.full((P, 8), -0.5),
             "C": c, "S": s, "nS": -s, "Cn": c / D, "nSn": -s / D}
    sel = np.zeros((3, E1, E1 // 2, 2, F1), np.float32)
    for e in range(E1):
        sel[:, e, e // 2, e % 2] = 1
    return packed(CST, N_CST, P, given), sel.reshape(3 * E1, E1 // 2 * P)


def arrays(i):
    tile = lambda a, n: a.reshape(n, P, -1).transpose(1, 0, 2).reshape(P, -1)
    heads = lambda a: a.transpose(1, 0, 2).reshape(a.shape[1], -1)
    cols = lambda a: a.reshape(-1, P).T
    words = lambda a: np.ascontiguousarray(a).view(np.uint32)
    a1, a2 = "L1_xattn_a1_", "L1_xattn_a2_"
    steps = lambda a: a.reshape(a.shape[:-1] + (4, 4, 8)).swapaxes(-3, -2).reshape(a.shape)
    split = {"L0q": steps(i["L0_xattn_Wq"]), "L3q": steps(i["L3_xattn_Wq"]), "L2q": i["L2_xattn_Wq"], "g0": i["L0_ffn_gate_w"],
             "g1": i["L1_ffn_gate_w"].T, "a1q": heads(i[a1 + "wq"]), "a1k": heads(i[a1 + "wk"]),
             "a1v": heads(i[a1 + "wv"]), "a1li2": i[a1 + "li2_w"], "a2q": heads(i[a2 + "wq"]), "a2li2": i[a2 + "li2_w"],
             "eg": heads(i["L1_ffn_expert_gate"]), "sg": i["L1_ffn_shared_gate"],
             "eu": heads(i["L1_ffn_expert_up"]), "su": i["L1_ffn_shared_up"]}
    wf = {"L0o": i["L0_xattn_Wo"], "L3o": i["L3_xattn_Wo"], "a1li1": tile(i[a1 + "li1_w"], 4),
          "a1li3": tile(i[a1 + "li3_w"], 4), "a2li1": tile(i[a2 + "li1_w"], 4), "a2li3": tile(i[a2 + "li3_w"], 4)}
    w64 = {f"L{n}{k}": i[f"L{n}_xattn_W{k}"] for n in (0, 2, 3) for k in "kv"}
    w64 |= {f"L{n}k": steps(w64[f"L{n}k"]) for n in (0, 3)}
    w64 |= {"a2k": heads(i[a2 + "wk"]), "a2v": heads(i[a2 + "wv"])}
    rows = {"L0bv": "L0_xattn_bv", "L2bv": "L2_xattn_bv", "L3bv": "L3_xattn_bv", "L0bo": "L0_xattn_bo",
            "L3bo": "L3_xattn_bo", "L3fb": "L3_ffn_bias", "a1li1b": a1 + "li1_b", "a1li3b": a1 + "li3_b",
            "a2li1b": a2 + "li1_b", "a2li3b": a2 + "li3_b", "ln1g": "L1_xattn_ln1_g", "ln1b": "L1_xattn_ln1_b",
            "ln2g": "L1_xattn_ln2_g", "ln2b": "L1_xattn_ln2_b"}
    row = {k: np.broadcast_to(i[v], (P, D)) for k, v in rows.items()}
    col = {f"L{n}b{k}": cols(i[f"L{n}_xattn_b{k}"]) for n in (0, 2, 3) for k in "qk"}
    col |= {f"L{n}b{k}": cols(steps(i[f"L{n}_xattn_b{k}"])) for n in (0, 3) for k in "qk"}
    for a, full in (("a1", a1), ("a2", a2)):
        for short, long in (("gx", "lnx_g"), ("bx", "lnx_b"), ("gy", "lny_g"), ("by", "lny_b"), ("g3", "ln3_g"),
                            ("b3", "ln3_b")):
            col[a + short] = i[full + long].reshape(-1, 1)
        col[a + "li2b"] = cols(i[full + "li2_b"])
    col["b1"] = cols(i["L0_ffn_dense_1_b"].reshape(E0, F0, 2).transpose(0, 2, 1).reshape(-1))
    col["gx"] = np.broadcast_to(i["g_xattn"], (P, 4))
    col["gf"] = np.broadcast_to(i["g_ffn"], (P, 4))
    col["s"] = np.broadcast_to(np.stack([i["L2_ffn_s0"], i["L2_ffn_s1"], i["L2_ffn_s2"]]), (P, 3))
    ctxT = np.zeros((NC, B, NKE), np.float32)
    ctxT[:, :, :NK] = i["ctx_512"].transpose(2, 0, 1)
    cst, sel = constants()
    return {
        "x": i["x"], "ctxT": ctxT, "ctx": i["ctx_512"],
        "wsplit": packed(SPLIT, N_STAGED, P, split), "wf": packed(WF, N_WF, P, wf), "w64": packed(W64, N_W64, NC, w64),
        "row": packed(ROW, N_ROW, P, row), "col": packed(COL, N_COL, P, col), "cst": cst, "sel48": sel,
        "freq_re": i["L3_ffn_w_freq_real"], "freq_im": i["L3_ffn_w_freq_imag"],
        "w1": i["L0_ffn_dense_1_w"].reshape(E0, F0, 2, D).transpose(3, 0, 2, 1).reshape(D, -1),
        "w2": i["L0_ffn_dense_2_w"].transpose(0, 2, 1).reshape(E0 * F0 // P, P, D).transpose(1, 0, 2),
        "b2": i["L0_ffn_dense_2_b"],
        "down": np.concatenate([i["L1_ffn_expert_down"].reshape(E1 * F1, D), i["L1_ffn_shared_down"]])
        .reshape(-1, P, D).transpose(1, 0, 2),
        "k0": words(i["L2_ffn_k0"].reshape(2, P, 512)), "k1": words(tile(i["L2_ffn_k1"], 4)),
        "k2": words(tile(i["L2_ffn_k2"], 4)),
    }


def kernel(**inputs):
    from concourse import bacc
    from concourse.bass_utils import run_bass_kernel_spmd

    given = arrays({k: np.asarray(v) for k, v in inputs.items()})
    nc = bacc.Bacc("TRN2", target_bir_lowering=False, num_devices=1)
    feed, io = {}, {}
    for name in IN:
        a = np.ascontiguousarray(given[name])
        feed["in_" + name] = a
        io[name] = nc.dram_tensor("in_" + name, a.shape, mybir.dt.from_np(a.dtype), kind="ExternalInput").ap()
    io["out"] = nc.dram_tensor("out_x", (B, T, D), F32, kind="ExternalOutput").ap()
    build(nc, io)
    r = run_bass_kernel_spmd(nc, [feed], core_ids=[0])
    return r.results[0]["out_x"]
```
